# Optimizing a Trainium2 kernel written in Bass

```python
import numpy as np
import jax
import jax.numpy as jnp

def _softmax(x, axis=-1):
    return jax.nn.softmax(x, axis=axis)

def _gelu(x):
    return jax.nn.gelu(x, approximate=True)

def _silu(x):
    return jax.nn.silu(x)

def _sigmoid(x):
    return jax.nn.sigmoid(x)

def _layernorm(x, axis=-1, eps=1e-05):
    m = jnp.mean(x, axis=axis, keepdims=True)
    v = jnp.var(x, axis=axis, keepdims=True)
    return (x - m) / jnp.sqrt(v + eps)

def _scatter_add(tgt, idx, src, axis=0):
    return tgt.at[idx].add(src)

def _segment_sum(src, seg, n):
    return jax.ops.segment_sum(src, seg, n)
kernel_name = 'mk_xattn_ffn_d2_seqx_r8_618804'

def setup_inputs(seed: int=0):
    np.random.seed(seed)
    _w = jnp.asarray

    def _rec_inputs():
        import jax
        import jax.numpy as jnp
        _rk = jax.random.key(seed)
        x = 7.22e-05 + 1 * jax.random.normal(jax.random.fold_in(_rk, 1), (16, 128, 256), jnp.float32)
        _lenS = 128 - jax.random.randint(jax.random.fold_in(_rk, 7), (16,), 0, max(1, 128 // 4) + 1, jnp.int32)
        _lenS2 = 128 - jax.random.randint(jax.random.fold_in(_rk, 8), (16,), 0, max(1, 128 // 4) + 1, jnp.int32)
        _ctx_2048P = jax.random.normal(jax.random.fold_in(_rk, 11), (16, 16, 256), jnp.float32)
        _ctx_2048c = jax.random.dirichlet(jax.random.fold_in(_rk, 511), 0.3 * jnp.ones((16,), jnp.float32), (16, 128))
        _ctx_2048t = jnp.einsum('bsk,bkd->bsd', _ctx_2048c, _ctx_2048P)
        _ctx_2048t = _ctx_2048t * jax.lax.rsqrt(jnp.mean(jnp.square(_ctx_2048t)) + 1e-12) * 0.953939
        ctx_2048 = 4.13588e-05 + 0.999923 * (_ctx_2048t + 0.3 * jax.random.normal(jax.random.fold_in(_rk, 611), (16, 128, 256), jnp.float32))
        return (x, ctx_2048)
    x, ctx_2048 = _rec_inputs()

    def _L0_xattn_setup():
        import jax, jax.numpy as jnp
        import numpy as np
        B, S, DIM, HD = (4, 128, 256, 128)
        H = DIM // HD
        GN_EPS = 0.001

        def _decay_masks(n_heads, seq_len):
            gam = 1.0 - 2.0 ** (-5.0 - jnp.arange(n_heads, dtype=jnp.float32))
            idx = jnp.arange(seq_len, dtype=jnp.float32)
            expo = idx[None, :] - idx[:, None]
            D = jnp.where(expo[None, :, :] <= 0, gam[:, None, None] ** expo[None, :, :], 0.0)
            return D / jnp.sqrt(D.sum(axis=-1))[:, None, :]
        key = jax.random.key(seed)
        ks = jax.random.split(key, 8)
        x = jax.random.normal(ks[0], (B, S, DIM), dtype=jnp.float32)
        k = jax.random.normal(ks[1], (B, S, DIM), dtype=jnp.float32)
        v = jax.random.normal(ks[2], (B, S, DIM), dtype=jnp.float32)
        Wh = jax.random.normal(ks[3], (H, HD, HD), dtype=jnp.float32) / np.sqrt(HD)
        wg_w = jax.random.normal(ks[4], (DIM, DIM), dtype=jnp.float32) / np.sqrt(DIM)
        wo_w = jax.random.normal(ks[5], (DIM, DIM), dtype=jnp.float32) / np.sqrt(DIM)
        gn_gamma = jnp.ones((DIM,), dtype=jnp.float32)
        gn_beta = jnp.zeros((DIM,), dtype=jnp.float32)
        return {'x': x, 'k': k, 'v': v, 'Wh': Wh, 'wg_w': wg_w, 'wo_w': wo_w, 'gn_gamma': gn_gamma, 'gn_beta': gn_beta}
    _L0_xattn_all = _L0_xattn_setup()
    _L0_xattn_in = {k: v for k, v in _L0_xattn_all.items() if k in ('Wh', 'wg_w', 'wo_w', 'gn_gamma', 'gn_beta')}
    del _L0_xattn_all

    def _L0_ffn_setup():
        import jax, jax.numpy as jnp
        import numpy as np
        E, TOPK, H, I = (8, 2, 256, 512)
        SOFTCAP = 30.0
        key = jax.random.key(seed)
        ks = jax.random.split(key, 5)
        s = 1.0 / np.sqrt(H)
        si = 1.0 / np.sqrt(I)
        return {'hidden_states': jax.random.normal(ks[0], (4, 256, H), jnp.float32), 'w_gate': jax.random.normal(ks[1], (H, E), jnp.float32) * s, 'w1': jax.random.normal(ks[2], (E, H, I), jnp.float32) * s, 'w3': jax.random.normal(ks[3], (E, H, I), jnp.float32) * s, 'w2': jax.random.normal(ks[4], (E, I, H), jnp.float32) * si}
    _L0_ffn_all = _L0_ffn_setup()
    _L0_ffn_in = {k: v for k, v in _L0_ffn_all.items() if k in ('w_gate', 'w1', 'w3', 'w2')}
    del _L0_ffn_all

    def _L1_xattn_setup():
        import jax, jax.numpy as jnp
        import numpy as np
        BS, S, DK = (8, 64, 256)
        key = jax.random.key(seed)
        kq, kk, kv = jax.random.split(key, 3)
        q = jax.random.normal(kq, (BS, S, DK), dtype=jnp.float32)
        k = jax.random.normal(kk, (BS, S, DK), dtype=jnp.float32)
        v = jax.random.normal(kv, (BS, S, DK), dtype=jnp.float32)
        return {'q': q, 'k': k, 'v': v}
    _L1_xattn_all = _L1_xattn_setup()
    _L1_xattn_in = {k: v for k, v in _L1_xattn_all.items() if k in ()}
    del _L1_xattn_all

    def _L1_ffn_setup():
        import jax, jax.numpy as jnp
        import numpy as np
        TOPK = 6
        CAP = 128
        ROUTE_SCALE = 1.0
        key = jax.random.key(seed)
        k = jax.random.split(key, 6)
        B, T, C = (2, 256, 256)
        E, H, HS = (64, 32, 64)
        std = 0.01
        return {'x': jax.random.normal(k[0], (B, T, C), jnp.float32), 'w_gate': jax.random.normal(k[1], (C, E), jnp.float32) * std, 'w_shared_up': jax.random.normal(k[2], (C, 2 * HS), jnp.float32) * std, 'w_shared_down': jax.random.normal(k[3], (HS, C), jnp.float32) * std, 'w_up': jax.random.normal(k[4], (E, C, 2 * H), jnp.float32) * std, 'w_down': jax.random.normal(k[5], (E, H, C), jnp.float32) * std}
    _L1_ffn_all = _L1_ffn_setup()
    _L1_ffn_in = {k: v for k, v in _L1_ffn_all.items() if k in ('w_gate', 'w_shared_up', 'w_shared_down', 'w_up', 'w_down')}
    del _L1_ffn_all
    return {'x': x, 'ctx_2048': ctx_2048, 'L0_xattn_Wh': _L0_xattn_in['Wh'], 'L0_xattn_wg_w': _L0_xattn_in['wg_w'], 'L0_xattn_wo_w': _L0_xattn_in['wo_w'], 'L0_xattn_gn_gamma': _L0_xattn_in['gn_gamma'], 'L0_xattn_gn_beta': _L0_xattn_in['gn_beta'], 'L0_ffn_w_gate': _L0_ffn_in['w_gate'], 'L0_ffn_w1': _L0_ffn_in['w1'], 'L0_ffn_w3': _L0_ffn_in['w3'], 'L0_ffn_w2': _L0_ffn_in['w2'], 'L1_ffn_w_gate': _L1_ffn_in['w_gate'], 'L1_ffn_w_shared_up': _L1_ffn_in['w_shared_up'], 'L1_ffn_w_shared_down': _L1_ffn_in['w_shared_down'], 'L1_ffn_w_up': _L1_ffn_in['w_up'], 'L1_ffn_w_down': _L1_ffn_in['w_down']}

def reference(x, ctx_2048, L0_xattn_Wh, L0_xattn_wg_w, L0_xattn_wo_w, L0_xattn_gn_gamma, L0_xattn_gn_beta, L0_ffn_w_gate, L0_ffn_w1, L0_ffn_w3, L0_ffn_w2, L1_ffn_w_gate, L1_ffn_w_shared_up, L1_ffn_w_shared_down, L1_ffn_w_up, L1_ffn_w_down):
    import jax
    import jax.numpy as jnp

    def _L0_xattn_ref(x, k, v, Wh, wg_w, wo_w, gn_gamma, gn_beta):
        import jax, jax.numpy as jnp
        import numpy as np
        B, S, DIM, HD = (4, 128, 256, 128)
        H = DIM // HD
        GN_EPS = 0.001

        def _decay_masks(n_heads, seq_len):
            gam = 1.0 - 2.0 ** (-5.0 - jnp.arange(n_heads, dtype=jnp.float32))
            idx = jnp.arange(seq_len, dtype=jnp.float32)
            expo = idx[None, :] - idx[:, None]
            D = jnp.where(expo[None, :, :] <= 0, gam[:, None, None] ** expo[None, :, :], 0.0)
            return D / jnp.sqrt(D.sum(axis=-1))[:, None, :]
        b, s, dim = x.shape
        h, hd, _ = Wh.shape
        xh = x.reshape(b, s, h, hd)
        kh = k.reshape(b, s, h, hd)
        vh = v.reshape(b, s, h, hd)
        Q = jnp.einsum('bshd,hde->bshe', xh, Wh)
        K = jnp.einsum('bshd,hde->bshe', kh, Wh)
        V = jnp.einsum('bshd,hde->bshe', vh, Wh)
        scores = jnp.einsum('bshe,bthe->bhst', Q, K) / jnp.sqrt(jnp.float32(hd))
        Dn = _decay_masks(h, s)
        masked = scores * Dn[None, :, :, :]
        A = jnp.maximum(jnp.abs(masked.sum(axis=0)), 1.0)
        O = jnp.einsum('hst,bthe->bshe', A, V).reshape(b, s, dim)
        mu = O.mean(axis=-1, keepdims=True)
        var = O.var(axis=-1, keepdims=True)
        Y = (O - mu) / jnp.sqrt(var + GN_EPS) * gn_gamma + gn_beta
        W = jax.nn.relu(x @ wg_w)
        return W * Y @ wo_w

    def _L0_ffn_ref(hidden_states, w_gate, w1, w3, w2):
        import jax, jax.numpy as jnp
        import numpy as np
        E, TOPK, H, I = (8, 2, 256, 512)
        SOFTCAP = 30.0
        orig_shape = hidden_states.shape
        x = hidden_states.reshape(-1, H)
        logits = x @ w_gate
        logits = SOFTCAP * jnp.tanh(logits / SOFTCAP)
        probs = jax.nn.softmax(logits, axis=-1)
        _, idx = jax.lax.top_k(probs, TOPK)
        mask = jax.nn.one_hot(idx, E, dtype=probs.dtype).sum(-2)
        weights = probs * mask
        out = jnp.zeros_like(x)
        for e in range(E):
            h = jax.nn.silu(x @ w1[e]) * (x @ w3[e])
            out = out + h @ w2[e] * weights[:, e:e + 1]
        return out.reshape(orig_shape)

    def _L1_xattn_ref(q, k, v):
        import jax, jax.numpy as jnp
        import numpy as np
        BS, S, DK = (8, 64, 256)
        dk = q.shape[-1]
        scale = 1.0 / jnp.sqrt(jnp.asarray(dk, dtype=q.dtype))
        scaled = jnp.einsum('bsd,bse->bde', q, k) * scale
        attn = jax.nn.softmax(scaled, axis=1)
        out = jnp.einsum('bde,bse->bsd', attn, v)
        return out

    def _L1_ffn_ref(x, w_gate, w_shared_up, w_shared_down, w_up, w_down):
        import jax, jax.numpy as jnp
        import numpy as np
        TOPK = 6
        CAP = 128
        ROUTE_SCALE = 1.0
        B, T, C = x.shape
        E = w_gate.shape[1]
        x_flat = x.reshape(-1, C)
        N = x_flat.shape[0]
        su = x_flat @ w_shared_up
        y_s, g_s = jnp.split(su, 2, axis=-1)
        shared = jax.nn.silu(g_s) * y_s @ w_shared_down
        scores = jax.nn.sigmoid(x_flat @ w_gate)
        _, topk_idx = jax.lax.top_k(scores, TOPK)
        w = jnp.take_along_axis(scores, topk_idx, axis=-1)
        w = w / w.sum(-1, keepdims=True) * ROUTE_SCALE
        flat_e = topk_idx.reshape(-1)
        oh = jax.nn.one_hot(flat_e, E, dtype=jnp.int32)
        pos = jnp.take_along_axis(jnp.cumsum(oh, axis=0), flat_e[:, None], axis=1)[:, 0] - 1
        valid = pos < CAP
        pos_c = jnp.where(valid, pos, CAP - 1)
        token_ids = jnp.repeat(jnp.arange(N), TOPK)
        x_disp = jnp.zeros((E, CAP, C), x.dtype).at[flat_e, pos].set(x_flat[token_ids], mode='drop')
        up = jnp.einsum('ecd,edh->ech', x_disp, w_up)
        g_r, v_r = jnp.split(up, 2, axis=-1)
        h_r = jax.nn.silu(g_r) * v_r
        out_r = jnp.einsum('ech,ehd->ecd', h_r, w_down)
        y_ts = out_r[flat_e, pos_c]
        y_ts = jnp.where(valid[:, None], y_ts, 0.0)
        routed = (y_ts.reshape(N, TOPK, C) * w[:, :, None]).sum(axis=1)
        return (shared + routed).reshape(B, T, C)
    x = x + _L0_xattn_ref(_layernorm(x, axis=-1), ctx_2048, ctx_2048, L0_xattn_Wh, L0_xattn_wg_w, L0_xattn_wo_w, L0_xattn_gn_gamma, L0_xattn_gn_beta)
    x = x + _L0_ffn_ref(_layernorm(x, axis=-1), L0_ffn_w_gate, L0_ffn_w1, L0_ffn_w3, L0_ffn_w2)
    x = x + _L1_xattn_ref(_layernorm(x, axis=-1), ctx_2048, ctx_2048)
    x = x + _L1_ffn_ref(_layernorm(x, axis=-1), L1_ffn_w_gate, L1_ffn_w_shared_up, L1_ffn_w_shared_down, L1_ffn_w_up, L1_ffn_w_down)
    return x

_drawn_inputs = setup_inputs


def setup_inputs(seed=0):
    import zlib

    import numpy as np

    out = dict(_drawn_inputs(seed))
    spreads = {'L0_xattn_gn_gamma': (1.0, 0.2), 'L0_xattn_gn_beta': (0.0, 0.1)}
    factors = {'L1_ffn_w_gate': 8.0,
     'L1_ffn_w_shared_up': 8.0,
     'L1_ffn_w_shared_down': 8.0,
     'L1_ffn_w_up': 8.0,
     'L1_ffn_w_down': 8.0}
    for name, (base, spread) in spreads.items():
        noise = np.random.default_rng([zlib.crc32(name.encode()), seed]).standard_normal(out[name].shape)
        drawn = base * np.exp(spread * noise) if base else spread * noise
        out[name] = jnp.asarray(drawn.astype(out[name].dtype))
    for name, factor in factors.items():
        out[name] = (out[name] * factor).astype(out[name].dtype)
    return out
```

```python
from contextlib import ExitStack

import numpy as np

import concourse.bass as bass
from concourse import mybir

F32 = mybir.dt.float32
F32R = mybir.dt.float32r
BF16 = mybir.dt.bfloat16
I32 = mybir.dt.int32
U32 = mybir.dt.uint32
ACT = mybir.ActivationFunctionType
ALU = mybir.AluOpType
X = mybir.AxisListType.X

P = 128
B = 16
D = 256
KD = D // P
H0 = 2
E0, TOP0, I0 = 8, 2, 512
KI = I0 // P
SOFTCAP = 30.0
E1, TOP1, HID1, CAP1 = 64, 6, 32, 128
HS = 64
LN_EPS, GN_EPS = 1e-5, 1e-3
TILES0 = (B * P * TOP0 - E0) // P + E0
TJ = TILES0 + 1
NOWHERE = float(1 << 20)
NPAIR = B * TOP0
W0E = 2 * KD * I0 + KI * D
CH = 8
NCH = E1 // CH
KCH = CH * HID1 // P
GS = E1 + 2 * HS


class Steps:

    def __init__(self, sem, names, items=1):
        self.sem, self.names, self.items, self.n = sem, names.split(), items, 0
        assert len(set(self.names)) == len(self.names)

    def step(self, name):
        want = self.names[self.n % len(self.names)]
        assert want == name, (name, want)
        self.n += 1
        return self.sem

    def at(self, item, name):
        return item * len(self.names) + (self.names.index(name) + 1)

    @property
    def all(self):
        return self.items * len(self.names)


def after(eng, *phases):
    for steps in phases:
        eng.wait_ge(steps.sem, steps.all)


def wait_apart(eng, consts, *waits):
    values = [v if isinstance(v, int) else eng.to_reg(v) for _, v in waits]
    eng.wait_ge(consts.sem, consts.all)
    for (sem, _), v in zip(waits, values):
        eng.wait_ge(sem, v)


def early(t):
    return isinstance(t, int) and t < 2


def pipeline(eng, n, *stages):
    most = max(lag for lag, _ in stages)
    head = most + 2 + most % 2

    def one(s, parity, half):
        for lag, body in stages:
            if isinstance(s, int) and not 0 <= s - lag < n:
                continue
            u = (parity - lag) % 2
            body(s - lag, u, half - (lag - parity + u) // 2)

    for s in range(head):
        one(s, s % 2, s // 2)
    with eng.Fori(head // 2, n // 2) as i:
        for v in range(2):
            one(2 * i + v, v, i)
    for s in range(n // 2 * 2, n + most):
        one(s, s % 2, s // 2)


def mm3(pe, out, lhs, rhs, first, last):
    (lh, ll), (rh, rl) = lhs, rhs
    pe.matmul(out, lh, rh, start=first, stop=False)
    pe.matmul(out, lh, rl, start=False, stop=False)
    return pe.matmul(out, ll, rh, start=False, stop=last)


class Map:

    def __init__(self, nc, at, end):
        self.nc, self.at, self.end = nc, at, end

    def __call__(self, name, shape, dt=F32):
        size = int(np.prod(shape[1:])) * (2 if dt == BF16 else 4)
        t = self.nc.alloc_sbuf_tensor_at(name, shape, dt, offset=self.at)
        self.at += (size + 31) // 32 * 32
        assert self.at <= self.end, (name, self.at, self.end)
        return t

    def pair(self, name, shape):
        return self(name + "_hi", shape, F32R), self(name + "_lo", shape, F32R)


def build(nc, x, ctx, Wh, wg, wo, gamma, beta, wgate0, w1, w3, w2, wgate1, wsu, wsd, wup, wdown, decay, out):
    st = ExitStack()
    KB = 1024
    base = (nc.sbuf_base + 63) // 64 * 64
    END = nc.sbuf_usable_end // 64 * 64
    keep = Map(nc, base, base + 27 * KB)
    big = Map(nc, keep.end, keep.end + 98 * KB)
    W = big.end
    big1 = Map(nc, keep.end, W)
    work_a, work_r, work_c, work_d = Map(nc, W, END), Map(nc, W, END), Map(nc, W, END), Map(nc, W, END)

    def psum(name, shape, dt=F32):
        return st.enter_context(nc.psum_tensor(name, shape, dt))

    def sem(name):
        return st.enter_context(nc.semaphore(name))

    xf = x.rearrange("b s d -> (b s) d")
    cf = ctx.rearrange("b s d -> (b s) d")
    of = out.rearrange("b s d -> (b s) d")
    xn_rows = nc.dram_tensor("xn_rows", [B * P, D], F32, kind="Internal").ap()
    y_rows = nc.dram_tensor("y_rows", [B * P * TOP0, D], F32, kind="Internal").ap()

    ident = keep("ident", [P, P])
    before = keep("before", [P, P], BF16)
    ones = keep("ones", [P, P], BF16)
    iota_row = keep("iota_row", [P, P])
    eps = keep("eps", [P, 2])
    x_res = keep("x_res", [P, B, D])
    bn = keep("bn", [P, B, 6])
    mom = keep("mom", [P, 5, B])
    mean = keep("mean", [P, B])
    sdev = keep("sdev", [P, B])
    rstd = keep("rstd", [P, B])
    gate1 = keep.pair("gate1", [P, KD, GS])
    wsd_s = keep.pair("wsd_s", [HS, D])
    lg = keep("lg", [P, B, E0])
    table = keep("table", [P, 3, TJ], I32)
    expert_of = keep("expert_of", [P, TJ], I32)

    W0 = big("W0", [P, E0, W0E])
    wup_s = big1.pair("wup_s", [P, KD, E1, 2 * HID1])
    wdn_s = big1.pair("wdn_s", [P, E1 * HID1 // P, D])

    wh_raw = work_a("wh_raw", [P, H0, P])
    wg_raw = work_a("wg_raw", [P, KD, D])
    wo_raw = work_a("wo_raw", [P, KD, D])
    gate0_raw = work_a("gate0_raw", [P, KD, E0])
    gate1_raw = work_a("gate1_raw", [P, KD, GS])
    wsd_raw = work_a("wsd_raw", [HS, D])
    wh = work_a.pair("wh", [P, H0, P])
    wgs = work_a.pair("wgs", [P, KD, D])
    wos = work_a.pair("wos", [P, KD, D])
    gate0 = work_a.pair("gate0", [P, KD, E0])
    dec = work_a("dec", [P, H0, P])
    gam = work_a("gam", [P, D])
    bet = work_a("bet", [P, D])
    G = work_a("G", [P, B, D])
    Gb = work_a("Gb", [P, B, D])
    xin = work_a("xin", [P, 2, D])
    cin = work_a("cin", [P, 2, D])
    xn = work_a("xn", [P, 2, D])
    sm = work_a("sm", [P, 2, 10])
    tT = work_a.pair("tT", [P, 2, 4, P])
    qk = work_a.pair("qk", [P, 2, 4, P])
    At = work_a.pair("At", [P, H0, P])
    Araw = work_a("Araw", [P, H0, P])

    rt = {}
    for name, shape in (("prob", [B, E0]), ("rev", [E0]), ("key", [B, E0]), ("hot1", [B, E0]), ("hot2", [B, E0]),
                        ("rest", [B, E0]), ("wsel", [TOP0, B]), ("m", [B]), ("r", [B]), ("k", [B]), ("slot", [B, E0]),
                        ("pick", [B, E0]), ("slotk", [TOP0, B]), ("cnt", [E0]), ("steps128", [B]), ("over", [E0, B]),
                        ("tiles", [E0]), ("one8", [E0]), ("tend", [E0]), ("tstart", [E0]), ("j128", [TJ + 1]),
                        ("jrow", [TJ]), ("passed", [TJ, E0]), ("ef", [TJ]), ("ge", [NPAIR, TJ + 1]),
                        ("hotj", [NPAIR, TJ]), ("tile_of", [NPAIR]), ("row_of", [NPAIR]), ("hotp", [NPAIR, P]),
                        ("val", [3, NPAIR]), ("R", [NPAIR, 3, TJ]), ("T", [3, TJ]), ("none", [TJ])):
        rt[name] = work_r("rt_" + name, [P, *shape])
    mask0 = work_r("mask0", [P, B, E0], BF16)

    xg = work_c("xg", [P, 2, D])
    xTc = work_c("xTc", [P, 2, KD, P])
    sa = work_c("sa", [P, 2, I0])
    hh = work_c("hh", [P, 2, I0])
    hTc = work_c("hTc", [P, 2, KI, P])
    ys = work_c("ys", [P, 2, D])
    stage_g = work_c("stage_g", [P, 2, 1], I32)
    stage_s = work_c("stage_s", [P, 2, 1], I32)
    raw1 = Map(nc, END - 50 * KB, END)
    wup_raw = raw1("wup_raw", [P, KD, E1, 2 * HID1])
    wdn_raw = raw1("wdn_raw", [P, E1 * HID1 // P, D])

    work_d.end = END - 50 * KB
    yin = work_d("yin", [P, 2, TOP0, D])
    cin2 = work_d("cin2", [P, 2, D])
    xn2 = work_d("xn2", [P, 2, D])
    cs = work_d.pair("cs", [P, 2, D])
    xs = work_d.pair("xs", [P, 2, D])
    cT = work_d.pair("cT", [P, 2, KD, P])
    ex = work_d("ex", [P, 2, KD, D])
    at = work_d.pair("at", [P, 2, KD, D])
    smx = work_d("smx", [P, 2, 4, KD])

    work_e = Map(nc, W, END - 50 * KB)
    xn3 = work_e("xn3", [P, 2, D])
    x3T = work_e.pair("x3T", [P, 2, KD, P])
    sg = work_e("sg", [P, 2, CH, HID1])
    hv = work_e("hv", [P, 2, CH, HID1])
    hw = work_e("hw", [P, 2, CH, HID1])
    hT = work_e.pair("hT", [P, 2, KCH, P])
    sgs = work_e("sgs", [P, 2, HS])
    hs = work_e("hs", [P, 2, HS])
    esc = work_e("esc", [P, 2, E1])
    sc = work_e("sc", [P, 2, E1])
    top8 = work_e("top8", [P, 8])
    idx8 = work_e("idx8", [P, 8], U32)
    idxf = work_e("idxf", [P, 8])
    hot = work_e("hot", [P, TOP1, E1])
    mask1 = work_e("mask1", [P, 2, E1], BF16)
    macc = work_e("macc", [P, 2, E1], BF16)
    ssel = work_e("ssel", [P, E1])
    wsum = work_e("wsum", [P, 2])
    valid = work_e("valid", [P, E1])
    wt = work_e("wt", [P, 2, E1])
    outb = work_e("outb", [P, 2, D])

    bank = [psum(f"bank{i}", [P, 512]) for i in range(8)]

    def view(i, *shape):
        names = "abc"[:len(shape)]
        n = int(np.prod(shape))
        return bank[i][:, 0:n].rearrange(f"p ({' '.join(names)}) -> p {' '.join(names)}",
                                         **dict(zip(names, shape)))

    tp_a = [view(i, 4, P) for i in (0, 1)]
    qk_a = [view(i, 4, P) for i in (2, 3)]
    S_a = [bank[i][:, 0:P] for i in (4, 5)]
    g_a = [bank[i][:, 0:D] for i in (6, 7)]
    two_a = [view(i, 2, P) for i in (0, 1)]
    u_a = [view(i, 2, P) for i in (2, 3)]
    row_a = [bank[i][:, 0:D] for i in (6, 7)]
    lg_a = [bank[i][:, 0:E0] for i in (6, 7)]
    pos_r = view(0, B + 1, E0)
    tab_r = view(1, 3, TJ)
    xT_c = [view(i, KD, P) for i in (0, 1)]
    up_c = [[bank[2][:, :], bank[3][:, :]], [bank[4][:, :], bank[5][:, :]]]
    hT_c = view(6, KI, P)
    y_c = bank[7][:, 0:D]
    cT_d = [view(i, KD, P) for i in (0, 1)]
    sc_d = [view(i, KD, D) for i in (2, 3)]
    o_d = [bank[i][:, 0:D] for i in (4, 5)]
    up_e = [view(i, CH, 2 * HID1) for i in (0, 1)]
    hT_e = [view(i, KCH, P) for i in (2, 3)]
    y_e = [bank[i][:, 0:D] for i in (4, 5)]
    x3T_e = view(6, KD, P)
    gs_e = bank[7][:, 0:GS]
    pos_e = bank[7][:, GS:GS + E1]

    small = {n: sem("got_" + n) for n in ("wh", "wg", "wo", "gate0", "gate1", "wsd", "decay", "gamma", "beta")}
    got_x = [sem("got_x0"), sem("got_x1")]
    got_c = [sem("got_c0"), sem("got_c1")]
    got_w0 = sem("got_w0")
    got_w1 = sem("got_w1")
    consts = Steps(sem("consts"), "zero_ident ident zero_before before ones iota eps_ln eps_gn")
    pool_w = Steps(sem("pool_weights"), "wo_hi wo_lo gate0_hi gate0_lo gate1_hi gate1_lo wsd_hi wsd_lo")
    dve_w = Steps(sem("dve_weights"), "wh_hi wh_lo wg_hi wg_lo")
    a_ln = Steps(sem("a_norm"), "stats aggr rstd xn", B)
    a_sd = Steps(sem("a_sdev"), "sd", B)
    a_tp = Steps(sem("a_turned"), "tp", B)
    a_thi = Steps(sem("a_turned_hi"), "hi", B)
    a_tlo = Steps(sem("a_turned_lo"), "lo", B)
    a_proj = Steps(sem("a_projected"), "qk gate", B)
    a_qhi = Steps(sem("a_qk_hi"), "hi", B)
    a_qlo = Steps(sem("a_qk_lo"), "lo", B)
    a_sc = Steps(sem("a_scored"), "s", B)
    a_gate = Steps(sem("a_gate"), "relu", B)
    a_gb = Steps(sem("a_gate_affine"), "beta gamma", B)
    b_mask = Steps(sem("b_masked"), "masked0 masked1 abs floor hi lo")
    b_chi = Steps(sem("b_ctx_hi"), "hi", B)
    b_clo = Steps(sem("b_ctx_lo"), "lo", B)
    b_u = Steps(sem("b_mixed"), "u", B)
    b_uhi = Steps(sem("b_mixed_hi"), "hi", B)
    b_ulo = Steps(sem("b_mixed_lo"), "lo", B)
    b_o = Steps(sem("b_heads"), "o", B)
    b_keep = Steps(sem("b_heads_kept"), "copy", B)
    b_stat = Steps(sem("b_heads_stats"), "stats", B)
    MOMENTS = "sum diff m2 mean sq var"
    mo = [Steps(sem(f"moments{i}"), MOMENTS) for i in range(4)]
    mo_sd = [Steps(sem(f"moments_sdev{i}"), "sd") for i in range(4)]
    mo_rs = [Steps(sem(f"moments_rstd{i}"), "rstd") for i in range(4)]
    c_wy = Steps(sem("c_gated"), "centred scaled", B)
    c_tp = Steps(sem("c_turned"), "tp", B)
    c_hi = Steps(sem("c_turned_hi"), "hi", B)
    c_lo = Steps(sem("c_turned_lo"), "lo", B)
    c_o = Steps(sem("c_out"), "o", B)
    c_res = Steps(sem("c_residual"), "add stats", B)
    d_xn = Steps(sem("d_norm"), "xn", B)
    d_st = [sem("d_stored0"), sem("d_stored1")]
    d_tp = Steps(sem("d_turned"), "tp", B)
    d_hi = Steps(sem("d_turned_hi"), "hi", B)
    d_lo = Steps(sem("d_turned_lo"), "lo", B)
    d_lg = Steps(sem("d_logits"), "logits", B)
    d_lgc = Steps(sem("d_logits_kept"), "copy", B)
    r_act = Steps(sem("r_scalar"), "tanh exp")
    r_iota = Steps(sem("r_iotas"), "rev steps128 j128 jrow code token")
    r_dve = Steps(sem("r_vector"), "cap max sub sum rsum prob "
                  "best1 is1 key1 first1 hot1 w1 rest best2 is2 key2 first2 hot2 w2 mask "
                  "count over tiles one8 tend tstart slot pick1 slot1 pick2 slot2 passed e emin eint "
                  "ge hotj tile_of row_of hotp r_code r_tok r_w none dest t_tok t_w t_dst")
    r_pe = Steps(sem("r_tensor"), "pos tab")
    e_tok = Steps(sem("e_tokens"), "copy", TILES0)
    e_dst = Steps(sem("e_destinations"), "copy", TILES0)
    e_xg = [sem("e_rows0"), sem("e_rows1")]
    e_yst = [sem("e_stored0"), sem("e_stored1")]
    e_tp = Steps(sem("e_turned"), "tp", TILES0)
    e_xT = Steps(sem("e_turned_kept"), "copy", TILES0)
    e_up = Steps(sem("e_up"), "a b", TILES0)
    e_silu = Steps(sem("e_silu"), "silu", TILES0)
    e_h = Steps(sem("e_hidden"), "h", TILES0)
    e_htp = Steps(sem("e_hidden_turned"), "tp", TILES0)
    e_hT = Steps(sem("e_hidden_kept"), "copy", TILES0)
    e_dn = Steps(sem("e_down"), "y", TILES0)
    e_ys = Steps(sem("e_weighted"), "y", TILES0)
    f_yin = [sem("f_rows0"), sem("f_rows1")]
    f_add = Steps(sem("f_added"), "y0 y1 stats", B)
    w1_sp = Steps(sem("w1_split"), " ".join(f"hi{i} lo{i}" for i in range(6)))
    got_c2 = [sem("got_ctx2_0"), sem("got_ctx2_1")]
    g_xn = Steps(sem("g_norm"), "xn", B)
    g_hi = Steps(sem("g_split_hi"), "ctx x", B)
    g_lo = Steps(sem("g_split_lo"), "ctx x", B)
    g_tp = Steps(sem("g_turned"), "tp", B)
    g_thi = Steps(sem("g_turned_hi"), "hi", B)
    g_tlo = Steps(sem("g_turned_lo"), "lo", B)
    g_sc = Steps(sem("g_scored"), "s", B)
    g_mx = Steps(sem("g_max"), "max neg", B)
    g_ex = Steps(sem("g_exp"), "e0 e1", B)
    g_rs = Steps(sem("g_rsum"), "r", B)
    g_ahi = Steps(sem("g_attn_hi"), "a0 a1", B)
    g_alo = Steps(sem("g_attn_lo"), "a0 a1", B)
    g_o = Steps(sem("g_out"), "o", B)
    g_res = Steps(sem("g_residual"), "add stats", B)
    h_xn = Steps(sem("h_norm"), "xn", B)
    h_tp = Steps(sem("h_turned"), "tp", B)
    h_thi = Steps(sem("h_turned_hi"), "hi", B)
    h_tlo = Steps(sem("h_turned_lo"), "lo", B)
    h_gs = Steps(sem("h_gate_shared"), "gs", B)
    h_act = Steps(sem("h_gate_scalar"), "exp silu", B)
    h_rt = Steps(sem("h_route"), "macc0 plus sig top index indexf hot mask sel sum rsum hs", B)
    h_pos = Steps(sem("h_position"), "pos", B)
    h_wt = Steps(sem("h_weights"), "valid wt", B)
    h_up = Steps(sem("h_up"), " ".join(f"u{c}" for c in range(NCH)), B)
    h_silu = Steps(sem("h_silu"), " ".join(f"s{c}" for c in range(NCH)), B)
    h_hv = Steps(sem("h_hidden"), " ".join(f"v{c} w{c}" for c in range(NCH)), B)
    h_htp = Steps(sem("h_hidden_turned"), " ".join(f"t{c}" for c in range(NCH + 1)), B)
    h_hhi = Steps(sem("h_hidden_hi"), " ".join(f"t{c}" for c in range(NCH + 1)), B)
    h_hlo = Steps(sem("h_hidden_lo"), " ".join(f"t{c}" for c in range(NCH + 1)), B)
    h_dn = Steps(sem("h_down"), " ".join(f"d{c}" for c in range(NCH + 1)), B)
    h_out = Steps(sem("h_result"), "out", B)
    h_st = [sem("h_stored0"), sem("h_stored1")]

    def h_slot(u, c):
        return (c + u) % 2

    def h_buffer(t, u, c):
        b = h_slot(u, c)
        if c == NCH:
            return b, (hT[0][0:HS, b, 0, :], hT[1][0:HS, b, 0, :]), hT_e[b][0:HS, 0, :]
        return b, (hT[0][:, b, :, :], hT[1][:, b, :, :]), hT_e[b]

    def wait_h_free(eng, t, c):
        if c >= 2:
            eng.wait_ge(h_dn.sem, h_dn.at(t, f"d{c - 2}"))
        elif not (isinstance(t, int) and t < 1):
            eng.wait_ge(h_dn.sem, h_dn.at(t - 1, f"d{NCH - 1 + c}"))

    def h_stages(f):
        order = []

        def put(lag, name, *args):
            if name in f:
                order.append((lag, f[name](*args) if args else f[name]))

        for c in range(NCH + 1):
            if c < NCH:
                put(1, "up", c)
                put(1, "silu", c)
                put(1, "vec", c)
            q = (c - 1) % (NCH + 1)
            lag = 1 if c >= 1 else 2
            put(lag, "tr", q)
            put(lag, "high", q)
            put(lag, "low", q)
            d = (c - 2) % (NCH + 1)
            lag = 1 if c >= 2 else 2
            put(lag, "down", d)
            if d == NCH:
                put(2, "result")
            if c == 0:
                put(0, "norm")
            if c == 1:
                put(0, "tr3")
                put(0, "turn")
                put(0, "low3")
            if c == 3:
                put(0, "gs")
                put(0, "gate")
                put(0, "route")
            if c == 5:
                put(0, "pos")
                put(0, "weights")
        return order

    block = st.enter_context(nc.Block())

    @block.sync
    def _(sp):
        def load_xc(t, u, r):
            if not early(t):
                wait_apart(sp, consts, (a_ln.sem, a_ln.at(t - 2, "xn")),
                           (a_tp.sem, a_tp.at(t - 2, "tp")))
            sp.dma_start(xin[:, u, :], x[bass.ds(t, 1), :, :].rearrange("a p d -> p (a d)")).then_inc(got_x[u], 16)
            sp.dma_start(cin[:, u, :], ctx[bass.ds(t, 1), :, :].rearrange("a p d -> p (a d)")).then_inc(got_c[u], 16)

        def load_c(t, u, r):
            if not early(t):
                wait_apart(sp, consts, (b_chi.sem, b_chi.at(t - 2, "hi")),
                           (b_clo.sem, b_clo.at(t - 2, "lo")))
            sp.dma_start(cin[:, u, :], ctx[bass.ds(t, 1), :, :].rearrange("a p d -> p (a d)")).then_inc(got_c[u], 16)

        def load_x(t, u, r):
            if not early(t):
                wait_apart(sp, consts, (c_res.sem, c_res.at(t - 2, "add")))
            sp.dma_start(xin[:, u, :], x[bass.ds(t, 1), :, :].rearrange("a p d -> p (a d)")).then_inc(got_x[u], 16)

        def store_rows(t, u, r):
            wait_apart(sp, consts, (d_xn.sem, d_xn.at(t, "xn")))
            sp.dma_start(xn_rows[bass.ds(t * P, P), :], xn[:, u, :]).then_inc(d_st[u], 16)

        def load_y(t, u, r):
            if not early(t):
                wait_apart(sp, consts, (f_add.sem, f_add.at(t - 2, "y1")))
            sp.dma_start(yin[:, u, :, :].rearrange("p k d -> p (k d)"),
                         y_rows[bass.ds(t * P * TOP0, P * TOP0), :].rearrange("(p k) d -> p (k d)", k=TOP0)
                         ).then_inc(f_yin[u], 16)

        def load_c2(t, u, r):
            if not early(t):
                wait_apart(sp, consts, (g_hi.sem, g_hi.at(t - 2, "ctx")),
                           (g_lo.sem, g_lo.at(t - 2, "ctx")),
                           (g_tp.sem, g_tp.at(t - 2, "tp")))
            sp.dma_start(cin2[:, u, :], ctx[bass.ds(t, 1), :, :].rearrange("a p d -> p (a d)")
                         ).then_inc(got_c2[u], 16)

        def store(t, u, r):
            wait_apart(sp, consts, (h_out.sem, h_out.at(t, "out")))
            sp.dma_start(out[bass.ds(t, 1), :, :].rearrange("a p d -> p (a d)"), outb[:, u, :]
                         ).then_inc(h_st[u], 16)

        pipeline(sp, B, (0, load_xc))
        after(sp, a_ln, a_tp)
        pipeline(sp, B, (0, load_c))
        pipeline(sp, B, (0, load_x))
        pipeline(sp, B, (0, store_rows))
        after(sp, r_dve, r_pe, r_iota)
        sp.dma_start(wup_raw[:, 0, :, :], wup[:, 0:P, :].rearrange("e p n -> p e n")).then_inc(got_w1, 16)
        sp.dma_start(wup_raw[:, 1, :, :], wup[:, P:D, :].rearrange("e p n -> p e n")).then_inc(got_w1, 16)
        sp.dma_start(wdn_raw[:, :, :], wdown.rearrange("(c e) h d -> (e h) c d", e=P // HID1)).then_inc(got_w1, 16)
        sp.wait_ge(e_yst[0], 16 * ((TILES0 + 1) // 2))
        sp.wait_ge(e_yst[1], 16 * (TILES0 // 2))
        pipeline(sp, B, (0, load_y))
        pipeline(sp, B, (0, load_c2))
        pipeline(sp, B, (0, store))
        for u in range(2):
            sp.wait_ge(h_st[u], 16 * (B // 2))
            sp.wait_ge(d_st[u], 16 * (B // 2))

    @block.gpsimd
    def _(pool):
        pool.memset(ident[:, :], 0.0).then_inc(consts.step("zero_ident"), 1)
        pool.wait_ge(consts.sem, consts.at(0, "zero_ident"))
        pool.affine_select(out=ident[:, :], in_=ident[:, :], compare_op=ALU.not_equal, fill=1.0, base=0,
                           pattern=[[-1, P]], channel_multiplier=1).then_inc(consts.step("ident"), 1)
        pool.memset(before[:, :], 0.0).then_inc(consts.step("zero_before"), 1)
        pool.wait_ge(consts.sem, consts.at(0, "zero_before"))
        pool.affine_select(out=before[:, :], in_=before[:, :], compare_op=ALU.is_ge, fill=1.0, base=0,
                           pattern=[[-1, P]], channel_multiplier=1).then_inc(consts.step("before"), 1)
        pool.memset(ones[:, :], 1.0).then_inc(consts.step("ones"), 1)
        pool.iota(iota_row[:, :], [[1, P]], base=0, channel_multiplier=0,
                  allow_small_or_imprecise_dtypes=True).then_inc(consts.step("iota"), 1)
        pool.memset(eps[:, 0:1], LN_EPS).then_inc(consts.step("eps_ln"), 1)
        pool.memset(eps[:, 1:2], GN_EPS).then_inc(consts.step("eps_gn"), 1)
        with pool.Fori(0, E0) as e:
            for a, w in ((0, w1), (1, w3)):
                pool.dma_start(W0[:, bass.ds(e, 1), a * KD * I0:(a + 1) * KD * I0]
                               .rearrange("p a (k n) -> p (a k) n", k=KD),
                               w[bass.ds(e, 1), :, :].rearrange("a (k p) n -> p (a k) n", p=P)).then_inc(got_w0, 16)
            pool.dma_start(W0[:, bass.ds(e, 1), 2 * KD * I0:W0E].rearrange("p a (k n) -> p (a k) n", k=KI),
                           w2[bass.ds(e, 1), :, :].rearrange("a (k p) n -> p (a k) n", p=P)).then_inc(got_w0, 16)
        for name, rawt, (hi, lo) in (("wo", wo_raw, wos), ("gate0", gate0_raw, gate0), ("gate1", gate1_raw, gate1),
                                     ("wsd", wsd_raw, wsd_s)):
            pool.wait_ge(small[name], 32 if name == "gate1" else 16)
            pool.tensor_copy(hi[:], rawt[:]).then_inc(pool_w.step(name + "_hi"), 1)
            pool.wait_ge(pool_w.sem, pool_w.at(0, name + "_hi"))
            pool.tensor_tensor(lo[:], rawt[:], hi[:].bitcast(F32), ALU.subtract).then_inc(pool_w.step(name + "_lo"), 1)

        def affine(t, u, r):
            wait_apart(pool, consts, (a_gate.sem, a_gate.at(t, "relu")))
            g = G[:, bass.ds(t, 1), :].rearrange("p a d -> p (a d)")
            pool.tensor_tensor(Gb[:, bass.ds(t, 1), :].rearrange("p a d -> p (a d)"), g, bet[:, :], ALU.mult
                               ).then_inc(a_gb.step("beta"), 1)
            wait_apart(pool, consts, (a_gb.sem, a_gb.at(t, "beta")))
            pool.tensor_tensor(g, g, gam[:, :], ALU.mult).then_inc(a_gb.step("gamma"), 1)

        pool.wait_ge(small["gamma"], 16)
        pool.wait_ge(small["beta"], 16)
        pipeline(pool, B, (0, affine))

        after(pool, d_xn, d_hi, d_lo, d_lg, c_wy, c_o)
        pool.iota(rt["rev"][:, :], [[-1, E0]], base=E0, channel_multiplier=0,
                  allow_small_or_imprecise_dtypes=True).then_inc(r_iota.step("rev"), 1)
        pool.iota(rt["steps128"][:, :], [[P, B]], base=0, channel_multiplier=0,
                  allow_small_or_imprecise_dtypes=True).then_inc(r_iota.step("steps128"), 1)
        pool.iota(rt["j128"][:, :], [[P, TJ + 1]], base=0, channel_multiplier=0,
                  allow_small_or_imprecise_dtypes=True).then_inc(r_iota.step("j128"), 1)
        pool.iota(rt["jrow"][:, :], [[1, TJ]], base=0, channel_multiplier=0,
                  allow_small_or_imprecise_dtypes=True).then_inc(r_iota.step("jrow"), 1)
        pool.iota(rt["val"][:, 0, :], [[1, TOP0], [P * TOP0, B]], base=1, channel_multiplier=TOP0,
                  allow_small_or_imprecise_dtypes=True).then_inc(r_iota.step("code"), 1)
        pool.iota(rt["val"][:, 1, :], [[0, TOP0], [P, B]], base=0, channel_multiplier=1,
                  allow_small_or_imprecise_dtypes=True).then_inc(r_iota.step("token"), 1)

        def gather(t, u, r):
            if not early(t):
                pool.wait_ge(e_xg[u], 16 * r)
            pool.tensor_copy(stage_g[:, u, :], table[:, 0, bass.ds(t, 1)]).then_inc(e_tok.step("copy"), 1)
            waits = [(e_tok.sem, e_tok.at(t, "copy"))]
            if not early(t):
                waits.append((e_tp.sem, e_tp.at(t - 2, "tp")))
            wait_apart(pool, consts, *waits)
            pool.indirect_dma_start(xg[:, u, :], None, xn_rows,
                                    bass.IndirectOffsetOnAxis(stage_g[:, u, :].bitcast(U32), 0)).then_inc(e_xg[u], 16)

        def scatter(t, u, r):
            if not early(t):
                pool.wait_ge(e_yst[u], 16 * r)
            pool.tensor_copy(stage_s[:, u, :], table[:, 1, bass.ds(t, 1)]).then_inc(e_dst.step("copy"), 1)
            wait_apart(pool, consts, (e_dst.sem, e_dst.at(t, "copy")), (e_ys.sem, e_ys.at(t, "y")))
            pool.indirect_dma_start(y_rows, bass.IndirectOffsetOnAxis(stage_s[:, u, :].bitcast(U32), 0),
                                    ys[:, u, :], None, bounds_check=B * P * TOP0 - 1, oob_is_err=False
                                    ).then_inc(e_yst[u], 16)

        after(pool, r_dve)
        for u in range(2):
            pool.wait_ge(d_st[u], 16 * (B // 2))
        pipeline(pool, TILES0, (0, gather), (3, scatter))

        pool.wait_ge(got_w1, 48)
        after(pool, e_dn)
        parts = [(wup_raw[:, k, e:e + 32, :], wup_s[0][:, k, e:e + 32, :], wup_s[1][:, k, e:e + 32, :])
                 for k in range(KD) for e in (0, 32)]
        parts += [(wdn_raw[:, k:k + 8, :], wdn_s[0][:, k:k + 8, :], wdn_s[1][:, k:k + 8, :]) for k in (0, 8)]
        for n, (rawt, hi, lo) in enumerate(parts):
            pool.tensor_copy(hi, rawt).then_inc(w1_sp.step(f"hi{n}"), 1)
            pool.wait_ge(w1_sp.sem, w1_sp.at(0, f"hi{n}"))
            pool.tensor_tensor(lo, rawt, hi.bitcast(F32), ALU.subtract).then_inc(w1_sp.step(f"lo{n}"), 1)

    @block.scalar
    def _(act):
        act.dma_start(wh_raw[:, :, :], Wh.rearrange("h d e -> d h e")).then_inc(small["wh"], 16)
        act.dma_start(wg_raw[:, :, :], wg.rearrange("(k p) n -> p k n", p=P)).then_inc(small["wg"], 16)
        act.dma_start(gam[:, :], gamma.rearrange("(a d) -> a d", a=1).broadcast_to([P, D])).then_inc(small["gamma"], 16)
        act.dma_start(bet[:, :], beta.rearrange("(a d) -> a d", a=1).broadcast_to([P, D])).then_inc(small["beta"], 16)
        act.dma_start(dec[:, :, :], decay).then_inc(small["decay"], 16)
        act.dma_start(wo_raw[:, :, :], wo.rearrange("(k p) n -> p k n", p=P)).then_inc(small["wo"], 16)
        act.dma_start(gate0_raw[:, :, :], wgate0.rearrange("(k p) n -> p k n", p=P)).then_inc(small["gate0"], 16)
        act.dma_start(gate1_raw[:, :, 0:E1], wgate1.rearrange("(k p) n -> p k n", p=P)).then_inc(small["gate1"], 16)
        act.dma_start(gate1_raw[:, :, E1:GS], wsu.rearrange("(k p) n -> p k n", p=P)).then_inc(small["gate1"], 16)
        act.dma_start(wsd_raw[:, :], wsd).then_inc(small["wsd"], 16)

        def a_sdev(t, u, r):
            act.wait_ge(a_ln.sem, a_ln.at(t, "aggr"))
            act.activation(sm[:, u, 8:9], sm[:, u, 7:8], ACT.Sqrt, bias=eps[:, 0:1]).then_inc(a_sd.step("sd"), 1)

        def a_hi(t, u, r):
            act.wait_ge(a_tp.sem, a_tp.at(t, "tp"))
            if not early(t):
                act.wait_ge(a_proj.sem, a_proj.at(t - 2, "gate"))
                act.wait_ge(a_tlo.sem, a_tlo.at(t - 2, "lo"))
            act.activation(tT[0][:, u, :, :], tp_a[u], ACT.Copy).then_inc(a_thi.step("hi"), 1)

        def a_qk(t, u, r):
            act.wait_ge(a_proj.sem, a_proj.at(t, "qk"))
            if not early(t):
                act.wait_ge(a_sc.sem, a_sc.at(t - 2, "s"))
                act.wait_ge(a_qlo.sem, a_qlo.at(t - 2, "lo"))
            act.activation(qk[0][:, u, :, :], qk_a[u], ACT.Copy).then_inc(a_qhi.step("hi"), 1)

        def a_relu(t, u, r):
            act.wait_ge(a_proj.sem, a_proj.at(t, "gate"))
            act.activation(G[:, bass.ds(t, 1), :].rearrange("p a d -> p (a d)"), g_a[u], ACT.Relu
                           ).then_inc(a_gate.step("relu"), 1)

        after(act, consts)
        pipeline(act, B, (0, a_sdev), (1, a_qk), (1, a_relu), (0, a_hi))
        after(act, a_sc, a_qlo)

        def b_ctx(t, u, r):
            act.wait_ge(got_c[u], 16 * (B // 2 + r + 1))
            if not early(t):
                act.wait_ge(b_u.sem, b_u.at(t - 2, "u"))
                act.wait_ge(b_clo.sem, b_clo.at(t - 2, "lo"))
            act.activation(tT[0][:, u, 0:2, :].rearrange("p k d -> p (k d)"), cin[:, u, :], ACT.Copy
                           ).then_inc(b_chi.step("hi"), 1)

        def b_mixed(t, u, r):
            act.wait_ge(b_u.sem, b_u.at(t, "u"))
            if not early(t):
                act.wait_ge(b_o.sem, b_o.at(t - 2, "o"))
                act.wait_ge(b_ulo.sem, b_ulo.at(t - 2, "lo"))
            act.activation(qk[0][:, u, 0:2, :], u_a[u], ACT.Copy).then_inc(b_uhi.step("hi"), 1)

        def b_kept(t, u, r):
            act.wait_ge(b_o.sem, b_o.at(t, "o"))
            act.activation(x_res[:, bass.ds(t, 1), :].rearrange("p a d -> p (a d)"), row_a[u], ACT.Copy
                           ).then_inc(b_keep.step("copy"), 1)

        pipeline(act, B, (0, b_ctx), (1, b_mixed), (2, b_kept))

        def sdev_all(i, e):
            act.wait_ge(mo[i].sem, mo[i].at(0, "var"))
            act.activation(sdev[:, :], mom[:, 4, :], ACT.Sqrt, bias=eps[:, e:e + 1], scale=1.0 / D).then_inc(mo_sd[i].step("sd"), 1)

        sdev_all(0, 1)
        after(act, b_o, b_ulo)

        def c_split(t, u, r):
            act.wait_ge(c_tp.sem, c_tp.at(t, "tp"))
            if not early(t):
                act.wait_ge(c_o.sem, c_o.at(t - 2, "o"))
                act.wait_ge(c_lo.sem, c_lo.at(t - 2, "lo"))
            act.activation(tT[0][:, u, 0:2, :], two_a[u], ACT.Copy).then_inc(c_hi.step("hi"), 1)

        pipeline(act, B, (0, c_split))
        sdev_all(1, 0)
        after(act, c_o, c_lo)

        def d_split(t, u, r):
            act.wait_ge(d_tp.sem, d_tp.at(t, "tp"))
            if not early(t):
                act.wait_ge(d_lg.sem, d_lg.at(t - 2, "logits"))
                act.wait_ge(d_lo.sem, d_lo.at(t - 2, "lo"))
            act.activation(tT[0][:, u, 0:2, :], two_a[u], ACT.Copy).then_inc(d_hi.step("hi"), 1)

        def d_keep(t, u, r):
            act.wait_ge(d_lg.sem, d_lg.at(t, "logits"))
            act.activation(lg[:, bass.ds(t, 1), :].rearrange("p a e -> p (a e)"), lg_a[u], ACT.Copy
                           ).then_inc(d_lgc.step("copy"), 1)

        pipeline(act, B, (0, d_split), (1, d_keep))

        after(act, d_lgc)
        act.activation(lg[:, :, :], lg[:, :, :], ACT.Tanh, scale=1.0 / SOFTCAP).then_inc(r_act.step("tanh"), 1)
        act.wait_ge(r_dve.sem, r_dve.at(0, "sub"))
        act.activation(rt["prob"][:, :, :], lg[:, :, :], ACT.Exp).then_inc(r_act.step("exp"), 1)

        def e_rows(t, u, r):
            act.wait_ge(e_tp.sem, e_tp.at(t, "tp"))
            if not early(t):
                act.wait_ge(e_up.sem, e_up.at(t - 2, "b"))
            act.activation(xTc[:, u, :, :], xT_c[u], ACT.Copy).then_inc(e_xT.step("copy"), 1)

        def e_act(t, u, r):
            act.wait_ge(e_up.sem, e_up.at(t, "a"))
            if not early(t):
                act.wait_ge(e_h.sem, e_h.at(t - 2, "h"))
            act.activation(sa[:, u, :], up_c[u][0], ACT.Silu).then_inc(e_silu.step("silu"), 1)

        def e_hid(t, u, r):
            act.wait_ge(e_htp.sem, e_htp.at(t, "tp"))
            if not early(t):
                act.wait_ge(e_dn.sem, e_dn.at(t - 2, "y"))
            act.activation(hTc[:, u, :, :], hT_c, ACT.Copy).then_inc(e_hT.step("copy"), 1)

        after(act, r_dve, r_pe)
        pipeline(act, TILES0, (0, e_rows), (1, e_act), (2, e_hid))

        sdev_all(2, 0)

        def g_high(t, u, r):
            act.wait_ge(got_c2[u], 16 * (r + 1))
            if not early(t):
                act.wait_ge(g_sc.sem, g_sc.at(t - 2, "s"))
                act.wait_ge(g_lo.sem, g_lo.at(t - 2, "x"))
            act.activation(cs[0][:, u, :], cin2[:, u, :], ACT.Copy).then_inc(g_hi.step("ctx"), 1)
            act.wait_ge(g_xn.sem, g_xn.at(t, "xn"))
            act.activation(xs[0][:, u, :], xn2[:, u, :], ACT.Copy).then_inc(g_hi.step("x"), 1)

        def g_turn(t, u, r):
            act.wait_ge(g_tp.sem, g_tp.at(t, "tp"))
            if not early(t):
                act.wait_ge(g_o.sem, g_o.at(t - 2, "o"))
                act.wait_ge(g_tlo.sem, g_tlo.at(t - 2, "lo"))
            act.activation(cT[0][:, u, :, :], cT_d[u], ACT.Copy).then_inc(g_thi.step("hi"), 1)

        def g_expo(t, u, r):
            act.wait_ge(g_mx.sem, g_mx.at(t, "neg"))
            if not early(t):
                act.wait_ge(g_ahi.sem, g_ahi.at(t - 2, "a1"))
                act.wait_ge(g_alo.sem, g_alo.at(t - 2, "a1"))
            for k in range(KD):
                act.activation(ex[:, u, k, :], sc_d[u][:, k, :], ACT.Exp, bias=smx[:, u, 1, k:k + 1],
                               scale=D ** -0.5, accum_out=smx[:, u, 2, k:k + 1]).then_inc(g_ex.step(f"e{k}"), 1)

        def g_attn(t, u, r):
            act.wait_ge(g_rs.sem, g_rs.at(t, "r"))
            if not early(t):
                act.wait_ge(g_o.sem, g_o.at(t - 2, "o"))
            for k in range(KD):
                act.activation(at[0][:, u, k, :], ex[:, u, k, :], ACT.Copy, scale=smx[:, u, 3, k:k + 1]
                               ).then_inc(g_ahi.step(f"a{k}"), 1)

        after(act, e_ys, f_add)
        pipeline(act, B, (0, g_high), (0, g_turn), (1, g_expo), (1, g_attn))
        sdev_all(3, 0)
        after(act, g_o, g_res)

        def h_turn(t, u, r):
            act.wait_ge(h_tp.sem, h_tp.at(t, "tp"))
            if not early(t):
                act.wait_ge(h_up.sem, h_up.at(t - 2, f"u{NCH - 1}"))
                act.wait_ge(h_tlo.sem, h_tlo.at(t - 2, "lo"))
            act.activation(x3T[0][:, u, :, :], x3T_e, ACT.Copy).then_inc(h_thi.step("hi"), 1)

        def h_gate(t, u, r):
            act.wait_ge(h_gs.sem, h_gs.at(t, "gs"))
            if not early(t):
                act.wait_ge(h_rt.sem, h_rt.at(t - 2, "hs"))
            act.activation(esc[:, u, :], gs_e[:, 0:E1], ACT.Exp, scale=-1.0).then_inc(h_act.step("exp"), 1)
            act.activation(sgs[:, u, :], gs_e[:, E1 + HS:GS], ACT.Silu).then_inc(h_act.step("silu"), 1)

        def h_act_c(c):
            def body(t, u, r):
                act.wait_ge(h_up.sem, h_up.at(t, f"u{c}"))
                if c >= 2:
                    act.wait_ge(h_hv.sem, h_hv.at(t, f"v{c - 2}"))
                elif not (isinstance(t, int) and t < 1):
                    act.wait_ge(h_hv.sem, h_hv.at(t - 1, f"v{NCH - 2 + c}"))
                act.activation(sg[:, c % 2, :, :], up_e[c % 2][:, :, 0:HID1], ACT.Silu
                               ).then_inc(h_silu.step(f"s{c}"), 1)
            return body

        def h_high(c):
            def body(t, u, r):
                act.wait_ge(h_htp.sem, h_htp.at(t, f"t{c}"))
                b, out_t, in_t = h_buffer(t, u, c)
                wait_h_free(act, t, c)
                act.activation(out_t[0], in_t, ACT.Copy).then_inc(h_hhi.step(f"t{c}"), 1)
            return body

        pipeline(act, B, *h_stages(dict(turn=h_turn, gate=h_gate, silu=h_act_c, high=h_high)))

    @block.vector
    def _(dve):
        for name, rawt, (hi, lo) in (("wh", wh_raw, wh), ("wg", wg_raw, wgs)):
            dve.wait_ge(small[name], 16)
            dve.tensor_copy(hi[:], rawt[:]).then_inc(dve_w.step(name + "_hi"), 1)
            dve.wait_ge(dve_w.sem, dve_w.at(0, name + "_hi"))
            dve.tensor_tensor(lo[:], rawt[:], hi[:].bitcast(F32), ALU.subtract).then_inc(dve_w.step(name + "_lo"), 1)

        def row(buf, t):
            return buf[:, bass.ds(t, 1), :].rearrange("p a d -> p (a d)")

        def a_norm(t, u, r):
            dve.wait_ge(got_x[u], 16 * (r + 1))
            dve.bn_stats(sm[:, u, 0:6], xin[:, u, :]).then_inc(a_ln.step("stats"), 1)
            wait_apart(dve, consts, (a_ln.sem, a_ln.at(t, "stats")))
            dve.bn_aggr(sm[:, u, 6:8], sm[:, u, 0:6]).then_inc(a_ln.step("aggr"), 1)
            dve.wait_ge(a_sd.sem, a_sd.at(t, "sd"))
            dve.reciprocal(sm[:, u, 9:10], sm[:, u, 8:9]).then_inc(a_ln.step("rstd"), 1)
            dve.wait_ge(a_ln.sem, a_ln.at(t, "rstd"))
            if not early(t):
                dve.wait_ge(a_tp.sem, a_tp.at(t - 2, "tp"))
            dve.tensor_scalar(xn[:, u, :], xin[:, u, :], sm[:, u, 6:7], sm[:, u, 9:10], ALU.subtract, ALU.mult
                              ).then_inc(a_ln.step("xn"), 1)

        def a_low(t, u, r):
            dve.wait_ge(a_thi.sem, a_thi.at(t, "hi"))
            if not early(t):
                dve.wait_ge(a_proj.sem, a_proj.at(t - 2, "gate"))
            dve.tensor_tensor(tT[1][:, u, :, :], tp_a[u], tT[0][:, u, :, :].bitcast(F32), ALU.subtract
                              ).then_inc(a_tlo.step("lo"), 1)

        def a_qklow(t, u, r):
            dve.wait_ge(a_qhi.sem, a_qhi.at(t, "hi"))
            if not early(t):
                dve.wait_ge(a_sc.sem, a_sc.at(t - 2, "s"))
            dve.tensor_tensor(qk[1][:, u, :, :], qk_a[u], qk[0][:, u, :, :].bitcast(F32), ALU.subtract
                              ).then_inc(a_qlo.step("lo"), 1)

        pipeline(dve, B, (0, a_norm), (0, a_low), (1, a_qklow))

        after(dve, a_sc)
        dve.wait_ge(small["decay"], 16)
        for h in range(H0):
            dve.tensor_tensor(Araw[:, h, :], S_a[h], dec[:, h, :], ALU.mult).then_inc(b_mask.step(f"masked{h}"), 1)
        dve.wait_ge(b_mask.sem, b_mask.at(0, "masked1"))
        dve.scalar_tensor_tensor(out=Araw[:, :, :], in0=Araw[:, :, :], scalar=-1.0, in1=Araw[:, :, :],
                                 op0=ALU.mult, op1=ALU.max).then_inc(b_mask.step("abs"), 1)
        dve.wait_ge(b_mask.sem, b_mask.at(0, "abs"))
        dve.tensor_scalar(Araw[:, :, :], Araw[:, :, :], 1.0, None, ALU.max).then_inc(b_mask.step("floor"), 1)
        dve.wait_ge(b_mask.sem, b_mask.at(0, "floor"))
        dve.tensor_copy(At[0][:, :, :], Araw[:, :, :]).then_inc(b_mask.step("hi"), 1)
        dve.wait_ge(b_mask.sem, b_mask.at(0, "hi"))
        dve.tensor_tensor(At[1][:, :, :], Araw[:, :, :], At[0][:, :, :].bitcast(F32), ALU.subtract
                          ).then_inc(b_mask.step("lo"), 1)

        def b_ctx(t, u, r):
            dve.wait_ge(b_chi.sem, b_chi.at(t, "hi"))
            if not early(t):
                dve.wait_ge(b_u.sem, b_u.at(t - 2, "u"))
            dve.tensor_tensor(tT[1][:, u, 0:2, :].rearrange("p k d -> p (k d)"), cin[:, u, :],
                              tT[0][:, u, 0:2, :].rearrange("p k d -> p (k d)").bitcast(F32), ALU.subtract
                              ).then_inc(b_clo.step("lo"), 1)

        def b_mixed(t, u, r):
            dve.wait_ge(b_uhi.sem, b_uhi.at(t, "hi"))
            if not early(t):
                dve.wait_ge(b_o.sem, b_o.at(t - 2, "o"))
            dve.tensor_tensor(qk[1][:, u, 0:2, :], u_a[u], qk[0][:, u, 0:2, :].bitcast(F32), ALU.subtract
                              ).then_inc(b_ulo.step("lo"), 1)

        def b_stats(t, u, r):
            dve.wait_ge(b_keep.sem, b_keep.at(t, "copy"))
            dve.bn_stats(row(bn, t), row_a[u]).then_inc(b_stat.step("stats"), 1)

        pipeline(dve, B, (0, b_ctx), (1, b_mixed), (2, b_stats))

        def moments(i, stats, e):
            m = mo[i]
            after(dve, stats)
            dve.tensor_tensor(mom[:, 0, :], bn[:, :, 1], bn[:, :, 4], ALU.add).then_inc(m.step("sum"), 1)
            dve.tensor_tensor(mom[:, 1, :], bn[:, :, 1], bn[:, :, 4], ALU.subtract).then_inc(m.step("diff"), 1)
            dve.tensor_tensor(mom[:, 2, :], bn[:, :, 2], bn[:, :, 5], ALU.add).then_inc(m.step("m2"), 1)
            dve.wait_ge(m.sem, m.at(0, "m2"))
            dve.tensor_scalar(mean[:, :], mom[:, 0, :], 0.5, None, ALU.mult).then_inc(m.step("mean"), 1)
            dve.scalar_tensor_tensor(out=mom[:, 3, :], in0=mom[:, 1, :], scalar=D / 4.0, in1=mom[:, 1, :],
                                     op0=ALU.mult, op1=ALU.mult).then_inc(m.step("sq"), 1)
            dve.wait_ge(m.sem, m.at(0, "sq"))
            dve.tensor_tensor(mom[:, 4, :], mom[:, 3, :], mom[:, 2, :], ALU.add).then_inc(m.step("var"), 1)
            dve.wait_ge(mo_sd[i].sem, mo_sd[i].at(0, "sd"))
            dve.reciprocal(rstd[:, :], sdev[:, :]).then_inc(mo_rs[i].step("rstd"), 1)
            dve.wait_ge(mo_rs[i].sem, mo_rs[i].at(0, "rstd"))

        moments(0, b_stat, 1)
        after(dve, b_keep, a_gb, b_o)

        def c_gate(t, u, r):
            dve.scalar_tensor_tensor(out=cin[:, u, :], in0=row(x_res, t), scalar=mean[:, bass.ds(t, 1)],
                                     in1=row(G, t), op0=ALU.subtract, op1=ALU.mult).then_inc(c_wy.step("centred"), 1)
            dve.wait_ge(c_wy.sem, c_wy.at(t, "centred"))
            if not early(t):
                dve.wait_ge(c_tp.sem, c_tp.at(t - 2, "tp"))
            dve.scalar_tensor_tensor(out=xn[:, u, :], in0=cin[:, u, :], scalar=rstd[:, bass.ds(t, 1)],
                                     in1=row(Gb, t), op0=ALU.mult, op1=ALU.add).then_inc(c_wy.step("scaled"), 1)

        def c_low(t, u, r):
            dve.wait_ge(c_hi.sem, c_hi.at(t, "hi"))
            if not early(t):
                dve.wait_ge(c_o.sem, c_o.at(t - 2, "o"))
            dve.tensor_tensor(tT[1][:, u, 0:2, :], two_a[u], tT[0][:, u, 0:2, :].bitcast(F32), ALU.subtract
                              ).then_inc(c_lo.step("lo"), 1)

        def c_add(t, u, r):
            dve.wait_ge(c_o.sem, c_o.at(t, "o"))
            dve.wait_ge(got_x[u], 16 * (B // 2 + r + 1))
            dve.tensor_tensor(row(x_res, t), row_a[u], xin[:, u, :], ALU.add).then_inc(c_res.step("add"), 1)
            dve.wait_ge(c_res.sem, c_res.at(t, "add"))
            dve.bn_stats(row(bn, t), row(x_res, t)).then_inc(c_res.step("stats"), 1)

        pipeline(dve, B, (0, c_gate), (0, c_low), (1, c_add))
        moments(1, c_res, 0)

        after(dve, c_tp, c_o)

        def d_norm(t, u, r):
            if not early(t):
                dve.wait_ge(d_tp.sem, d_tp.at(t - 2, "tp"))
                dve.wait_ge(d_st[u], 16 * r)
            dve.tensor_scalar(xn[:, u, :], row(x_res, t), mean[:, bass.ds(t, 1)], rstd[:, bass.ds(t, 1)],
                              ALU.subtract, ALU.mult).then_inc(d_xn.step("xn"), 1)

        def d_low(t, u, r):
            dve.wait_ge(d_hi.sem, d_hi.at(t, "hi"))
            if not early(t):
                dve.wait_ge(d_lg.sem, d_lg.at(t - 2, "logits"))
            dve.tensor_tensor(tT[1][:, u, 0:2, :], two_a[u], tT[0][:, u, 0:2, :].bitcast(F32), ALU.subtract
                              ).then_inc(d_lo.step("lo"), 1)

        pipeline(dve, B, (0, d_norm), (0, d_low))

        R = r_dve

        def own(name):
            dve.wait_ge(R.sem, R.at(0, name))

        def over(ap, *shape):
            return ap.to_broadcast([P, *shape])

        after(dve, r_iota, d_lg)
        for u in range(2):
            dve.wait_ge(d_st[u], 16 * (B // 2))
        dve.wait_ge(r_act.sem, r_act.at(0, "tanh"))
        prob, rest, key, m, k_ = rt["prob"], rt["rest"], rt["key"], rt["m"], rt["k"]
        dve.tensor_scalar(lg[:, :, :], lg[:, :, :], SOFTCAP, None, ALU.mult).then_inc(R.step("cap"), 1)
        own("cap")
        dve.tensor_reduce(m[:, :], lg[:, :, :], X, ALU.max).then_inc(R.step("max"), 1)
        own("max")
        dve.tensor_tensor(lg[:, :, :], lg[:, :, :], over(m[:, :].unsqueeze(2), B, E0), ALU.subtract
                          ).then_inc(R.step("sub"), 1)
        dve.wait_ge(r_act.sem, r_act.at(0, "exp"))
        dve.tensor_reduce(m[:, :], prob[:, :, :], X, ALU.add).then_inc(R.step("sum"), 1)
        own("sum")
        dve.reciprocal(rt["r"][:, :], m[:, :]).then_inc(R.step("rsum"), 1)
        own("rsum")
        dve.tensor_tensor(prob[:, :, :], prob[:, :, :], over(rt["r"][:, :].unsqueeze(2), B, E0), ALU.mult
                          ).then_inc(R.step("prob"), 1)
        own("prob")
        for n, source in ((1, prob), (2, rest)):
            hot_n = rt[f"hot{n}"]
            dve.tensor_reduce(rt["val"][:, 2, (n - 1) * B:n * B], source[:, :, :], X, ALU.max
                              ).then_inc(R.step(f"best{n}"), 1)
            own(f"best{n}")
            best = over(rt["val"][:, 2, (n - 1) * B:n * B].unsqueeze(2), B, E0)
            dve.tensor_tensor(key[:, :, :], source[:, :, :], best, ALU.is_equal).then_inc(R.step(f"is{n}"), 1)
            own(f"is{n}")
            dve.tensor_tensor(key[:, :, :], key[:, :, :], over(rt["rev"][:, :].unsqueeze(1), B, E0), ALU.mult
                              ).then_inc(R.step(f"key{n}"), 1)
            own(f"key{n}")
            dve.tensor_reduce(k_[:, :], key[:, :, :], X, ALU.max).then_inc(R.step(f"first{n}"), 1)
            own(f"first{n}")
            dve.tensor_tensor(hot_n[:, :, :], key[:, :, :], over(k_[:, :].unsqueeze(2), B, E0), ALU.is_equal
                              ).then_inc(R.step(f"hot{n}"), 1)
            own(f"hot{n}")
            dve.tensor_copy(rt["wsel"][:, n - 1, :], rt["val"][:, 2, (n - 1) * B:n * B]).then_inc(R.step(f"w{n}"), 1)
            if n == 1:
                dve.scalar_tensor_tensor(out=rest[:, :, :], in0=hot_n[:, :, :], scalar=-4.0, in1=prob[:, :, :],
                                         op0=ALU.mult, op1=ALU.add).then_inc(R.step("rest"), 1)
                own("rest")
        dve.tensor_tensor(mask0[:, :, :], rt["hot1"][:, :, :], rt["hot2"][:, :, :], ALU.add).then_inc(R.step("mask"), 1)
        dve.wait_ge(r_pe.sem, r_pe.at(0, "pos"))
        dve.tensor_copy(rt["cnt"][:, :], pos_r[:, B, :]).then_inc(R.step("count"), 1)
        own("count")
        two = rt["over"]
        dve.tensor_tensor(two[:, :, :], over(rt["cnt"][:, :].unsqueeze(2), E0, B),
                          over(rt["steps128"][:, :].unsqueeze(1), E0, B), ALU.is_gt).then_inc(R.step("over"), 1)
        own("over")
        dve.tensor_reduce(rt["tiles"][:, :], two[:, :, :], X, ALU.add).then_inc(R.step("tiles"), 1)
        dve.memset(rt["one8"][:, :], 1.0).then_inc(R.step("one8"), 1)
        own("one8")
        dve.tensor_tensor_scan(rt["tend"][:, :], rt["one8"][:, :], rt["tiles"][:, :], 0.0, ALU.mult, ALU.add
                               ).then_inc(R.step("tend"), 1)
        own("tend")
        dve.tensor_tensor(rt["tstart"][:, :], rt["tend"][:, :], rt["tiles"][:, :], ALU.subtract
                          ).then_inc(R.step("tstart"), 1)
        own("tstart")
        dve.scalar_tensor_tensor(out=rt["slot"][:, :, :], in0=over(rt["tstart"][:, :].unsqueeze(1), B, E0),
                                 scalar=float(P), in1=pos_r[:, 0:B, :], op0=ALU.mult, op1=ALU.add
                                 ).then_inc(R.step("slot"), 1)
        own("slot")
        for n in (1, 2):
            dve.tensor_tensor(rt["pick"][:, :, :], rt["slot"][:, :, :], rt[f"hot{n}"][:, :, :], ALU.mult
                              ).then_inc(R.step(f"pick{n}"), 1)
            own(f"pick{n}")
            dve.tensor_reduce(rt["slotk"][:, n - 1, :], rt["pick"][:, :, :], X, ALU.add).then_inc(R.step(f"slot{n}"), 1)
            own(f"slot{n}")
        dve.tensor_tensor(rt["passed"][:, :, :], over(rt["tend"][:, :].unsqueeze(1), TJ, E0),
                          over(rt["jrow"][:, :].unsqueeze(2), TJ, E0), ALU.is_le).then_inc(R.step("passed"), 1)
        own("passed")
        dve.tensor_reduce(rt["ef"][:, :], rt["passed"][:, :, :], X, ALU.add).then_inc(R.step("e"), 1)
        own("e")
        dve.tensor_scalar(rt["ef"][:, :], rt["ef"][:, :], float(E0 - 1), None, ALU.min).then_inc(R.step("emin"), 1)
        own("emin")
        dve.tensor_copy(expert_of[:, :], rt["ef"][:, :]).then_inc(R.step("eint"), 1)
        slotk = rt["slotk"][:, :, :].rearrange("p k b -> p (k b)")
        dve.tensor_tensor(rt["ge"][:, :, :], over(slotk.unsqueeze(2), NPAIR, TJ + 1),
                          over(rt["j128"][:, :].unsqueeze(1), NPAIR, TJ + 1), ALU.is_ge).then_inc(R.step("ge"), 1)
        own("ge")
        dve.tensor_tensor(rt["hotj"][:, :, :], rt["ge"][:, :, 0:TJ], rt["ge"][:, :, 1:TJ + 1], ALU.subtract
                          ).then_inc(R.step("hotj"), 1)
        dve.tensor_reduce(rt["tile_of"][:, :], rt["ge"][:, :, 1:TJ + 1], X, ALU.add).then_inc(R.step("tile_of"), 1)
        own("tile_of")
        dve.scalar_tensor_tensor(out=rt["row_of"][:, :], in0=rt["tile_of"][:, :], scalar=-float(P), in1=slotk,
                                 op0=ALU.mult, op1=ALU.add).then_inc(R.step("row_of"), 1)
        own("row_of")
        dve.tensor_tensor(rt["hotp"][:, :, :], over(rt["row_of"][:, :].unsqueeze(2), NPAIR, P),
                          over(iota_row[:, :].unsqueeze(1), NPAIR, P), ALU.is_equal).then_inc(R.step("hotp"), 1)
        for n, name in enumerate(("r_code", "r_tok", "r_w")):
            dve.tensor_tensor(rt["R"][:, :, n, :], rt["hotj"][:, :, :], over(rt["val"][:, n, :].unsqueeze(2), NPAIR, TJ),
                              ALU.mult).then_inc(R.step(name), 1)
        dve.wait_ge(r_pe.sem, r_pe.at(0, "tab"))
        dve.tensor_scalar(rt["none"][:, :], tab_r[:, 0, :], 0.0, NOWHERE, ALU.is_equal, ALU.mult
                          ).then_inc(R.step("none"), 1)
        own("none")
        dve.scalar_tensor_tensor(out=rt["T"][:, 0, :], in0=tab_r[:, 0, :], scalar=-1.0, in1=rt["none"][:, :],
                                 op0=ALU.add, op1=ALU.add).then_inc(R.step("dest"), 1)
        dve.tensor_copy(table[:, 0, :], tab_r[:, 1, :]).then_inc(R.step("t_tok"), 1)
        dve.tensor_copy(table[:, 2, :].bitcast(F32), tab_r[:, 2, :]).then_inc(R.step("t_w"), 1)
        own("dest")
        dve.tensor_copy(table[:, 1, :], rt["T"][:, 0, :]).then_inc(R.step("t_dst"), 1)

        def e_hidden(t, u, r):
            dve.wait_ge(e_silu.sem, e_silu.at(t, "silu"))
            dve.wait_ge(e_up.sem, e_up.at(t, "b"))
            if not early(t):
                dve.wait_ge(e_htp.sem, e_htp.at(t - 2, "tp"))
            dve.tensor_tensor(hh[:, u, :], sa[:, u, :], up_c[u][1], ALU.mult).then_inc(e_h.step("h"), 1)

        def e_weigh(t, u, r):
            dve.wait_ge(e_dn.sem, e_dn.at(t, "y"))
            if not early(t):
                dve.wait_ge(e_yst[u], 16 * r)
            dve.tensor_scalar(ys[:, u, :], y_c, table[:, 2, bass.ds(t, 1)].bitcast(F32), None, ALU.mult
                              ).then_inc(e_ys.step("y"), 1)

        after(dve, R)
        pipeline(dve, TILES0, (1, e_hidden), (2, e_weigh))

        def f_sum(t, u, r):
            dve.wait_ge(f_yin[u], 16 * (r + 1))
            dve.tensor_tensor(yin[:, u, 0, :], yin[:, u, 0, :], yin[:, u, 1, :], ALU.add).then_inc(f_add.step("y0"), 1)
            dve.wait_ge(f_add.sem, f_add.at(t, "y0"))
            dve.tensor_tensor(row(x_res, t), row(x_res, t), yin[:, u, 0, :], ALU.add).then_inc(f_add.step("y1"), 1)
            dve.wait_ge(f_add.sem, f_add.at(t, "y1"))
            dve.bn_stats(row(bn, t), row(x_res, t)).then_inc(f_add.step("stats"), 1)

        pipeline(dve, B, (0, f_sum))
        moments(2, f_add, 0)

        def g_norm(t, u, r):
            if not early(t):
                dve.wait_ge(g_hi.sem, g_hi.at(t - 2, "x"))
                dve.wait_ge(g_lo.sem, g_lo.at(t - 2, "x"))
            dve.tensor_scalar(xn2[:, u, :], row(x_res, t), mean[:, bass.ds(t, 1)], rstd[:, bass.ds(t, 1)],
                              ALU.subtract, ALU.mult).then_inc(g_xn.step("xn"), 1)

        def g_low(t, u, r):
            dve.wait_ge(g_hi.sem, g_hi.at(t, "x"))
            if not early(t):
                dve.wait_ge(g_sc.sem, g_sc.at(t - 2, "s"))
            dve.tensor_tensor(cs[1][:, u, :], cin2[:, u, :], cs[0][:, u, :].bitcast(F32), ALU.subtract
                              ).then_inc(g_lo.step("ctx"), 1)
            dve.tensor_tensor(xs[1][:, u, :], xn2[:, u, :], xs[0][:, u, :].bitcast(F32), ALU.subtract
                              ).then_inc(g_lo.step("x"), 1)

        def g_turnlow(t, u, r):
            dve.wait_ge(g_thi.sem, g_thi.at(t, "hi"))
            if not early(t):
                dve.wait_ge(g_o.sem, g_o.at(t - 2, "o"))
            dve.tensor_tensor(cT[1][:, u, :, :], cT_d[u], cT[0][:, u, :, :].bitcast(F32), ALU.subtract
                              ).then_inc(g_tlo.step("lo"), 1)

        def g_max(t, u, r):
            dve.wait_ge(g_sc.sem, g_sc.at(t, "s"))
            dve.tensor_reduce(smx[:, u, 0, :], sc_d[u], X, ALU.max).then_inc(g_mx.step("max"), 1)
            dve.wait_ge(g_mx.sem, g_mx.at(t, "max"))
            dve.tensor_scalar(smx[:, u, 1, :], smx[:, u, 0, :], -(D ** -0.5), None, ALU.mult
                              ).then_inc(g_mx.step("neg"), 1)

        def g_soft(t, u, r):
            dve.wait_ge(g_ex.sem, g_ex.at(t, "e1"))
            dve.reciprocal(smx[:, u, 3, :], smx[:, u, 2, :]).then_inc(g_rs.step("r"), 1)
            if not early(t):
                dve.wait_ge(g_o.sem, g_o.at(t - 2, "o"))
            for k in range(KD):
                dve.wait_ge(g_ahi.sem, g_ahi.at(t, f"a{k}"))
                dve.scalar_tensor_tensor(out=at[1][:, u, k, :], in0=ex[:, u, k, :], scalar=smx[:, u, 3, k:k + 1],
                                         in1=at[0][:, u, k, :].bitcast(F32), op0=ALU.mult, op1=ALU.subtract
                                         ).then_inc(g_alo.step(f"a{k}"), 1)

        def g_add(t, u, r):
            dve.wait_ge(g_o.sem, g_o.at(t, "o"))
            dve.tensor_tensor(row(x_res, t), o_d[u], row(x_res, t), ALU.add).then_inc(g_res.step("add"), 1)
            dve.wait_ge(g_res.sem, g_res.at(t, "add"))
            dve.bn_stats(row(bn, t), row(x_res, t)).then_inc(g_res.step("stats"), 1)

        pipeline(dve, B, (0, g_norm), (0, g_low), (0, g_turnlow), (1, g_max), (1, g_soft), (2, g_add))
        moments(3, g_res, 0)

        def h_norm(t, u, r):
            if not early(t):
                dve.wait_ge(h_tp.sem, h_tp.at(t - 2, "tp"))
            dve.tensor_scalar(xn3[:, u, :], row(x_res, t), mean[:, bass.ds(t, 1)], rstd[:, bass.ds(t, 1)],
                              ALU.subtract, ALU.mult).then_inc(h_xn.step("xn"), 1)

        def h_low3(t, u, r):
            dve.wait_ge(h_thi.sem, h_thi.at(t, "hi"))
            if not early(t):
                dve.wait_ge(h_up.sem, h_up.at(t - 2, f"u{NCH - 1}"))
            dve.tensor_tensor(x3T[1][:, u, :, :], x3T_e, x3T[0][:, u, :, :].bitcast(F32), ALU.subtract
                              ).then_inc(h_tlo.step("lo"), 1)

        def h_route(t, u, r):
            Q = h_rt

            def mine(name):
                dve.wait_ge(Q.sem, Q.at(t, name))

            if isinstance(t, int) and t == 0:
                dve.memset(macc[:, 0, :], 0.0).then_inc(Q.step("macc0"), 1)
            else:
                if not early(t):
                    dve.wait_ge(h_pos.sem, h_pos.at(t - 2, "pos"))
                dve.tensor_tensor(macc[:, u, :], macc[:, 1 - u, :], mask1[:, 1 - u, :], ALU.add
                                  ).then_inc(Q.step("macc0"), 1)
            dve.wait_ge(h_act.sem, h_act.at(t, "exp"))
            dve.tensor_scalar(esc[:, u, :], esc[:, u, :], 1.0, None, ALU.add).then_inc(Q.step("plus"), 1)
            mine("plus")
            dve.reciprocal(sc[:, u, :], esc[:, u, :]).then_inc(Q.step("sig"), 1)
            wait_apart(dve, consts, (Q.sem, Q.at(t, "sig")))
            dve.max(top8[:, :], sc[:, u, :]).then_inc(Q.step("top"), 1)
            wait_apart(dve, consts, (Q.sem, Q.at(t, "top")))
            dve.max_index(idx8[:, :], top8[:, :], sc[:, u, :]).then_inc(Q.step("index"), 1)
            mine("index")
            dve.tensor_copy(idxf[:, :], idx8[:, :]).then_inc(Q.step("indexf"), 1)
            mine("indexf")
            dve.tensor_tensor(hot[:, :, :], over(idxf[:, 0:TOP1].unsqueeze(2), TOP1, E1),
                              over(iota_row[:, 0:E1].unsqueeze(1), TOP1, E1), ALU.is_equal).then_inc(Q.step("hot"), 1)
            mine("hot")
            if not early(t):
                dve.wait_ge(h_pos.sem, h_pos.at(t - 2, "pos"))
            with nc.allow_low_precision(reason="zeros and ones"):
                dve.tensor_reduce(mask1[:, u, :], hot[:, :, :].rearrange("p k e -> p e k"), X, ALU.add
                                  ).then_inc(Q.step("mask"), 1)
            mine("mask")
            dve.tensor_tensor(ssel[:, :], sc[:, u, :], mask1[:, u, :], ALU.mult).then_inc(Q.step("sel"), 1)
            mine("sel")
            dve.tensor_reduce(wsum[:, 0:1], ssel[:, :], X, ALU.add).then_inc(Q.step("sum"), 1)
            mine("sum")
            dve.reciprocal(wsum[:, 1:2], wsum[:, 0:1]).then_inc(Q.step("rsum"), 1)
            dve.wait_ge(h_act.sem, h_act.at(t, "silu"))
            if not early(t):
                dve.wait_ge(h_htp.sem, h_htp.at(t - 2, f"t{NCH}"))
            dve.tensor_tensor(hs[:, u, :], sgs[:, u, :], gs_e[:, E1:E1 + HS], ALU.mult).then_inc(Q.step("hs"), 1)

        def h_weights(t, u, r):
            dve.wait_ge(h_pos.sem, h_pos.at(t, "pos"))
            dve.wait_ge(h_rt.sem, h_rt.at(t, "rsum"))
            dve.tensor_scalar(valid[:, :], pos_e, float(CAP1), None, ALU.is_lt).then_inc(h_wt.step("valid"), 1)
            dve.wait_ge(h_wt.sem, h_wt.at(t, "valid"))
            if not early(t):
                dve.wait_ge(h_hv.sem, h_hv.at(t - 2, f"w{NCH - 1}"))
            dve.scalar_tensor_tensor(out=wt[:, u, :], in0=ssel[:, :], scalar=wsum[:, 1:2], in1=valid[:, :],
                                     op0=ALU.mult, op1=ALU.mult).then_inc(h_wt.step("wt"), 1)

        def h_vec(c):
            def body(t, u, r):
                dve.wait_ge(h_silu.sem, h_silu.at(t, f"s{c}"))
                dve.tensor_tensor(hv[:, c % 2, :, :], sg[:, c % 2, :, :], up_e[c % 2][:, :, HID1:2 * HID1], ALU.mult
                                  ).then_inc(h_hv.step(f"v{c}"), 1)
                dve.wait_ge(h_hv.sem, h_hv.at(t, f"v{c}"))
                dve.wait_ge(h_wt.sem, h_wt.at(t, "wt"))
                if c >= 2:
                    dve.wait_ge(h_htp.sem, h_htp.at(t, f"t{c - 2}"))
                elif not (isinstance(t, int) and t < 1):
                    dve.wait_ge(h_htp.sem, h_htp.at(t - 1, f"t{NCH - 2 + c}"))
                dve.tensor_tensor(hw[:, c % 2, :, :], hv[:, c % 2, :, :],
                                  over(wt[:, u, c * CH:(c + 1) * CH].unsqueeze(2), CH, HID1), ALU.mult
                                  ).then_inc(h_hv.step(f"w{c}"), 1)
            return body

        def h_low(c):
            def body(t, u, r):
                dve.wait_ge(h_hhi.sem, h_hhi.at(t, f"t{c}"))
                b, out_t, in_t = h_buffer(t, u, c)
                wait_h_free(dve, t, c)
                dve.tensor_tensor(out_t[1], in_t, out_t[0].bitcast(F32), ALU.subtract).then_inc(h_hlo.step(f"t{c}"), 1)
            return body

        def h_result(t, u, r):
            dve.wait_ge(h_dn.sem, h_dn.at(t, f"d{NCH}"))
            if not early(t):
                dve.wait_ge(h_st[u], 16 * r)
            dve.tensor_tensor(outb[:, u, :], y_e[u], row(x_res, t), ALU.add).then_inc(h_out.step("out"), 1)

        after(dve, g_o)
        pipeline(dve, B, *h_stages(dict(norm=h_norm, low3=h_low3, route=h_route, weights=h_weights, vec=h_vec,
                                        low=h_low, result=h_result)))

    @block.tensor
    def _(pe):
        def both(pair, *idx):
            return pair[0][idx], pair[1][idx]

        A = slice(None)

        def a_turn(t, u, r):
            pe.wait_ge(got_c[u], 16 * (r + 1))
            pe.wait_ge(a_ln.sem, a_ln.at(t, "xn"))
            if not early(t):
                pe.wait_ge(a_thi.sem, a_thi.at(t - 2, "hi"))
                pe.wait_ge(a_tlo.sem, a_tlo.at(t - 2, "lo"))
            for k in range(KD):
                pe.transpose(tp_a[u][:, k, :], xn[:, u, k * P:(k + 1) * P], ident[:, :])
            for k in range(KD):
                mm = pe.transpose(tp_a[u][:, KD + k, :], cin[:, u, k * P:(k + 1) * P], ident[:, :])
            mm.then_inc(a_tp.step("tp"), 1)

        def a_project(t, u, r):
            pe.wait_ge(a_tlo.sem, a_tlo.at(t, "lo"))
            if not early(t):
                pe.wait_ge(a_qhi.sem, a_qhi.at(t - 2, "hi"))
                pe.wait_ge(a_qlo.sem, a_qlo.at(t - 2, "lo"))
            for h in range(H0):
                mm = mm3(pe, qk_a[u][:, 2 * h:2 * h + 2, :], both(wh, A, h, A), both(tT, A, u, slice(h, 4, 2), A),
                         True, True)
            mm.then_inc(a_proj.step("qk"), 1)
            if not early(t):
                pe.wait_ge(a_gate.sem, a_gate.at(t - 2, "relu"))
            for k in range(KD):
                mm = mm3(pe, g_a[u], both(tT, A, u, k, A), both(wgs, A, k, A), k == 0, k == KD - 1)
            mm.then_inc(a_proj.step("gate"), 1)

        def a_score(t, u, r):
            pe.wait_ge(a_qlo.sem, a_qlo.at(t, "lo"))
            for h in range(H0):
                mm = mm3(pe, S_a[h], both(qk, A, u, 2 * h + 1, A), both(qk, A, u, 2 * h, A),
                         isinstance(t, int) and t == 0, isinstance(t, int) and t == B - 1)
            mm.then_inc(a_sc.step("s"), 1)

        after(pe, consts, dve_w)
        pipeline(pe, B, (0, a_turn), (1, a_project), (2, a_score))

        def b_mix(t, u, r):
            pe.wait_ge(b_clo.sem, b_clo.at(t, "lo"))
            if not early(t):
                pe.wait_ge(b_uhi.sem, b_uhi.at(t - 2, "hi"))
                pe.wait_ge(b_ulo.sem, b_ulo.at(t - 2, "lo"))
            for h in range(H0):
                mm = mm3(pe, u_a[u][:, h, :], both(tT, A, u, h, A), both(At, A, h, A), True, True)
            mm.then_inc(b_u.step("u"), 1)

        def b_out(t, u, r):
            pe.wait_ge(b_ulo.sem, b_ulo.at(t, "lo"))
            if not early(t):
                pe.wait_ge(b_keep.sem, b_keep.at(t - 2, "copy"))
                pe.wait_ge(b_stat.sem, b_stat.at(t - 2, "stats"))
            for h in range(H0):
                mm = mm3(pe, row_a[u][:, h * P:(h + 1) * P], both(qk, A, u, h, A), both(wh, A, h, A), True, True)
            mm.then_inc(b_o.step("o"), 1)

        after(pe, b_mask, a_gate, a_qlo)
        pipeline(pe, B, (0, b_mix), (1, b_out))

        def turn(t, u, r, ready, name, done, hi, lo):
            pe.wait_ge(ready.sem, ready.at(t, name))
            if not early(t):
                pe.wait_ge(hi.sem, hi.at(t - 2, "hi"))
                pe.wait_ge(lo.sem, lo.at(t - 2, "lo"))
            for k in range(KD):
                mm = pe.transpose(two_a[u][:, k, :], xn[:, u, k * P:(k + 1) * P], ident[:, :])
            mm.then_inc(done.step("tp"), 1)

        def c_turn(t, u, r):
            turn(t, u, r, c_wy, "scaled", c_tp, c_hi, c_lo)

        def c_project(t, u, r):
            pe.wait_ge(c_lo.sem, c_lo.at(t, "lo"))
            if not early(t):
                pe.wait_ge(c_res.sem, c_res.at(t - 2, "add"))
            for k in range(KD):
                mm = mm3(pe, row_a[u], both(tT, A, u, k, A), both(wos, A, k, A), k == 0, k == KD - 1)
            mm.then_inc(c_o.step("o"), 1)

        after(pe, pool_w, b_keep, b_stat, b_ulo)
        pipeline(pe, B, (0, c_turn), (1, c_project))

        def d_turn(t, u, r):
            turn(t, u, r, d_xn, "xn", d_tp, d_hi, d_lo)

        def d_logits(t, u, r):
            pe.wait_ge(d_lo.sem, d_lo.at(t, "lo"))
            if not early(t):
                pe.wait_ge(d_lgc.sem, d_lgc.at(t - 2, "copy"))
            for k in range(KD):
                mm = mm3(pe, lg_a[u], both(tT, A, u, k, A), both(gate0, A, k, A), k == 0, k == KD - 1)
            mm.then_inc(d_lg.step("logits"), 1)

        after(pe, c_res, c_lo)
        pipeline(pe, B, (0, d_turn), (1, d_logits))

        pe.wait_ge(r_dve.sem, r_dve.at(0, "mask"))
        after(pe, d_lo)
        pe.matmul(pos_r[:, 0:B, :], before[:, :], mask0[:, :, :], start=True, stop=False, skip_group_check=True)
        for s in range(1, B + 1):
            mm = pe.matmul(pos_r[:, s:B + 1, :], ones[:, :], mask0[:, 0:B + 1 - s, :], start=False, stop=s == B,
                           skip_group_check=True)
        mm.then_inc(r_pe.step("pos"), 1)
        pe.wait_ge(r_dve.sem, r_dve.at(0, "r_w"))
        for n in range(NPAIR):
            mm = pe.matmul(tab_r, rt["hotp"][:, n, :], rt["R"][:, n, :, :], start=n == 0, stop=n == NPAIR - 1)
        mm.then_inc(r_pe.step("tab"), 1)

        def e_turn(t, u, r):
            pe.wait_ge(e_xg[u], 16 * (r + 1))
            if not early(t):
                pe.wait_ge(e_xT.sem, e_xT.at(t - 2, "copy"))
            for k in range(KD):
                mm = pe.transpose(xT_c[u][:, k, :], xg[:, u, k * P:(k + 1) * P], ident[:, :])
            mm.then_inc(e_tp.step("tp"), 1)

        def expert(t):
            return pe.value_load(expert_of[0:1, bass.ds(t, 1)], min_val=0, max_val=E0 - 1)

        def e_gate(t, u, r):
            e = expert(t)
            pe.wait_ge(e_xT.sem, e_xT.at(t, "copy"))
            if not early(t):
                pe.wait_ge(e_silu.sem, e_silu.at(t - 2, "silu"))
            for k in range(KD):
                mm = pe.matmul(up_c[u][0], xTc[:, u, k, :],
                               W0[:, bass.ds(e, 1), k * I0:(k + 1) * I0].rearrange("p a n -> p (a n)"),
                               start=k == 0, stop=k == KD - 1)
            mm.then_inc(e_up.step("a"), 1)

        def e_value(t, u, r):
            e = expert(t)
            if not early(t):
                pe.wait_ge(e_h.sem, e_h.at(t - 2, "h"))
            for k in range(KD):
                mm = pe.matmul(up_c[u][1], xTc[:, u, k, :],
                               W0[:, bass.ds(e, 1), (KD + k) * I0:(KD + k + 1) * I0].rearrange("p a n -> p (a n)"),
                               start=k == 0, stop=k == KD - 1)
            mm.then_inc(e_up.step("b"), 1)

        def e_hturn(t, u, r):
            pe.wait_ge(e_h.sem, e_h.at(t, "h"))
            if not (isinstance(t, int) and t < 1):
                pe.wait_ge(e_hT.sem, e_hT.at(t - 1, "copy"))
            for k in range(KI):
                mm = pe.transpose(hT_c[:, k, :], hh[:, u, k * P:(k + 1) * P], ident[:, :])
            mm.then_inc(e_htp.step("tp"), 1)

        def e_down(t, u, r):
            e = expert(t)
            pe.wait_ge(e_hT.sem, e_hT.at(t, "copy"))
            if not (isinstance(t, int) and t < 1):
                pe.wait_ge(e_ys.sem, e_ys.at(t - 1, "y"))
            for k in range(KI):
                o = 2 * KD * I0 + k * D
                mm = pe.matmul(y_c, hTc[:, u, k, :],
                               W0[:, bass.ds(e, 1), o:o + D].rearrange("p a n -> p (a n)"),
                               start=k == 0, stop=k == KI - 1)
            mm.then_inc(e_dn.step("y"), 1)

        pe.wait_ge(got_w0, 16 * 3 * E0)
        after(pe, r_dve)
        pipeline(pe, TILES0, (0, e_turn), (1, e_gate), (2, e_hturn), (1, e_value), (2, e_down))

        def g_turn(t, u, r):
            pe.wait_ge(got_c2[u], 16 * (r + 1))
            if not early(t):
                pe.wait_ge(g_thi.sem, g_thi.at(t - 2, "hi"))
                pe.wait_ge(g_tlo.sem, g_tlo.at(t - 2, "lo"))
            for k in range(KD):
                mm = pe.transpose(cT_d[u][:, k, :], cin2[:, u, k * P:(k + 1) * P], ident[:, :])
            mm.then_inc(g_tp.step("tp"), 1)

        def g_score(t, u, r):
            pe.wait_ge(g_lo.sem, g_lo.at(t, "x"))
            if not early(t):
                pe.wait_ge(g_ex.sem, g_ex.at(t - 2, "e1"))
            for k in range(KD):
                mm = mm3(pe, sc_d[u][:, k, :], both(cs, A, u, slice(k * P, (k + 1) * P)), both(xs, A, u, A), True, True)
            mm.then_inc(g_sc.step("s"), 1)

        def g_value(t, u, r):
            pe.wait_ge(g_alo.sem, g_alo.at(t, "a1"))
            pe.wait_ge(g_tlo.sem, g_tlo.at(t, "lo"))
            if not early(t):
                pe.wait_ge(g_res.sem, g_res.at(t - 2, "add"))
            for k in range(KD):
                mm = mm3(pe, o_d[u], both(cT, A, u, k, A), both(at, A, u, k, A), k == 0, k == KD - 1)
            mm.then_inc(g_o.step("o"), 1)

        after(pe, e_ys)
        pipeline(pe, B, (0, g_turn), (1, g_score), (2, g_value))

        def h_turn3(t, u, r):
            pe.wait_ge(h_xn.sem, h_xn.at(t, "xn"))
            if not (isinstance(t, int) and t < 1):
                pe.wait_ge(h_thi.sem, h_thi.at(t - 1, "hi"))
                pe.wait_ge(h_tlo.sem, h_tlo.at(t - 1, "lo"))
            for k in range(KD):
                mm = pe.transpose(x3T_e[:, k, :], xn3[:, u, k * P:(k + 1) * P], ident[:, :])
            mm.then_inc(h_tp.step("tp"), 1)

        def h_gates(t, u, r):
            pe.wait_ge(h_tlo.sem, h_tlo.at(t, "lo"))
            if not (isinstance(t, int) and t < 1):
                pe.wait_ge(h_rt.sem, h_rt.at(t - 1, "hs"))
                pe.wait_ge(h_wt.sem, h_wt.at(t - 1, "valid"))
            for k in range(KD):
                mm = mm3(pe, gs_e, both(x3T, A, u, k, A), both(gate1, A, k, A), k == 0, k == KD - 1)
            mm.then_inc(h_gs.step("gs"), 1)

        def h_place(t, u, r):
            pe.wait_ge(h_rt.sem, h_rt.at(t, "hs"))
            pe.matmul(pos_e, before[:, :], mask1[:, u, :], start=True, stop=False)
            pe.matmul(pos_e, ones[:, :], macc[:, u, :], start=False, stop=True).then_inc(h_pos.step("pos"), 1)

        def h_upc(c):
            def body(t, u, r):
                if c == 0:
                    pe.wait_ge(h_tlo.sem, h_tlo.at(t, "lo"))
                if c >= 2:
                    pe.wait_ge(h_hv.sem, h_hv.at(t, f"v{c - 2}"))
                elif not (isinstance(t, int) and t < 1):
                    pe.wait_ge(h_hv.sem, h_hv.at(t - 1, f"v{NCH - 2 + c}"))
                for k in range(KD):
                    mm = mm3(pe, up_e[c % 2], both(x3T, A, u, k, A), both(wup_s, A, k, slice(c * CH, (c + 1) * CH), A),
                             k == 0, k == KD - 1)
                mm.then_inc(h_up.step(f"u{c}"), 1)
            return body

        def h_tr(c):
            def body(t, u, r):
                b, _, in_t = h_buffer(t, u, c)
                if c == NCH:
                    wait_apart(pe, consts, (h_hlo.sem, h_hlo.at(t, f"t{c - 2}")), (h_rt.sem, h_rt.at(t, "hs")))
                elif c >= 2:
                    pe.wait_ge(h_hlo.sem, h_hlo.at(t, f"t{c - 2}"))
                elif not (isinstance(t, int) and t < 1):
                    pe.wait_ge(h_hlo.sem, h_hlo.at(t - 1, f"t{NCH - 1 + c}"))
                if c == NCH:
                    mm = pe.transpose(in_t, hs[:, u, :], ident[:, :])
                else:
                    pe.wait_ge(h_hv.sem, h_hv.at(t, f"w{c}"))
                    for k in range(KCH):
                        mm = pe.transpose(in_t[:, k, :], hw[:, c % 2, k * 4:(k + 1) * 4, :].rearrange("p e h -> p (e h)"),
                                          ident[:, :])
                mm.then_inc(h_htp.step(f"t{c}"), 1)
            return body

        def h_downc(c):
            def body(t, u, r):
                b, (hi, lo), _ = h_buffer(t, u, c)
                pe.wait_ge(h_hlo.sem, h_hlo.at(t, f"t{c}"))
                if c == 0 and not early(t):
                    pe.wait_ge(h_out.sem, h_out.at(t - 2, "out"))
                if c == NCH:
                    mm = mm3(pe, y_e[u], (hi, lo), both(wsd_s, A, A), False, True)
                else:
                    for k in range(KCH):
                        mm = mm3(pe, y_e[u], (hi[:, k, :], lo[:, k, :]), both(wdn_s, A, c * KCH + k, A),
                                 c == 0 and k == 0, False)
                mm.then_inc(h_dn.step(f"d{c}"), 1)
            return body

        after(pe, w1_sp, g_res)
        pipeline(pe, B, *h_stages(dict(tr3=h_turn3, gs=h_gates, pos=h_place, up=h_upc, tr=h_tr, down=h_downc)))

    st.close()


_INS = ["x", "ctx_2048", "L0_xattn_Wh", "L0_xattn_wg_w", "L0_xattn_wo_w", "L0_xattn_gn_gamma", "L0_xattn_gn_beta",
        "L0_ffn_w_gate", "L0_ffn_w1", "L0_ffn_w3", "L0_ffn_w2", "L1_ffn_w_gate", "L1_ffn_w_shared_up",
        "L1_ffn_w_shared_down", "L1_ffn_w_up", "L1_ffn_w_down"]


def decay_table(heads, seq, width):
    gam = (1.0 - 2.0 ** (-5.0 - np.arange(heads, dtype=np.float32))).astype(np.float32)
    idx = np.arange(seq, dtype=np.float32)
    expo = idx[None, :] - idx[:, None]
    d = np.where(expo[None] <= 0, gam[:, None, None] ** expo[None], 0.0).astype(np.float32)
    d = d / np.sqrt(d.sum(axis=-1))[:, None, :] / np.sqrt(np.float32(width))
    return np.ascontiguousarray(d.transpose(2, 0, 1)).astype(np.float32)


def kernel(**inputs):
    import numpy as _np
    import concourse.bacc as _bacc
    from concourse import mybir as _mybir
    from concourse.bass_utils import run_bass_kernel_spmd as _run

    nc = _bacc.Bacc("TRN2", target_bir_lowering=False, num_devices=1)
    arrays, args = {}, []

    def give(name, a):
        arrays[f"in_{name}"] = a
        args.append(nc.dram_tensor(f"in_{name}", a.shape, _mybir.dt.from_np(a.dtype), kind="ExternalInput").ap())

    for name in _INS:
        give(name, _np.ascontiguousarray(inputs[name]))
    give("decay", decay_table(H0, P, P))
    shape = tuple(inputs["x"].shape)
    args.append(nc.dram_tensor("out_0", shape, _mybir.dt.float32, kind="ExternalOutput").ap())
    build(nc, *args)
    r = _run(nc, [arrays], core_ids=[0])
    return r.results[0]["out_0"]
```

```python
from contextlib import ExitStack

import numpy as np

import concourse.bass as bass
from concourse import mybir

F32 = mybir.dt.float32
F32R = mybir.dt.float32r
BF16 = mybir.dt.bfloat16
I32 = mybir.dt.int32
U32 = mybir.dt.uint32
ACT = mybir.ActivationFunctionType
ALU = mybir.AluOpType
X = mybir.AxisListType.X

P = 128
B = 16
D = 256
KD = D // P
H0 = 2
E0, TOP0, I0 = 8, 2, 512
KI = I0 // P
SOFTCAP = 30.0
E1, TOP1, HID1, CAP1 = 64, 6, 32, 128
HS = 64
LN_EPS, GN_EPS = 1e-5, 1e-3
TILES0 = (B * P * TOP0 - E0) // P + E0
TJ = TILES0 + 1
NOWHERE = float(1 << 20)
NPAIR = B * TOP0
W0E = 2 * KD * I0 + KI * D
CH = 8
NCH = E1 // CH
W1E = 16
W1N = KD * E1 // W1E + E1 * HID1 // P // 4
KCH = CH * HID1 // P
GS = E1 + 2 * HS


LOADS = (0, 2, 6, B)
LOADS = tuple(zip(LOADS[:-1], LOADS[1:]))


class Steps:

    def __init__(self, sem, names, items=1):
        self.sem, self.names, self.items, self.n = sem, names.split(), items, 0
        assert len(set(self.names)) == len(self.names)

    def step(self, name):
        want = self.names[self.n % len(self.names)]
        assert want == name, (name, want)
        self.n += 1
        return self.sem

    def at(self, item, name):
        return item * len(self.names) + (self.names.index(name) + 1)

    @property
    def all(self):
        return self.items * len(self.names)


def after(eng, *phases):
    for steps in phases:
        eng.wait_ge(steps.sem, steps.all)


def wait_apart(eng, consts, *waits):
    values = [v if isinstance(v, int) else eng.to_reg(v) for _, v in waits]
    eng.wait_ge(consts.sem, consts.all)
    for (sem, _), v in zip(waits, values):
        eng.wait_ge(sem, v)


def wait_loaded(eng, sems, t):
    for (start, end), sem in zip(LOADS, sems):
        if (isinstance(t, int) and t == start) or (not isinstance(t, int) and end == B):
            eng.wait_ge(sem, 16)


def early(t):
    return isinstance(t, int) and t < 2


def pipeline(eng, n, *stages):
    most = max(lag for lag, _ in stages)
    head = most + 2 + most % 2

    def one(s, parity, half):
        for lag, body in stages:
            if isinstance(s, int) and not 0 <= s - lag < n:
                continue
            u = (parity - lag) % 2
            body(s - lag, u, half - (lag - parity + u) // 2)

    for s in range(head):
        one(s, s % 2, s // 2)
    with eng.Fori(head // 2, n // 2) as i:
        for v in range(2):
            one(2 * i + v, v, i)
    for s in range(n // 2 * 2, n + most):
        one(s, s % 2, s // 2)


def mm3(pe, out, lhs, rhs, first, last):
    (lh, ll), (rh, rl) = lhs, rhs
    pe.matmul(out, lh, rh, start=first, stop=False)
    pe.matmul(out, lh, rl, start=False, stop=False)
    return pe.matmul(out, ll, rh, start=False, stop=last)


class Map:

    def __init__(self, nc, at, end):
        self.nc, self.at, self.end = nc, at, end

    def __call__(self, name, shape, dt=F32):
        size = int(np.prod(shape[1:])) * (2 if dt == BF16 else 4)
        t = self.nc.alloc_sbuf_tensor_at(name, shape, dt, offset=self.at)
        self.at += (size + 31) // 32 * 32
        assert self.at <= self.end, (name, self.at, self.end)
        return t

    def pair(self, name, shape):
        return self(name + "_hi", shape, F32R), self(name + "_lo", shape, F32R)


def build(nc, x, ctx, Wh, wg, wo, gamma, beta, wgate0, w1, w3, w2, wgate1, wsu, wsd, wup, wdown, decay, out):
    st = ExitStack()
    KB = 1024
    base = (nc.sbuf_base + 63) // 64 * 64
    END = nc.sbuf_usable_end // 64 * 64
    keep = Map(nc, base, base + 27 * KB)
    big = Map(nc, keep.end, keep.end + 98 * KB)
    W = big.end
    big1 = Map(nc, keep.end, W)
    work_a, work_r, work_c, work_d = Map(nc, W, END), Map(nc, W, END), Map(nc, W, END), Map(nc, W, END)

    def psum(name, shape, dt=F32):
        return st.enter_context(nc.psum_tensor(name, shape, dt))

    def sem(name):
        return st.enter_context(nc.semaphore(name))

    xf = x.rearrange("b s d -> (b s) d")
    cf = ctx.rearrange("b s d -> (b s) d")
    of = out.rearrange("b s d -> (b s) d")
    xn_rows = nc.dram_tensor("xn_rows", [B * P, D], F32, kind="Internal").ap()
    y_rows = nc.dram_tensor("y_rows", [B * P * TOP0, D], F32, kind="Internal").ap()

    ident = keep("ident", [P, P])
    before = keep("before", [P, P], BF16)
    ones = keep("ones", [P, P], BF16)
    iota_row = keep("iota_row", [P, P])
    eps = keep("eps", [P, 2])
    x_res = keep("x_res", [P, B, D])
    bn = keep("bn", [P, B, 6])
    mom = keep("mom", [P, 5, B])
    mean = keep("mean", [P, B])
    sdev = keep("sdev", [P, B])
    rstd = keep("rstd", [P, B])
    gate1 = keep.pair("gate1", [P, KD, GS])
    wsd_s = keep.pair("wsd_s", [HS, D])
    lg = keep("lg", [P, B, E0])
    table = keep("table", [P, 3, TJ], I32)
    expert_of = keep("expert_of", [P, TJ], I32)

    W0 = big("W0", [P, E0, W0E])
    wup_s = big1.pair("wup_s", [P, KD, E1, 2 * HID1])
    wdn_s = big1.pair("wdn_s", [P, E1 * HID1 // P, D])

    wh_raw = work_a("wh_raw", [P, H0, P])
    wg_raw = work_a("wg_raw", [P, KD, D])
    wo_raw = work_a("wo_raw", [P, KD, D])
    gate0_raw = work_a("gate0_raw", [P, KD, E0])
    gate1_raw = work_a("gate1_raw", [P, KD, GS])
    wsd_raw = work_a("wsd_raw", [HS, D])
    wh = work_a.pair("wh", [P, H0, P])
    wgs = work_a.pair("wgs", [P, KD, D])
    wos = work_a.pair("wos", [P, KD, D])
    gate0 = work_a.pair("gate0", [P, KD, E0])
    dec = work_a("dec", [P, H0, P])
    gam = work_a("gam", [P, D])
    bet = work_a("bet", [P, D])
    G = work_a("G", [P, B, D])
    Gg = work_a("Gg", [P, 2, D])
    Gb = work_a("Gb", [P, 2, D])
    cin = work_a("cin", [P, 2, D])
    cen = work_a("cen", [P, 2, D])
    xn = work_a("xn", [P, 2, D])
    sm = work_a("sm", [P, 2, 10])
    tT = work_a.pair("tT", [P, 2, 4, P])
    qk = work_a.pair("qk", [P, 2, 4, P])
    At = work_a.pair("At", [P, H0, P])
    Araw = work_a("Araw", [P, H0, P])
    rows = work_a("rows", [P, B, D])

    rt = {}
    for name, shape in (("prob", [B, E0]), ("rev", [E0]), ("key", [B, E0]), ("hot1", [B, E0]), ("hot2", [B, E0]),
                        ("rest", [B, E0]), ("wsel", [TOP0, B]), ("m", [B]), ("r", [B]), ("k", [B]), ("slot", [B, E0]),
                        ("pick", [B, E0]), ("slotk", [TOP0, B]), ("cnt", [E0]), ("steps128", [B]), ("over", [E0, B]),
                        ("tiles", [E0]), ("one8", [E0]), ("tend", [E0]), ("tstart", [E0]), ("j128", [TJ + 1]),
                        ("jrow", [TJ]), ("passed", [TJ, E0]), ("ef", [TJ]), ("ge", [NPAIR, TJ + 1]),
                        ("hotj", [NPAIR, TJ]), ("tile_of", [NPAIR]), ("row_of", [NPAIR]), ("hotp", [NPAIR, P]),
                        ("val", [3, NPAIR]), ("R", [NPAIR, 3, TJ]), ("T", [3, TJ]), ("none", [TJ])):
        rt[name] = work_r("rt_" + name, [P, *shape])
    mask0 = work_r("mask0", [P, B, E0], BF16)

    xg = work_c("xg", [P, 2, D])
    xTc = work_c("xTc", [P, 2, KD, P])
    sa = work_c("sa", [P, 2, I0])
    hh = work_c("hh", [P, 2, I0])
    hTc = work_c("hTc", [P, 2, KI, P])
    ys = work_c("ys", [P, 2, D])
    stage_g = work_c("stage_g", [P, 2, 1], I32)
    stage_s = work_c("stage_s", [P, 2, 1], I32)
    raw1 = Map(nc, END - 50 * KB, END)
    wup_raw = raw1("wup_raw", [P, KD, E1, 2 * HID1])
    wdn_raw = raw1("wdn_raw", [P, E1 * HID1 // P, D])

    work_d.end = END - 50 * KB

    cin2 = work_d("cin2", [P, 2, D])
    cin3 = work_d("cin3", [P, 2, D])
    xn2 = work_d("xn2", [P, 2, D])
    cs = work_d.pair("cs", [P, 2, D])
    xs = work_d.pair("xs", [P, 2, D])
    cT = work_d.pair("cT", [P, 2, KD, P])
    yin = Map(nc, work_d.at, work_d.end)("yin", [P, 2, 2, TOP0 * D])
    ex = work_d("ex", [P, 2, KD, D])
    at = work_d.pair("at", [P, 2, KD, D])
    smx = work_d("smx", [P, 2, 4, KD])

    work_e, late_e = Map(nc, W, END - 50 * KB), Map(nc, END - 50 * KB, END)
    x3_all = late_e("x3_all", [P, B, 2 * KD * P], F32R)
    shr = late_e("shr", [P, B, 2 * HS])
    esc = work_e("esc", [P, B, E1])
    xn3 = work_e("xn3", [P, 2, D])
    x3T = work_e("x3T", [P, 2, 2, KD, P], F32R)
    sg = work_e("sg", [P, 2, CH, HID1])
    hv = work_e("hv", [P, 2, CH, HID1])
    hw = work_e("hw", [P, 2, CH, HID1])
    hT = work_e.pair("hT", [P, 2, KCH, P])
    sgs = work_e("sgs", [P, 2, HS])
    hs = work_e("hs", [P, 2, HS])
    escp = work_e("escp", [P, E1])
    sc = work_e("sc", [P, 2, E1])
    top8 = work_e("top8", [P, 8])
    idx8 = work_e("idx8", [P, 8], U32)
    idxf = work_e("idxf", [P, 8])
    hot = work_e("hot", [P, TOP1, E1])
    mask1 = work_e("mask1", [P, 2, E1], BF16)
    macc = work_e("macc", [P, 2, E1], BF16)
    ssel = work_e("ssel", [P, E1])
    wsum = work_e("wsum", [P, 2])
    valid = work_e("valid", [P, E1])
    wt = work_e("wt", [P, 2, E1])
    outb = work_e("outb", [P, 2, D])

    bank = [psum(f"bank{i}", [P, 512]) for i in range(8)]

    def view(i, *shape):
        names = "abc"[:len(shape)]
        n = int(np.prod(shape))
        return bank[i][:, 0:n].rearrange(f"p ({' '.join(names)}) -> p {' '.join(names)}",
                                         **dict(zip(names, shape)))

    tp_a = [view(i, 4, P) for i in (0, 1)]
    qk_a = [view(i, 4, P) for i in (2, 3)]
    S_a = [bank[i][:, 0:P] for i in (4, 5)]
    g_a = [bank[i][:, 0:D] for i in (6, 7)]
    two_a = [view(i, 2, P) for i in (0, 1)]
    u_a = [view(i, 2, P) for i in (2, 3)]
    row_a = [bank[i][:, 0:D] for i in (6, 7)]
    lg_a = [bank[i][:, 0:E0] for i in (6, 7)]
    pos_r = view(0, B + 1, E0)
    tab_r = view(1, 3, TJ)
    xT_c = [view(i, KD, P) for i in (0, 1)]
    up_c = [[bank[2][:, :], bank[3][:, :]], [bank[4][:, :], bank[5][:, :]]]
    hT_c = view(6, KI, P)
    y_c = bank[7][:, 0:D]
    cT_d = [view(i, KD, P) for i in (0, 1)]
    sc_d = [view(i, KD, D) for i in (2, 3)]
    o_d = [bank[i][:, 0:D] for i in (4, 5)]
    up_e = [view(i, CH, 2 * HID1) for i in (0, 1)]
    hT_e = [view(i, KCH, P) for i in (2, 3)]
    y_e = [bank[i][:, 0:D] for i in (4, 5)]
    x3T_e = [view(i, KD, P) for i in (0, 1)]
    gs_e = [bank[i][:, 0:GS] for i in (2, 3)]
    pos_e = bank[7][:, 0:E1]

    small = {n: sem("got_" + n) for n in ("wh", "wg", "wo", "gate0", "gate1", "wsd", "decay", "gamma", "beta")}
    got_x = [sem(f"got_x{g}") for g in range(len(LOADS))]
    got_c = [sem(f"got_c{g}") for g in range(len(LOADS))]
    got_w0 = sem("got_w0")
    got_w1 = sem("got_w1")
    consts = Steps(sem("consts"), "zero_ident ident zero_before before ones iota eps_ln eps_gn")
    pool_w = Steps(sem("pool_weights"), "wo_hi wo_lo gate0_hi gate0_lo gate1_hi gate1_lo wsd_hi wsd_lo")
    dve_w = Steps(sem("dve_weights"), "wh_hi wh_lo wg_hi wg_lo")
    a_ln = Steps(sem("a_norm"), "stats aggr rstd xn", B)
    a_sd = Steps(sem("a_sdev"), "sd", B)
    a_cin = Steps(sem("a_context_taken"), "copy", B)
    a_tp = Steps(sem("a_turned"), "tp", B)
    a_thi = Steps(sem("a_turned_hi"), "hi", B)
    a_tlo = Steps(sem("a_turned_lo"), "lo", B)
    a_proj = Steps(sem("a_projected"), "qk gate", B)
    a_qhi = Steps(sem("a_qk_hi"), "hi", B)
    a_qlo = Steps(sem("a_qk_lo"), "lo", B)
    a_sc = Steps(sem("a_scored"), "s", B)
    a_gate = Steps(sem("a_gate"), "relu", B)

    b_mask = Steps(sem("b_masked"), "masked0 masked1 abs floor hi lo")
    b_chi = Steps(sem("b_ctx_hi"), "hi", B)
    b_clo = Steps(sem("b_ctx_lo"), "lo", B)
    b_u = Steps(sem("b_mixed"), "u", B)
    b_uhi = Steps(sem("b_mixed_hi"), "hi", B)
    b_ulo = Steps(sem("b_mixed_lo"), "lo", B)
    b_o = Steps(sem("b_heads"), "o", B)
    b_keep = Steps(sem("b_heads_kept"), "copy", B)
    b_stat = Steps(sem("b_heads_stats"), "stats", B)
    MOMENTS = "sum diff m2 mean sq var"
    mo = [Steps(sem(f"moments{i}"), MOMENTS) for i in range(4)]
    mo_sd = [Steps(sem(f"moments_sdev{i}"), "sd") for i in range(4)]
    mo_rs = [Steps(sem(f"moments_rstd{i}"), "rstd") for i in range(4)]
    c_gb = Steps(sem("c_gate_affine"), "gamma beta", B)
    c_wy = Steps(sem("c_gated"), "centred scaled", B)
    c_tp = Steps(sem("c_turned"), "tp", B)
    c_hi = Steps(sem("c_turned_hi"), "hi", B)
    c_lo = Steps(sem("c_turned_lo"), "lo", B)
    c_o = Steps(sem("c_out"), "o", B)
    c_res = Steps(sem("c_residual"), "add stats", B)
    d_xn = Steps(sem("d_norm"), "xn", B)
    d_row = Steps(sem("d_rows_kept"), "copy", B)
    d_st = [sem("d_stored0"), sem("d_stored1")]
    d_tp = Steps(sem("d_turned"), "tp", B)
    d_hi = Steps(sem("d_turned_hi"), "hi", B)
    d_lo = Steps(sem("d_turned_lo"), "lo", B)
    d_lg = Steps(sem("d_logits"), "logits", B)
    d_lgc = Steps(sem("d_logits_kept"), "copy", B)
    r_act = Steps(sem("r_scalar"), "tanh exp")
    r_iota = Steps(sem("r_iotas"), "rev steps128 j128 jrow code token")
    r_dve = Steps(sem("r_vector"), "cap max sub sum rsum prob "
                  "best1 is1 key1 first1 hot1 w1 rest best2 is2 key2 first2 hot2 w2 mask "
                  "count over tiles one8 tend tstart slot pick1 slot1 pick2 slot2 passed e emin eint "
                  "ge hotj tile_of row_of hotp r_code r_tok r_w none dest t_tok t_w t_dst")
    r_pe = Steps(sem("r_tensor"), "pos tab")
    e_tok = Steps(sem("e_tokens"), "copy", TILES0)
    e_dst = Steps(sem("e_destinations"), "copy", TILES0)
    e_xg = [sem("e_rows0"), sem("e_rows1")]
    e_yst = [sem("e_stored0"), sem("e_stored1")]
    e_tp = Steps(sem("e_turned"), "tp", TILES0)
    e_xT = Steps(sem("e_turned_kept"), "copy", TILES0)
    e_up = Steps(sem("e_up"), "a b", TILES0)
    e_silu = Steps(sem("e_silu"), "silu", TILES0)
    e_h = Steps(sem("e_hidden"), "h", TILES0)
    e_htp = Steps(sem("e_hidden_turned"), "tp", TILES0)
    e_hT = Steps(sem("e_hidden_kept"), "copy", TILES0)
    e_dn = Steps(sem("e_down"), "y", TILES0)
    e_ys = Steps(sem("e_weighted"), "y", TILES0)
    f_yin = [sem("f_rows0"), sem("f_rows1")]
    f_add = Steps(sem("f_added"), "y0 y1 stats0 stats1", B // 2)
    w1_sp = Steps(sem("w1_split"), " ".join(f"hi{i} lo{i}" for i in range(6)))
    got_c2 = [sem("got_ctx2_0"), sem("got_ctx2_1")]
    got_c3 = [sem("got_ctx3_0"), sem("got_ctx3_1")]
    g_xn = Steps(sem("g_norm"), "xn", B)
    g_hi = Steps(sem("g_split_hi"), "ctx x", B)
    g_lo = Steps(sem("g_split_lo"), "ctx x", B)
    g_tp = Steps(sem("g_turned"), "tp", B)
    g_thi = Steps(sem("g_turned_hi"), "hi", B)
    g_tlo = Steps(sem("g_turned_lo"), "lo", B)
    g_sc = Steps(sem("g_scored"), "s", B)
    g_mx = Steps(sem("g_max"), "max neg", B)
    g_ex = Steps(sem("g_exp"), "e0 e1", B)
    g_rs = Steps(sem("g_rsum"), "r", B)
    g_ahi = Steps(sem("g_attn_hi"), "a0 a1", B)
    g_alo = Steps(sem("g_attn_lo"), "a0 a1", B)
    g_o = Steps(sem("g_out"), "o", B)
    g_res = Steps(sem("g_residual"), "add stats", B)
    p_xn = Steps(sem("p_norm"), "xn", B)
    p_tp = Steps(sem("p_turned"), "tp", B)
    p_hi = Steps(sem("p_turned_hi"), "hi", B)
    p_lo = Steps(sem("p_turned_lo"), "lo", B)
    p_keep = Steps(sem("p_turned_kept"), "copy", B)
    p_gs = Steps(sem("p_gate_shared"), "gs", B)
    p_act = Steps(sem("p_gate_scalar"), "exp copy", B)
    h_x = Steps(sem("h_tile_taken"), "copy", B)
    h_sh = Steps(sem("h_shared_silu"), "silu", B)
    h_hw = Steps(sem("h_hidden_weighted"), " ".join(f"w{c}" for c in range(NCH)), B)
    h_rt = Steps(sem("h_route"), "macc0 plus sig top index indexf hot mask sel sum rsum hs", B)
    h_pos = Steps(sem("h_position"), "pos", B)
    h_wt = Steps(sem("h_weights"), "valid wt", B)
    h_up = Steps(sem("h_up"), " ".join(f"u{c}" for c in range(NCH)), B)
    h_silu = Steps(sem("h_silu"), " ".join(f"s{c}" for c in range(NCH)), B)
    h_hv = Steps(sem("h_hidden"), " ".join(f"v{c}" for c in range(NCH)), B)
    h_htp = Steps(sem("h_hidden_turned"), " ".join(f"t{c}" for c in range(NCH + 1)), B)
    h_hhi = Steps(sem("h_hidden_hi"), " ".join(f"t{c}" for c in range(NCH + 1)), B)
    h_hlo = Steps(sem("h_hidden_lo"), " ".join(f"t{c}" for c in range(NCH + 1)), B)
    h_dn = Steps(sem("h_down"), " ".join(f"d{c}" for c in range(NCH + 1)), B)
    h_out = Steps(sem("h_result"), "out", B)
    h_st = [sem("h_stored0"), sem("h_stored1")]

    def h_slot(u, c):
        return (c + u) % 2

    def h_buffer(t, u, c):
        b = h_slot(u, c)
        if c == NCH:
            return b, (hT[0][0:HS, b, 0, :], hT[1][0:HS, b, 0, :]), hT_e[b][0:HS, 0, :]
        return b, (hT[0][:, b, :, :], hT[1][:, b, :, :]), hT_e[b]

    def wait_h_free(eng, t, c):
        if c >= 2:
            eng.wait_ge(h_dn.sem, h_dn.at(t, f"d{c - 2}"))
        elif not (isinstance(t, int) and t < 1):
            eng.wait_ge(h_dn.sem, h_dn.at(t - 1, f"d{NCH - 1 + c}"))

    def h_stages(f):
        order = []

        def put(lag, name, *args):
            if name in f:
                order.append((lag, f[name](*args) if args else f[name]))

        for c in range(NCH + 1):
            if c < NCH:
                put(1, "up", c)
                put(1, "silu", c)
                put(1, "vec", c)
                put(1, "weigh", c)
            q = (c - 1) % (NCH + 1)
            lag = 1 if c >= 1 else 2
            put(lag, "tr", q)
            put(lag, "high", q)
            put(lag, "low", q)
            d = (c - 2) % (NCH + 1)
            lag = 1 if c >= 2 else 2
            put(lag, "down", d)
            if d == NCH:
                put(2, "result")
            if c == 2:
                put(0, "take")
            if c == 4:
                put(0, "shared")
            put(0, "route", c)
            if c == 6:
                put(0, "pos")
            if c == 7:
                put(0, "weights")
        return order

    def tile_of(buf, t):
        return buf[:, bass.ds(t, 1), :].rearrange("p a d -> p (a d)")

    block = st.enter_context(nc.Block())

    @block.sync
    def _(sp):
        def store_rows(t, u, r):
            wait_apart(sp, consts, (d_row.sem, d_row.at(t, "copy")))
            sp.dma_start(xn_rows[bass.ds(t * P, P), :], rows[:, bass.ds(t, 1), :].rearrange("p a d -> p (a d)")
                         ).then_inc(d_st[u], 16)

        def load_y(t, u, r):
            if not early(t):
                wait_apart(sp, consts, (f_add.sem, f_add.at(t - 2, "y1")))
            sp.dma_start(yin[:, u, :, :].rearrange("p a (k d) -> p a (k d)", k=TOP0),
                         y_rows[bass.ds(t * 2 * P * TOP0, 2 * P * TOP0), :]
                         .rearrange("(a p k) d -> p a (k d)", k=TOP0, p=P)).then_inc(f_yin[u], 16)

        def load_c2(t, u, r):
            if not early(t):
                wait_apart(sp, consts, (g_hi.sem, g_hi.at(t - 2, "ctx")),
                           (g_lo.sem, g_lo.at(t - 2, "ctx")))
            sp.dma_start(cin2[:, u, :], ctx[bass.ds(t, 1), :, :].rearrange("a p d -> p (a d)")
                         ).then_inc(got_c2[u], 16)

        def load_c3(t, u, r):
            if not early(t):
                wait_apart(sp, consts, (g_tp.sem, g_tp.at(t - 2, "tp")))
            sp.dma_start(cin3[:, u, :], ctx[bass.ds(t, 1), :, :].rearrange("a p d -> p (a d)")
                         ).then_inc(got_c3[u], 16)

        def store(t, u, r):
            wait_apart(sp, consts, (h_out.sem, h_out.at(t, "out")))
            sp.dma_start(out[bass.ds(t, 1), :, :].rearrange("a p d -> p (a d)"), outb[:, u, :]
                         ).then_inc(h_st[u], 16)

        for (a, b), gx, gc in zip(LOADS, got_x, got_c):
            sp.dma_start(x_res[:, a:b, :], x[a:b].rearrange("b p d -> p b d")).then_inc(gx, 16)
            sp.dma_start(rows[:, a:b, :], ctx[a:b].rearrange("b p d -> p b d")).then_inc(gc, 16)
        for g in range(len(LOADS)):
            sp.wait_ge(got_x[g], 16)
            sp.wait_ge(got_c[g], 16)
        with sp.Fori(0, E0) as e:
            for a, w in ((0, w1), (1, w3)):
                sp.dma_start(W0[:, bass.ds(e, 1), a * KD * I0:(a + 1) * KD * I0]
                             .rearrange("p a (k n) -> p (a k) n", k=KD),
                             w[bass.ds(e, 1), :, :].rearrange("a (k p) n -> p (a k) n", p=P)).then_inc(got_w0, 16)
            sp.dma_start(W0[:, bass.ds(e, 1), 2 * KD * I0:W0E].rearrange("p a (k n) -> p (a k) n", k=KI),
                         w2[bass.ds(e, 1), :, :].rearrange("a (k p) n -> p (a k) n", p=P)).then_inc(got_w0, 16)
        pipeline(sp, B, (0, store_rows))
        after(sp, r_dve, r_pe, r_iota)
        pieces = [(wup_raw[:, k, e:e + W1E, :], wup[e:e + W1E, k * P:(k + 1) * P, :].rearrange("e p n -> p e n"))
                  for k in range(KD) for e in range(0, E1, W1E)]
        wd = wdown.rearrange("(c e) h d -> (e h) c d", e=P // HID1)
        pieces += [(wdn_raw[:, c:c + 4, :], wd[:, c:c + 4, :]) for c in range(0, E1 * HID1 // P, 4)]
        assert len(pieces) == W1N
        for n, (to, fr) in enumerate(pieces):
            sp.wait_ge(e_xg[1], 16 * (n + 1))
            sp.dma_start(to, fr).then_inc(got_w1, 16)
        sp.wait_ge(e_yst[0], 16 * ((TILES0 + 1) // 2))
        sp.wait_ge(e_yst[1], 16 * (TILES0 // 2))
        pipeline(sp, B // 2, (0, load_y))
        pipeline(sp, B, (0, load_c2), (2, load_c3))
        pipeline(sp, B, (0, store))
        for u in range(2):
            sp.wait_ge(h_st[u], 16 * (B // 2))
            sp.wait_ge(d_st[u], 16 * (B // 2))

    @block.gpsimd
    def _(pool):
        pool.memset(ident[:, :], 0.0).then_inc(consts.step("zero_ident"), 1)
        pool.wait_ge(consts.sem, consts.at(0, "zero_ident"))
        pool.affine_select(out=ident[:, :], in_=ident[:, :], compare_op=ALU.not_equal, fill=1.0, base=0,
                           pattern=[[-1, P]], channel_multiplier=1).then_inc(consts.step("ident"), 1)
        pool.memset(before[:, :], 0.0).then_inc(consts.step("zero_before"), 1)
        pool.wait_ge(consts.sem, consts.at(0, "zero_before"))
        pool.affine_select(out=before[:, :], in_=before[:, :], compare_op=ALU.is_ge, fill=1.0, base=0,
                           pattern=[[-1, P]], channel_multiplier=1).then_inc(consts.step("before"), 1)
        pool.memset(ones[:, :], 1.0).then_inc(consts.step("ones"), 1)
        pool.iota(iota_row[:, :], [[1, P]], base=0, channel_multiplier=0,
                  allow_small_or_imprecise_dtypes=True).then_inc(consts.step("iota"), 1)
        pool.memset(eps[:, 0:1], LN_EPS).then_inc(consts.step("eps_ln"), 1)
        pool.memset(eps[:, 1:2], GN_EPS).then_inc(consts.step("eps_gn"), 1)

        def weights(*names):
            raws = dict(wo=(wo_raw, wos), gate0=(gate0_raw, gate0), gate1=(gate1_raw, gate1), wsd=(wsd_raw, wsd_s))
            for name in names:
                rawt, (hi, lo) = raws[name]
                pool.wait_ge(small[name], 32 if name == "gate1" else 16)
                pool.tensor_copy(hi[:], rawt[:]).then_inc(pool_w.step(name + "_hi"), 1)
                pool.wait_ge(pool_w.sem, pool_w.at(0, name + "_hi"))
                pool.tensor_tensor(lo[:], rawt[:], hi[:].bitcast(F32), ALU.subtract
                                   ).then_inc(pool_w.step(name + "_lo"), 1)

        def take_context(t, u, r):
            wait_loaded(pool, got_c, t)
            if not early(t):
                wait_apart(pool, consts, (a_tp.sem, a_tp.at(t - 2, "tp")))
            pool.tensor_copy(cin[:, u, :], tile_of(rows, t)).then_inc(a_cin.step("copy"), 1)

        def affine(t, u, r):
            if not early(t):
                wait_apart(pool, consts, (c_wy.sem, c_wy.at(t - 2, "scaled")))
            g = G[:, bass.ds(t, 1), :].rearrange("p a d -> p (a d)")
            pool.tensor_tensor(Gg[:, u, :], g, gam[:, :], ALU.mult).then_inc(c_gb.step("gamma"), 1)
            pool.tensor_tensor(Gb[:, u, :], g, bet[:, :], ALU.mult).then_inc(c_gb.step("beta"), 1)

        pipeline(pool, B, (0, take_context))
        weights("wo", "gate0", "gate1", "wsd")
        pool.wait_ge(small["gamma"], 16)
        pool.wait_ge(small["beta"], 16)
        after(pool, a_gate)
        pipeline(pool, B, (0, affine))

        def keep_rows(t, u, r):
            wait_apart(pool, consts, (d_xn.sem, d_xn.at(t, "xn")))
            pool.tensor_copy(tile_of(rows, t), xn[:, u, :]).then_inc(d_row.step("copy"), 1)

        after(pool, c_wy)
        pipeline(pool, B, (0, keep_rows))

        after(pool, d_xn, d_hi, d_lo, d_lg, c_wy, c_o)
        pool.iota(rt["rev"][:, :], [[-1, E0]], base=E0, channel_multiplier=0,
                  allow_small_or_imprecise_dtypes=True).then_inc(r_iota.step("rev"), 1)
        pool.iota(rt["steps128"][:, :], [[P, B]], base=0, channel_multiplier=0,
                  allow_small_or_imprecise_dtypes=True).then_inc(r_iota.step("steps128"), 1)
        pool.iota(rt["j128"][:, :], [[P, TJ + 1]], base=0, channel_multiplier=0,
                  allow_small_or_imprecise_dtypes=True).then_inc(r_iota.step("j128"), 1)
        pool.iota(rt["jrow"][:, :], [[1, TJ]], base=0, channel_multiplier=0,
                  allow_small_or_imprecise_dtypes=True).then_inc(r_iota.step("jrow"), 1)
        pool.iota(rt["val"][:, 0, :], [[1, TOP0], [P * TOP0, B]], base=1, channel_multiplier=TOP0,
                  allow_small_or_imprecise_dtypes=True).then_inc(r_iota.step("code"), 1)
        pool.iota(rt["val"][:, 1, :], [[0, TOP0], [P, B]], base=0, channel_multiplier=1,
                  allow_small_or_imprecise_dtypes=True).then_inc(r_iota.step("token"), 1)

        def gather(t, u, r):
            if not early(t):
                pool.wait_ge(e_xg[u], 16 * r)
            pool.tensor_copy(stage_g[:, u, :], table[:, 0, bass.ds(t, 1)]).then_inc(e_tok.step("copy"), 1)
            waits = [(e_tok.sem, e_tok.at(t, "copy"))]
            if not early(t):
                waits.append((e_tp.sem, e_tp.at(t - 2, "tp")))
            wait_apart(pool, consts, *waits)
            pool.indirect_dma_start(xg[:, u, :], None, xn_rows,
                                    bass.IndirectOffsetOnAxis(stage_g[:, u, :].bitcast(U32), 0)).then_inc(e_xg[u], 16)

        def scatter(t, u, r):
            if not early(t):
                pool.wait_ge(e_yst[u], 16 * r)
            pool.tensor_copy(stage_s[:, u, :], table[:, 1, bass.ds(t, 1)]).then_inc(e_dst.step("copy"), 1)
            wait_apart(pool, consts, (e_dst.sem, e_dst.at(t, "copy")), (e_ys.sem, e_ys.at(t, "y")))
            pool.indirect_dma_start(y_rows, bass.IndirectOffsetOnAxis(stage_s[:, u, :].bitcast(U32), 0),
                                    ys[:, u, :], None, bounds_check=B * P * TOP0 - 1, oob_is_err=False
                                    ).then_inc(e_yst[u], 16)

        after(pool, r_dve)
        for u in range(2):
            pool.wait_ge(d_st[u], 16 * (B // 2))
        pipeline(pool, TILES0, (0, gather), (3, scatter))

        pool.wait_ge(got_w1, 16 * W1N)
        after(pool, e_dn)
        parts = [(wup_raw[:, k, e:e + 32, :], wup_s[0][:, k, e:e + 32, :], wup_s[1][:, k, e:e + 32, :])
                 for k in range(KD) for e in (0, 32)]
        parts += [(wdn_raw[:, k:k + 8, :], wdn_s[0][:, k:k + 8, :], wdn_s[1][:, k:k + 8, :]) for k in (0, 8)]
        for n, (rawt, hi, lo) in enumerate(parts):
            pool.tensor_copy(hi, rawt).then_inc(w1_sp.step(f"hi{n}"), 1)
            pool.wait_ge(w1_sp.sem, w1_sp.at(0, f"hi{n}"))
            pool.tensor_tensor(lo, rawt, hi.bitcast(F32), ALU.subtract).then_inc(w1_sp.step(f"lo{n}"), 1)

        def p_kept(t, u, r):
            wait_apart(pool, consts, (p_lo.sem, p_lo.at(t, "lo")))
            pool.tensor_copy(tile_of(x3_all, t), x3T[:, u].rearrange("p j k d -> p (j k d)")
                             ).then_inc(p_keep.step("copy"), 1)

        after(pool, g_o, g_res, w1_sp)
        pipeline(pool, B, (1, p_kept))
        after(pool, p_keep, p_gs)

        def h_take(t, u, r):
            if not early(t):
                wait_apart(pool, consts, (h_up.sem, h_up.at(t - 2, f"u{NCH - 1}")))
            pool.tensor_copy(x3T[:, u].rearrange("p j k d -> p (j k d)"), tile_of(x3_all, t)
                             ).then_inc(h_x.step("copy"), 1)

        def h_weigh(c):
            def body(t, u, r):
                waits = [(h_hv.sem, h_hv.at(t, f"v{c}")), (h_wt.sem, h_wt.at(t, "wt"))]
                if c >= 2:
                    waits.append((h_htp.sem, h_htp.at(t, f"t{c - 2}")))
                elif not (isinstance(t, int) and t < 1):
                    waits.append((h_htp.sem, h_htp.at(t - 1, f"t{NCH - 2 + c}")))
                wait_apart(pool, consts, *waits)
                pool.tensor_tensor(hw[:, c % 2, :, :], hv[:, c % 2, :, :],
                                   wt[:, u, c * CH:(c + 1) * CH].unsqueeze(2).to_broadcast([P, CH, HID1]), ALU.mult
                                   ).then_inc(h_hw.step(f"w{c}"), 1)
            return body

        pipeline(pool, B, *h_stages(dict(take=h_take, weigh=h_weigh)))

    @block.scalar
    def _(act):
        act.dma_start(wh_raw[:, :, :], Wh.rearrange("h d e -> d h e")).then_inc(small["wh"], 16)
        act.dma_start(wg_raw[:, :, :], wg.rearrange("(k p) n -> p k n", p=P)).then_inc(small["wg"], 16)
        act.dma_start(gam[:, :], gamma.rearrange("(a d) -> a d", a=1).broadcast_to([P, D])).then_inc(small["gamma"], 16)
        act.dma_start(bet[:, :], beta.rearrange("(a d) -> a d", a=1).broadcast_to([P, D])).then_inc(small["beta"], 16)
        act.dma_start(dec[:, :, :], decay).then_inc(small["decay"], 16)
        act.dma_start(wo_raw[:, :, :], wo.rearrange("(k p) n -> p k n", p=P)).then_inc(small["wo"], 16)
        act.dma_start(gate0_raw[:, :, :], wgate0.rearrange("(k p) n -> p k n", p=P)).then_inc(small["gate0"], 16)
        act.dma_start(gate1_raw[:, :, 0:E1], wgate1.rearrange("(k p) n -> p k n", p=P)).then_inc(small["gate1"], 16)
        act.dma_start(gate1_raw[:, :, E1:GS], wsu.rearrange("(k p) n -> p k n", p=P)).then_inc(small["gate1"], 16)
        act.dma_start(wsd_raw[:, :], wsd).then_inc(small["wsd"], 16)

        def a_sdev(t, u, r):
            act.wait_ge(a_ln.sem, a_ln.at(t, "aggr"))
            act.activation(sm[:, u, 8:9], sm[:, u, 7:8], ACT.Sqrt, bias=eps[:, 0:1]).then_inc(a_sd.step("sd"), 1)

        def a_hi(t, u, r):
            act.wait_ge(a_tp.sem, a_tp.at(t, "tp"))
            if not early(t):
                act.wait_ge(a_proj.sem, a_proj.at(t - 2, "gate"))
                act.wait_ge(a_tlo.sem, a_tlo.at(t - 2, "lo"))
            act.activation(tT[0][:, u, :, :], tp_a[u], ACT.Copy).then_inc(a_thi.step("hi"), 1)

        def a_qk(t, u, r):
            act.wait_ge(a_proj.sem, a_proj.at(t, "qk"))
            if not early(t):
                act.wait_ge(a_sc.sem, a_sc.at(t - 2, "s"))
                act.wait_ge(a_qlo.sem, a_qlo.at(t - 2, "lo"))
            act.activation(qk[0][:, u, :, :], qk_a[u], ACT.Copy).then_inc(a_qhi.step("hi"), 1)

        def a_relu(t, u, r):
            act.wait_ge(a_proj.sem, a_proj.at(t, "gate"))
            act.activation(G[:, bass.ds(t, 1), :].rearrange("p a d -> p (a d)"), g_a[u], ACT.Relu
                           ).then_inc(a_gate.step("relu"), 1)

        after(act, consts)
        pipeline(act, B, (3, a_qk), (0, a_sdev), (1, a_hi), (3, a_relu))
        after(act, a_sc, a_qlo)

        def b_ctx(t, u, r):
            if not early(t):
                act.wait_ge(b_u.sem, b_u.at(t - 2, "u"))
                act.wait_ge(b_clo.sem, b_clo.at(t - 2, "lo"))
            act.activation(tT[0][:, u, 0:2, :].rearrange("p k d -> p (k d)"),
                           rows[:, bass.ds(t, 1), :].rearrange("p a d -> p (a d)"), ACT.Copy
                           ).then_inc(b_chi.step("hi"), 1)

        def b_mixed(t, u, r):
            act.wait_ge(b_u.sem, b_u.at(t, "u"))
            if not early(t):
                act.wait_ge(b_o.sem, b_o.at(t - 2, "o"))
                act.wait_ge(b_ulo.sem, b_ulo.at(t - 2, "lo"))
            act.activation(qk[0][:, u, 0:2, :], u_a[u], ACT.Copy).then_inc(b_uhi.step("hi"), 1)

        def b_kept(t, u, r):
            act.wait_ge(b_o.sem, b_o.at(t, "o"))
            act.wait_ge(b_clo.sem, b_clo.at(t, "lo"))
            act.activation(rows[:, bass.ds(t, 1), :].rearrange("p a d -> p (a d)"), row_a[u], ACT.Copy
                           ).then_inc(b_keep.step("copy"), 1)

        pipeline(act, B, (3, b_mixed), (0, b_ctx), (5, b_kept))

        def sdev_all(i, e):
            act.wait_ge(mo[i].sem, mo[i].at(0, "var"))
            act.activation(sdev[:, :], mom[:, 4, :], ACT.Sqrt, bias=eps[:, e:e + 1], scale=1.0 / D).then_inc(mo_sd[i].step("sd"), 1)

        sdev_all(0, 1)
        after(act, b_o, b_ulo)

        def c_split(t, u, r):
            act.wait_ge(c_tp.sem, c_tp.at(t, "tp"))
            if not early(t):
                act.wait_ge(c_o.sem, c_o.at(t - 2, "o"))
                act.wait_ge(c_lo.sem, c_lo.at(t - 2, "lo"))
            act.activation(tT[0][:, u, 0:2, :], two_a[u], ACT.Copy).then_inc(c_hi.step("hi"), 1)

        pipeline(act, B, (2, c_split))
        sdev_all(1, 0)
        after(act, c_o, c_lo)

        def d_split(t, u, r):
            act.wait_ge(d_tp.sem, d_tp.at(t, "tp"))
            if not early(t):
                act.wait_ge(d_lg.sem, d_lg.at(t - 2, "logits"))
                act.wait_ge(d_lo.sem, d_lo.at(t - 2, "lo"))
            act.activation(tT[0][:, u, 0:2, :], two_a[u], ACT.Copy).then_inc(d_hi.step("hi"), 1)

        def d_keep(t, u, r):
            act.wait_ge(d_lg.sem, d_lg.at(t, "logits"))
            act.activation(lg[:, bass.ds(t, 1), :].rearrange("p a e -> p (a e)"), lg_a[u], ACT.Copy
                           ).then_inc(d_lgc.step("copy"), 1)

        pipeline(act, B, (3, d_keep), (1, d_split))

        after(act, d_lgc)
        act.activation(lg[:, :, :], lg[:, :, :], ACT.Tanh, scale=1.0 / SOFTCAP).then_inc(r_act.step("tanh"), 1)
        act.wait_ge(r_dve.sem, r_dve.at(0, "sub"))
        act.activation(rt["prob"][:, :, :], lg[:, :, :], ACT.Exp).then_inc(r_act.step("exp"), 1)

        def e_rows(t, u, r):
            act.wait_ge(e_tp.sem, e_tp.at(t, "tp"))
            if not early(t):
                act.wait_ge(e_up.sem, e_up.at(t - 2, "b"))
            act.activation(xTc[:, u, :, :], xT_c[u], ACT.Copy).then_inc(e_xT.step("copy"), 1)

        def e_act(t, u, r):
            act.wait_ge(e_up.sem, e_up.at(t, "a"))
            if not early(t):
                act.wait_ge(e_h.sem, e_h.at(t - 2, "h"))
            act.activation(sa[:, u, :], up_c[u][0], ACT.Silu).then_inc(e_silu.step("silu"), 1)

        def e_hid(t, u, r):
            act.wait_ge(e_htp.sem, e_htp.at(t, "tp"))
            if not early(t):
                act.wait_ge(e_dn.sem, e_dn.at(t - 2, "y"))
            act.activation(hTc[:, u, :, :], hT_c, ACT.Copy).then_inc(e_hT.step("copy"), 1)

        after(act, r_dve, r_pe)
        pipeline(act, TILES0, (0, e_rows), (1, e_act), (2, e_hid))

        sdev_all(2, 0)

        def g_high(t, u, r):
            act.wait_ge(got_c2[u], 16 * (r + 1))
            if not early(t):
                act.wait_ge(g_sc.sem, g_sc.at(t - 2, "s"))
                act.wait_ge(g_lo.sem, g_lo.at(t - 2, "x"))
            act.activation(cs[0][:, u, :], cin2[:, u, :], ACT.Copy).then_inc(g_hi.step("ctx"), 1)
            act.wait_ge(g_xn.sem, g_xn.at(t, "xn"))
            act.activation(xs[0][:, u, :], xn2[:, u, :], ACT.Copy).then_inc(g_hi.step("x"), 1)

        def g_turn(t, u, r):
            act.wait_ge(g_tp.sem, g_tp.at(t, "tp"))
            if not early(t):
                act.wait_ge(g_o.sem, g_o.at(t - 2, "o"))
                act.wait_ge(g_tlo.sem, g_tlo.at(t - 2, "lo"))
            act.activation(cT[0][:, u, :, :], cT_d[u], ACT.Copy).then_inc(g_thi.step("hi"), 1)

        def g_expo(t, u, r):
            act.wait_ge(g_mx.sem, g_mx.at(t, "neg"))
            if not early(t):
                act.wait_ge(g_ahi.sem, g_ahi.at(t - 2, "a1"))
                act.wait_ge(g_alo.sem, g_alo.at(t - 2, "a1"))
            for k in range(KD):
                act.activation(ex[:, u, k, :], sc_d[u][:, k, :], ACT.Exp, bias=smx[:, u, 1, k:k + 1],
                               scale=D ** -0.5, accum_out=smx[:, u, 2, k:k + 1]).then_inc(g_ex.step(f"e{k}"), 1)

        def g_attn(t, u, r):
            act.wait_ge(g_rs.sem, g_rs.at(t, "r"))
            if not early(t):
                act.wait_ge(g_o.sem, g_o.at(t - 2, "o"))
            for k in range(KD):
                act.activation(at[0][:, u, k, :], ex[:, u, k, :], ACT.Copy, scale=smx[:, u, 3, k:k + 1]
                               ).then_inc(g_ahi.step(f"a{k}"), 1)

        after(act, e_ys, f_add)
        pipeline(act, B, (1, g_high), (4, g_turn), (4, g_attn), (3, g_expo))
        sdev_all(3, 0)
        after(act, g_o, g_res)

        def p_high(t, u, r):
            act.wait_ge(p_tp.sem, p_tp.at(t, "tp"))
            if not early(t):
                act.wait_ge(p_gs.sem, p_gs.at(t - 2, "gs"))
                act.wait_ge(p_keep.sem, p_keep.at(t - 2, "copy"))
                act.wait_ge(p_lo.sem, p_lo.at(t - 2, "lo"))
            act.activation(x3T[:, u, 0, :, :], x3T_e[u], ACT.Copy).then_inc(p_hi.step("hi"), 1)

        def p_gate(t, u, r):
            act.wait_ge(p_gs.sem, p_gs.at(t, "gs"))
            act.activation(tile_of(esc, t), gs_e[u][:, 0:E1], ACT.Exp, scale=-1.0).then_inc(p_act.step("exp"), 1)
            act.activation(tile_of(shr, t), gs_e[u][:, E1:GS], ACT.Copy).then_inc(p_act.step("copy"), 1)

        after(act, w1_sp)
        pipeline(act, B, (3, p_gate), (1, p_high))

        def h_shared(t, u, r):
            if not early(t):
                act.wait_ge(h_rt.sem, h_rt.at(t - 2, "hs"))
            act.activation(sgs[:, u, :], tile_of(shr, t)[:, HS:2 * HS], ACT.Silu).then_inc(h_sh.step("silu"), 1)

        def h_act_c(c):
            def body(t, u, r):
                act.wait_ge(h_up.sem, h_up.at(t, f"u{c}"))
                if c >= 2:
                    act.wait_ge(h_hv.sem, h_hv.at(t, f"v{c - 2}"))
                elif not (isinstance(t, int) and t < 1):
                    act.wait_ge(h_hv.sem, h_hv.at(t - 1, f"v{NCH - 2 + c}"))
                act.activation(sg[:, c % 2, :, :], up_e[c % 2][:, :, 0:HID1], ACT.Silu
                               ).then_inc(h_silu.step(f"s{c}"), 1)
            return body

        def h_high(c):
            def body(t, u, r):
                act.wait_ge(h_htp.sem, h_htp.at(t, f"t{c}"))
                b, out_t, in_t = h_buffer(t, u, c)
                wait_h_free(act, t, c)
                act.activation(out_t[0], in_t, ACT.Copy).then_inc(h_hhi.step(f"t{c}"), 1)
            return body

        after(act, p_act)
        pipeline(act, B, *h_stages(dict(shared=h_shared, silu=h_act_c, high=h_high)))

    @block.vector
    def _(dve):
        for name, rawt, (hi, lo) in (("wh", wh_raw, wh), ("wg", wg_raw, wgs)):
            dve.wait_ge(small[name], 16)
            dve.tensor_copy(hi[:], rawt[:]).then_inc(dve_w.step(name + "_hi"), 1)
            dve.wait_ge(dve_w.sem, dve_w.at(0, name + "_hi"))
            dve.tensor_tensor(lo[:], rawt[:], hi[:].bitcast(F32), ALU.subtract).then_inc(dve_w.step(name + "_lo"), 1)

        def row(buf, t):
            return buf[:, bass.ds(t, 1), :].rearrange("p a d -> p (a d)")

        def a_stats(t, u, r):
            wait_loaded(dve, got_x, t)
            dve.bn_stats(sm[:, u, 0:6], row(x_res, t)).then_inc(a_ln.step("stats"), 1)
            wait_apart(dve, consts, (a_ln.sem, a_ln.at(t, "stats")))
            dve.bn_aggr(sm[:, u, 6:8], sm[:, u, 0:6]).then_inc(a_ln.step("aggr"), 1)

        def a_norm(t, u, r):
            dve.wait_ge(a_sd.sem, a_sd.at(t, "sd"))
            dve.reciprocal(sm[:, u, 9:10], sm[:, u, 8:9]).then_inc(a_ln.step("rstd"), 1)
            dve.wait_ge(a_ln.sem, a_ln.at(t, "rstd"))
            if not early(t):
                dve.wait_ge(a_tp.sem, a_tp.at(t - 2, "tp"))
            dve.tensor_scalar(xn[:, u, :], row(x_res, t), sm[:, u, 6:7], sm[:, u, 9:10], ALU.subtract, ALU.mult
                              ).then_inc(a_ln.step("xn"), 1)

        def a_low(t, u, r):
            dve.wait_ge(a_thi.sem, a_thi.at(t, "hi"))
            if not early(t):
                dve.wait_ge(a_proj.sem, a_proj.at(t - 2, "gate"))
            dve.tensor_tensor(tT[1][:, u, :, :], tp_a[u], tT[0][:, u, :, :].bitcast(F32), ALU.subtract
                              ).then_inc(a_tlo.step("lo"), 1)

        def a_qklow(t, u, r):
            dve.wait_ge(a_qhi.sem, a_qhi.at(t, "hi"))
            if not early(t):
                dve.wait_ge(a_sc.sem, a_sc.at(t - 2, "s"))
            dve.tensor_tensor(qk[1][:, u, :, :], qk_a[u], qk[0][:, u, :, :].bitcast(F32), ALU.subtract
                              ).then_inc(a_qlo.step("lo"), 1)

        pipeline(dve, B, (0, a_stats), (3, a_qklow), (1, a_low), (0, a_norm))

        after(dve, a_sc)
        dve.wait_ge(small["decay"], 16)
        for h in range(H0):
            dve.tensor_tensor(Araw[:, h, :], S_a[h], dec[:, h, :], ALU.mult).then_inc(b_mask.step(f"masked{h}"), 1)
        dve.wait_ge(b_mask.sem, b_mask.at(0, "masked1"))
        dve.scalar_tensor_tensor(out=Araw[:, :, :], in0=Araw[:, :, :], scalar=-1.0, in1=Araw[:, :, :],
                                 op0=ALU.mult, op1=ALU.max).then_inc(b_mask.step("abs"), 1)
        dve.wait_ge(b_mask.sem, b_mask.at(0, "abs"))
        dve.tensor_scalar(Araw[:, :, :], Araw[:, :, :], 1.0, None, ALU.max).then_inc(b_mask.step("floor"), 1)
        dve.wait_ge(b_mask.sem, b_mask.at(0, "floor"))
        dve.tensor_copy(At[0][:, :, :], Araw[:, :, :]).then_inc(b_mask.step("hi"), 1)
        dve.wait_ge(b_mask.sem, b_mask.at(0, "hi"))
        dve.tensor_tensor(At[1][:, :, :], Araw[:, :, :], At[0][:, :, :].bitcast(F32), ALU.subtract
                          ).then_inc(b_mask.step("lo"), 1)

        def b_ctx(t, u, r):
            dve.wait_ge(b_chi.sem, b_chi.at(t, "hi"))
            if not early(t):
                dve.wait_ge(b_u.sem, b_u.at(t - 2, "u"))
            dve.tensor_tensor(tT[1][:, u, 0:2, :].rearrange("p k d -> p (k d)"), row(rows, t),
                              tT[0][:, u, 0:2, :].rearrange("p k d -> p (k d)").bitcast(F32), ALU.subtract
                              ).then_inc(b_clo.step("lo"), 1)

        def b_mixed(t, u, r):
            dve.wait_ge(b_uhi.sem, b_uhi.at(t, "hi"))
            if not early(t):
                dve.wait_ge(b_o.sem, b_o.at(t - 2, "o"))
            dve.tensor_tensor(qk[1][:, u, 0:2, :], u_a[u], qk[0][:, u, 0:2, :].bitcast(F32), ALU.subtract
                              ).then_inc(b_ulo.step("lo"), 1)

        def b_stats(t, u, r):
            dve.wait_ge(b_keep.sem, b_keep.at(t, "copy"))
            dve.bn_stats(row(bn, t), row_a[u]).then_inc(b_stat.step("stats"), 1)

        pipeline(dve, B, (6, b_stats), (3, b_mixed), (1, b_ctx))

        def moments(i, stats, e):
            m = mo[i]
            after(dve, stats)
            dve.tensor_tensor(mom[:, 0, :], bn[:, :, 1], bn[:, :, 4], ALU.add).then_inc(m.step("sum"), 1)
            dve.tensor_tensor(mom[:, 1, :], bn[:, :, 1], bn[:, :, 4], ALU.subtract).then_inc(m.step("diff"), 1)
            dve.tensor_tensor(mom[:, 2, :], bn[:, :, 2], bn[:, :, 5], ALU.add).then_inc(m.step("m2"), 1)
            dve.wait_ge(m.sem, m.at(0, "m2"))
            dve.tensor_scalar(mean[:, :], mom[:, 0, :], 0.5, None, ALU.mult).then_inc(m.step("mean"), 1)
            dve.scalar_tensor_tensor(out=mom[:, 3, :], in0=mom[:, 1, :], scalar=D / 4.0, in1=mom[:, 1, :],
                                     op0=ALU.mult, op1=ALU.mult).then_inc(m.step("sq"), 1)
            dve.wait_ge(m.sem, m.at(0, "sq"))
            dve.tensor_tensor(mom[:, 4, :], mom[:, 3, :], mom[:, 2, :], ALU.add).then_inc(m.step("var"), 1)
            dve.wait_ge(mo_sd[i].sem, mo_sd[i].at(0, "sd"))
            dve.reciprocal(rstd[:, :], sdev[:, :]).then_inc(mo_rs[i].step("rstd"), 1)
            dve.wait_ge(mo_rs[i].sem, mo_rs[i].at(0, "rstd"))

        moments(0, b_stat, 1)
        after(dve, b_keep, b_o)

        def c_gate(t, u, r):
            dve.wait_ge(c_gb.sem, c_gb.at(t, "beta"))
            dve.scalar_tensor_tensor(out=cen[:, u, :], in0=row(rows, t), scalar=mean[:, bass.ds(t, 1)],
                                     in1=Gg[:, u, :], op0=ALU.subtract, op1=ALU.mult).then_inc(c_wy.step("centred"), 1)
            dve.wait_ge(c_wy.sem, c_wy.at(t, "centred"))
            if not early(t):
                dve.wait_ge(c_tp.sem, c_tp.at(t - 2, "tp"))
            dve.scalar_tensor_tensor(out=xn[:, u, :], in0=cen[:, u, :], scalar=rstd[:, bass.ds(t, 1)],
                                     in1=Gb[:, u, :], op0=ALU.mult, op1=ALU.add).then_inc(c_wy.step("scaled"), 1)

        def c_low(t, u, r):
            dve.wait_ge(c_hi.sem, c_hi.at(t, "hi"))
            if not early(t):
                dve.wait_ge(c_o.sem, c_o.at(t - 2, "o"))
            dve.tensor_tensor(tT[1][:, u, 0:2, :], two_a[u], tT[0][:, u, 0:2, :].bitcast(F32), ALU.subtract
                              ).then_inc(c_lo.step("lo"), 1)

        def c_add(t, u, r):
            dve.wait_ge(c_o.sem, c_o.at(t, "o"))
            dve.tensor_tensor(row(x_res, t), row_a[u], row(x_res, t), ALU.add).then_inc(c_res.step("add"), 1)
            dve.wait_ge(c_res.sem, c_res.at(t, "add"))
            dve.bn_stats(row(bn, t), row(x_res, t)).then_inc(c_res.step("stats"), 1)

        pipeline(dve, B, (4, c_add), (1, c_gate), (2, c_low))
        moments(1, c_res, 0)

        after(dve, c_tp, c_o)

        def d_norm(t, u, r):
            if not early(t):
                dve.wait_ge(d_tp.sem, d_tp.at(t - 2, "tp"))
                dve.wait_ge(d_row.sem, d_row.at(t - 2, "copy"))
            dve.tensor_scalar(xn[:, u, :], row(x_res, t), mean[:, bass.ds(t, 1)], rstd[:, bass.ds(t, 1)],
                              ALU.subtract, ALU.mult).then_inc(d_xn.step("xn"), 1)

        def d_low(t, u, r):
            dve.wait_ge(d_hi.sem, d_hi.at(t, "hi"))
            if not early(t):
                dve.wait_ge(d_lg.sem, d_lg.at(t - 2, "logits"))
            dve.tensor_tensor(tT[1][:, u, 0:2, :], two_a[u], tT[0][:, u, 0:2, :].bitcast(F32), ALU.subtract
                              ).then_inc(d_lo.step("lo"), 1)

        pipeline(dve, B, (0, d_norm), (1, d_low))

        R = r_dve

        def own(name):
            dve.wait_ge(R.sem, R.at(0, name))

        def over(ap, *shape):
            return ap.to_broadcast([P, *shape])

        after(dve, r_iota, d_lg)
        for u in range(2):
            dve.wait_ge(d_st[u], 16 * (B // 2))
        dve.wait_ge(r_act.sem, r_act.at(0, "tanh"))
        prob, rest, key, m, k_ = rt["prob"], rt["rest"], rt["key"], rt["m"], rt["k"]
        dve.tensor_scalar(lg[:, :, :], lg[:, :, :], SOFTCAP, None, ALU.mult).then_inc(R.step("cap"), 1)
        own("cap")
        dve.tensor_reduce(m[:, :], lg[:, :, :], X, ALU.max).then_inc(R.step("max"), 1)
        own("max")
        dve.tensor_tensor(lg[:, :, :], lg[:, :, :], over(m[:, :].unsqueeze(2), B, E0), ALU.subtract
                          ).then_inc(R.step("sub"), 1)
        dve.wait_ge(r_act.sem, r_act.at(0, "exp"))
        dve.tensor_reduce(m[:, :], prob[:, :, :], X, ALU.add).then_inc(R.step("sum"), 1)
        own("sum")
        dve.reciprocal(rt["r"][:, :], m[:, :]).then_inc(R.step("rsum"), 1)
        own("rsum")
        dve.tensor_tensor(prob[:, :, :], prob[:, :, :], over(rt["r"][:, :].unsqueeze(2), B, E0), ALU.mult
                          ).then_inc(R.step("prob"), 1)
        own("prob")
        for n, source in ((1, prob), (2, rest)):
            hot_n = rt[f"hot{n}"]
            dve.tensor_reduce(rt["val"][:, 2, (n - 1) * B:n * B], source[:, :, :], X, ALU.max
                              ).then_inc(R.step(f"best{n}"), 1)
            own(f"best{n}")
            best = over(rt["val"][:, 2, (n - 1) * B:n * B].unsqueeze(2), B, E0)
            dve.tensor_tensor(key[:, :, :], source[:, :, :], best, ALU.is_equal).then_inc(R.step(f"is{n}"), 1)
            own(f"is{n}")
            dve.tensor_tensor(key[:, :, :], key[:, :, :], over(rt["rev"][:, :].unsqueeze(1), B, E0), ALU.mult
                              ).then_inc(R.step(f"key{n}"), 1)
            own(f"key{n}")
            dve.tensor_reduce(k_[:, :], key[:, :, :], X, ALU.max).then_inc(R.step(f"first{n}"), 1)
            own(f"first{n}")
            dve.tensor_tensor(hot_n[:, :, :], key[:, :, :], over(k_[:, :].unsqueeze(2), B, E0), ALU.is_equal
                              ).then_inc(R.step(f"hot{n}"), 1)
            own(f"hot{n}")
            dve.tensor_copy(rt["wsel"][:, n - 1, :], rt["val"][:, 2, (n - 1) * B:n * B]).then_inc(R.step(f"w{n}"), 1)
            if n == 1:
                dve.scalar_tensor_tensor(out=rest[:, :, :], in0=hot_n[:, :, :], scalar=-4.0, in1=prob[:, :, :],
                                         op0=ALU.mult, op1=ALU.add).then_inc(R.step("rest"), 1)
                own("rest")
        dve.tensor_tensor(mask0[:, :, :], rt["hot1"][:, :, :], rt["hot2"][:, :, :], ALU.add).then_inc(R.step("mask"), 1)
        dve.wait_ge(r_pe.sem, r_pe.at(0, "pos"))
        dve.tensor_copy(rt["cnt"][:, :], pos_r[:, B, :]).then_inc(R.step("count"), 1)
        own("count")
        two = rt["over"]
        dve.tensor_tensor(two[:, :, :], over(rt["cnt"][:, :].unsqueeze(2), E0, B),
                          over(rt["steps128"][:, :].unsqueeze(1), E0, B), ALU.is_gt).then_inc(R.step("over"), 1)
        own("over")
        dve.tensor_reduce(rt["tiles"][:, :], two[:, :, :], X, ALU.add).then_inc(R.step("tiles"), 1)
        dve.memset(rt["one8"][:, :], 1.0).then_inc(R.step("one8"), 1)
        own("one8")
        dve.tensor_tensor_scan(rt["tend"][:, :], rt["one8"][:, :], rt["tiles"][:, :], 0.0, ALU.mult, ALU.add
                               ).then_inc(R.step("tend"), 1)
        own("tend")
        dve.tensor_tensor(rt["tstart"][:, :], rt["tend"][:, :], rt["tiles"][:, :], ALU.subtract
                          ).then_inc(R.step("tstart"), 1)
        own("tstart")
        dve.scalar_tensor_tensor(out=rt["slot"][:, :, :], in0=over(rt["tstart"][:, :].unsqueeze(1), B, E0),
                                 scalar=float(P), in1=pos_r[:, 0:B, :], op0=ALU.mult, op1=ALU.add
                                 ).then_inc(R.step("slot"), 1)
        own("slot")
        for n in (1, 2):
            dve.tensor_tensor(rt["pick"][:, :, :], rt["slot"][:, :, :], rt[f"hot{n}"][:, :, :], ALU.mult
                              ).then_inc(R.step(f"pick{n}"), 1)
            own(f"pick{n}")
            dve.tensor_reduce(rt["slotk"][:, n - 1, :], rt["pick"][:, :, :], X, ALU.add).then_inc(R.step(f"slot{n}"), 1)
            own(f"slot{n}")
        dve.tensor_tensor(rt["passed"][:, :, :], over(rt["tend"][:, :].unsqueeze(1), TJ, E0),
                          over(rt["jrow"][:, :].unsqueeze(2), TJ, E0), ALU.is_le).then_inc(R.step("passed"), 1)
        own("passed")
        dve.tensor_reduce(rt["ef"][:, :], rt["passed"][:, :, :], X, ALU.add).then_inc(R.step("e"), 1)
        own("e")
        dve.tensor_scalar(rt["ef"][:, :], rt["ef"][:, :], float(E0 - 1), None, ALU.min).then_inc(R.step("emin"), 1)
        own("emin")
        dve.tensor_copy(expert_of[:, :], rt["ef"][:, :]).then_inc(R.step("eint"), 1)
        slotk = rt["slotk"][:, :, :].rearrange("p k b -> p (k b)")
        dve.tensor_tensor(rt["ge"][:, :, :], over(slotk.unsqueeze(2), NPAIR, TJ + 1),
                          over(rt["j128"][:, :].unsqueeze(1), NPAIR, TJ + 1), ALU.is_ge).then_inc(R.step("ge"), 1)
        own("ge")
        dve.tensor_tensor(rt["hotj"][:, :, :], rt["ge"][:, :, 0:TJ], rt["ge"][:, :, 1:TJ + 1], ALU.subtract
                          ).then_inc(R.step("hotj"), 1)
        dve.tensor_reduce(rt["tile_of"][:, :], rt["ge"][:, :, 1:TJ + 1], X, ALU.add).then_inc(R.step("tile_of"), 1)
        own("tile_of")
        dve.scalar_tensor_tensor(out=rt["row_of"][:, :], in0=rt["tile_of"][:, :], scalar=-float(P), in1=slotk,
                                 op0=ALU.mult, op1=ALU.add).then_inc(R.step("row_of"), 1)
        own("row_of")
        dve.tensor_tensor(rt["hotp"][:, :, :], over(rt["row_of"][:, :].unsqueeze(2), NPAIR, P),
                          over(iota_row[:, :].unsqueeze(1), NPAIR, P), ALU.is_equal).then_inc(R.step("hotp"), 1)
        for n, name in enumerate(("r_code", "r_tok", "r_w")):
            dve.tensor_tensor(rt["R"][:, :, n, :], rt["hotj"][:, :, :], over(rt["val"][:, n, :].unsqueeze(2), NPAIR, TJ),
                              ALU.mult).then_inc(R.step(name), 1)
        dve.wait_ge(r_pe.sem, r_pe.at(0, "tab"))
        dve.tensor_scalar(rt["none"][:, :], tab_r[:, 0, :], 0.0, NOWHERE, ALU.is_equal, ALU.mult
                          ).then_inc(R.step("none"), 1)
        own("none")
        dve.scalar_tensor_tensor(out=rt["T"][:, 0, :], in0=tab_r[:, 0, :], scalar=-1.0, in1=rt["none"][:, :],
                                 op0=ALU.add, op1=ALU.add).then_inc(R.step("dest"), 1)
        dve.tensor_copy(table[:, 0, :], tab_r[:, 1, :]).then_inc(R.step("t_tok"), 1)
        dve.tensor_copy(table[:, 2, :].bitcast(F32), tab_r[:, 2, :]).then_inc(R.step("t_w"), 1)
        own("dest")
        dve.tensor_copy(table[:, 1, :], rt["T"][:, 0, :]).then_inc(R.step("t_dst"), 1)

        def e_hidden(t, u, r):
            dve.wait_ge(e_silu.sem, e_silu.at(t, "silu"))
            dve.wait_ge(e_up.sem, e_up.at(t, "b"))
            if not early(t):
                dve.wait_ge(e_htp.sem, e_htp.at(t - 2, "tp"))
            dve.tensor_tensor(hh[:, u, :], sa[:, u, :], up_c[u][1], ALU.mult).then_inc(e_h.step("h"), 1)

        def e_weigh(t, u, r):
            dve.wait_ge(e_dn.sem, e_dn.at(t, "y"))
            if not early(t):
                dve.wait_ge(e_yst[u], 16 * r)
            dve.tensor_scalar(ys[:, u, :], y_c, table[:, 2, bass.ds(t, 1)].bitcast(F32), None, ALU.mult
                              ).then_inc(e_ys.step("y"), 1)

        after(dve, R)
        pipeline(dve, TILES0, (1, e_hidden), (2, e_weigh))

        def f_sum(t, u, r):
            dve.wait_ge(f_yin[u], 16 * (r + 1))
            both_x = x_res[:, bass.ds(2 * t, 2), :]
            dve.tensor_tensor(both_x, both_x, yin[:, u, :, 0:D], ALU.add).then_inc(f_add.step("y0"), 1)
            dve.wait_ge(f_add.sem, f_add.at(t, "y0"))
            dve.tensor_tensor(both_x, both_x, yin[:, u, :, D:2 * D], ALU.add).then_inc(f_add.step("y1"), 1)
            dve.wait_ge(f_add.sem, f_add.at(t, "y1"))
            for v in range(2):
                dve.bn_stats(row(bn, 2 * t + v), row(x_res, 2 * t + v)).then_inc(f_add.step(f"stats{v}"), 1)

        pipeline(dve, B // 2, (0, f_sum))
        moments(2, f_add, 0)

        def g_norm(t, u, r):
            if not early(t):
                dve.wait_ge(g_hi.sem, g_hi.at(t - 2, "x"))
                dve.wait_ge(g_lo.sem, g_lo.at(t - 2, "x"))
            dve.tensor_scalar(xn2[:, u, :], row(x_res, t), mean[:, bass.ds(t, 1)], rstd[:, bass.ds(t, 1)],
                              ALU.subtract, ALU.mult).then_inc(g_xn.step("xn"), 1)

        def g_low(t, u, r):
            dve.wait_ge(g_hi.sem, g_hi.at(t, "x"))
            if not early(t):
                dve.wait_ge(g_sc.sem, g_sc.at(t - 2, "s"))
            dve.tensor_tensor(cs[1][:, u, :], cin2[:, u, :], cs[0][:, u, :].bitcast(F32), ALU.subtract
                              ).then_inc(g_lo.step("ctx"), 1)
            dve.tensor_tensor(xs[1][:, u, :], xn2[:, u, :], xs[0][:, u, :].bitcast(F32), ALU.subtract
                              ).then_inc(g_lo.step("x"), 1)

        def g_turnlow(t, u, r):
            dve.wait_ge(g_thi.sem, g_thi.at(t, "hi"))
            if not early(t):
                dve.wait_ge(g_o.sem, g_o.at(t - 2, "o"))
            dve.tensor_tensor(cT[1][:, u, :, :], cT_d[u], cT[0][:, u, :, :].bitcast(F32), ALU.subtract
                              ).then_inc(g_tlo.step("lo"), 1)

        def g_max(t, u, r):
            dve.wait_ge(g_sc.sem, g_sc.at(t, "s"))
            dve.tensor_reduce(smx[:, u, 0, :], sc_d[u], X, ALU.max).then_inc(g_mx.step("max"), 1)
            dve.wait_ge(g_mx.sem, g_mx.at(t, "max"))
            dve.tensor_scalar(smx[:, u, 1, :], smx[:, u, 0, :], -(D ** -0.5), None, ALU.mult
                              ).then_inc(g_mx.step("neg"), 1)

        def g_rsum(t, u, r):
            dve.wait_ge(g_ex.sem, g_ex.at(t, "e1"))
            dve.reciprocal(smx[:, u, 3, :], smx[:, u, 2, :]).then_inc(g_rs.step("r"), 1)

        def g_soft(t, u, r):
            if not early(t):
                dve.wait_ge(g_o.sem, g_o.at(t - 2, "o"))
            for k in range(KD):
                dve.wait_ge(g_ahi.sem, g_ahi.at(t, f"a{k}"))
                dve.scalar_tensor_tensor(out=at[1][:, u, k, :], in0=ex[:, u, k, :], scalar=smx[:, u, 3, k:k + 1],
                                         in1=at[0][:, u, k, :].bitcast(F32), op0=ALU.mult, op1=ALU.subtract
                                         ).then_inc(g_alo.step(f"a{k}"), 1)

        def g_add(t, u, r):
            dve.wait_ge(g_o.sem, g_o.at(t, "o"))
            dve.tensor_tensor(row(x_res, t), o_d[u], row(x_res, t), ALU.add).then_inc(g_res.step("add"), 1)
            dve.wait_ge(g_res.sem, g_res.at(t, "add"))
            dve.bn_stats(row(bn, t), row(x_res, t)).then_inc(g_res.step("stats"), 1)

        pipeline(dve, B, (4, g_rsum), (6, g_add), (1, g_low), (3, g_max), (0, g_norm), (4, g_turnlow), (4, g_soft))
        moments(3, g_res, 0)

        def p_norm(t, u, r):
            if not early(t):
                dve.wait_ge(p_tp.sem, p_tp.at(t - 2, "tp"))
            dve.tensor_scalar(xn3[:, u, :], row(x_res, t), mean[:, bass.ds(t, 1)], rstd[:, bass.ds(t, 1)],
                              ALU.subtract, ALU.mult).then_inc(p_xn.step("xn"), 1)

        def p_low(t, u, r):
            dve.wait_ge(p_hi.sem, p_hi.at(t, "hi"))
            if not early(t):
                dve.wait_ge(p_gs.sem, p_gs.at(t - 2, "gs"))
                dve.wait_ge(p_keep.sem, p_keep.at(t - 2, "copy"))
            dve.tensor_tensor(x3T[:, u, 1, :, :], x3T_e[u], x3T[:, u, 0, :, :].bitcast(F32), ALU.subtract
                              ).then_inc(p_lo.step("lo"), 1)

        def h_route(c):
            Q = h_rt

            def body(t, u, r):
                def mine(name):
                    dve.wait_ge(Q.sem, Q.at(t, name))

                if c == 0:
                    if isinstance(t, int) and t == 0:
                        dve.memset(macc[:, 0, :], 0.0).then_inc(Q.step("macc0"), 1)
                    else:
                        if not early(t):
                            dve.wait_ge(h_pos.sem, h_pos.at(t - 2, "pos"))
                        dve.tensor_tensor(macc[:, u, :], macc[:, 1 - u, :], mask1[:, 1 - u, :], ALU.add
                                          ).then_inc(Q.step("macc0"), 1)
                    dve.tensor_scalar(escp[:, :], row(esc, t), 1.0, None, ALU.add).then_inc(Q.step("plus"), 1)
                if c == 1:
                    mine("plus")
                    dve.reciprocal(sc[:, u, :], escp[:, :]).then_inc(Q.step("sig"), 1)
                if c == 2:
                    wait_apart(dve, consts, (Q.sem, Q.at(t, "sig")))
                    dve.max(top8[:, :], sc[:, u, :]).then_inc(Q.step("top"), 1)
                    wait_apart(dve, consts, (Q.sem, Q.at(t, "top")))
                    dve.max_index(idx8[:, :], top8[:, :], sc[:, u, :]).then_inc(Q.step("index"), 1)
                    mine("index")
                    dve.tensor_copy(idxf[:, :], idx8[:, :]).then_inc(Q.step("indexf"), 1)
                if c == 3:
                    mine("indexf")
                    dve.tensor_tensor(hot[:, :, :], over(idxf[:, 0:TOP1].unsqueeze(2), TOP1, E1),
                                      over(iota_row[:, 0:E1].unsqueeze(1), TOP1, E1), ALU.is_equal
                                      ).then_inc(Q.step("hot"), 1)
                if c == 4:
                    mine("hot")
                    if not early(t):
                        dve.wait_ge(h_pos.sem, h_pos.at(t - 2, "pos"))
                    with nc.allow_low_precision(reason="zeros and ones"):
                        dve.tensor_reduce(mask1[:, u, :], hot[:, :, :].rearrange("p k e -> p e k"), X, ALU.add
                                          ).then_inc(Q.step("mask"), 1)
                if c == 5:
                    mine("mask")
                    dve.tensor_tensor(ssel[:, :], sc[:, u, :], mask1[:, u, :], ALU.mult).then_inc(Q.step("sel"), 1)
                    mine("sel")
                    dve.tensor_reduce(wsum[:, 0:1], ssel[:, :], X, ALU.add).then_inc(Q.step("sum"), 1)
                    mine("sum")
                    dve.reciprocal(wsum[:, 1:2], wsum[:, 0:1]).then_inc(Q.step("rsum"), 1)
                if c == 6:
                    dve.wait_ge(h_sh.sem, h_sh.at(t, "silu"))
                    if not early(t):
                        dve.wait_ge(h_htp.sem, h_htp.at(t - 2, f"t{NCH}"))
                    dve.tensor_tensor(hs[:, u, :], sgs[:, u, :], row(shr, t)[:, 0:HS], ALU.mult).then_inc(Q.step("hs"), 1)

            return body

        def h_weights(t, u, r):
            dve.wait_ge(h_pos.sem, h_pos.at(t, "pos"))
            dve.wait_ge(h_rt.sem, h_rt.at(t, "rsum"))
            dve.tensor_scalar(valid[:, :], pos_e, float(CAP1), None, ALU.is_lt).then_inc(h_wt.step("valid"), 1)
            dve.wait_ge(h_wt.sem, h_wt.at(t, "valid"))
            if not early(t):
                dve.wait_ge(h_hw.sem, h_hw.at(t - 2, f"w{NCH - 1}"))
            dve.scalar_tensor_tensor(out=wt[:, u, :], in0=ssel[:, :], scalar=wsum[:, 1:2], in1=valid[:, :],
                                     op0=ALU.mult, op1=ALU.mult).then_inc(h_wt.step("wt"), 1)

        def h_vec(c):
            def body(t, u, r):
                dve.wait_ge(h_silu.sem, h_silu.at(t, f"s{c}"))
                if c >= 2:
                    dve.wait_ge(h_hw.sem, h_hw.at(t, f"w{c - 2}"))
                elif not (isinstance(t, int) and t < 1):
                    dve.wait_ge(h_hw.sem, h_hw.at(t - 1, f"w{NCH - 2 + c}"))
                dve.tensor_tensor(hv[:, c % 2, :, :], sg[:, c % 2, :, :], up_e[c % 2][:, :, HID1:2 * HID1], ALU.mult
                                  ).then_inc(h_hv.step(f"v{c}"), 1)
            return body

        def h_low(c):
            def body(t, u, r):
                dve.wait_ge(h_hhi.sem, h_hhi.at(t, f"t{c}"))
                b, out_t, in_t = h_buffer(t, u, c)
                wait_h_free(dve, t, c)
                dve.tensor_tensor(out_t[1], in_t, out_t[0].bitcast(F32), ALU.subtract).then_inc(h_hlo.step(f"t{c}"), 1)
            return body

        def h_result(t, u, r):
            dve.wait_ge(h_dn.sem, h_dn.at(t, f"d{NCH}"))
            if not early(t):
                dve.wait_ge(h_st[u], 16 * r)
            dve.tensor_tensor(outb[:, u, :], y_e[u], row(x_res, t), ALU.add).then_inc(h_out.step("out"), 1)

        after(dve, g_o)
        pipeline(dve, B, (0, p_norm), (1, p_low))
        after(dve, p_act)
        pipeline(dve, B, *h_stages(dict(route=h_route, weights=h_weights, vec=h_vec,
                                        low=h_low, result=h_result)))

    @block.tensor
    def _(pe):
        def both(pair, *idx):
            return pair[0][idx], pair[1][idx]

        A = slice(None)

        def a_turn(t, u, r):
            pe.wait_ge(a_cin.sem, a_cin.at(t, "copy"))
            pe.wait_ge(a_ln.sem, a_ln.at(t, "xn"))
            if not early(t):
                pe.wait_ge(a_thi.sem, a_thi.at(t - 2, "hi"))
                pe.wait_ge(a_tlo.sem, a_tlo.at(t - 2, "lo"))
            for k in range(KD):
                pe.transpose(tp_a[u][:, k, :], xn[:, u, k * P:(k + 1) * P], ident[:, :])
            for k in range(KD):
                mm = pe.transpose(tp_a[u][:, KD + k, :], cin[:, u, k * P:(k + 1) * P], ident[:, :])
            mm.then_inc(a_tp.step("tp"), 1)

        def a_project(t, u, r):
            pe.wait_ge(a_tlo.sem, a_tlo.at(t, "lo"))
            if not early(t):
                pe.wait_ge(a_qhi.sem, a_qhi.at(t - 2, "hi"))
                pe.wait_ge(a_qlo.sem, a_qlo.at(t - 2, "lo"))
            for h in range(H0):
                mm = mm3(pe, qk_a[u][:, 2 * h:2 * h + 2, :], both(wh, A, h, A), both(tT, A, u, slice(h, 4, 2), A),
                         True, True)
            mm.then_inc(a_proj.step("qk"), 1)
            if not early(t):
                pe.wait_ge(a_gate.sem, a_gate.at(t - 2, "relu"))
            for k in range(KD):
                mm = mm3(pe, g_a[u], both(tT, A, u, k, A), both(wgs, A, k, A), k == 0, k == KD - 1)
            mm.then_inc(a_proj.step("gate"), 1)

        def a_score(t, u, r):
            pe.wait_ge(a_qlo.sem, a_qlo.at(t, "lo"))
            for h in range(H0):
                mm = mm3(pe, S_a[h], both(qk, A, u, 2 * h + 1, A), both(qk, A, u, 2 * h, A),
                         isinstance(t, int) and t == 0, isinstance(t, int) and t == B - 1)
            mm.then_inc(a_sc.step("s"), 1)

        after(pe, consts, dve_w)
        pipeline(pe, B, (1, a_turn), (4, a_score), (2, a_project))

        def b_mix(t, u, r):
            pe.wait_ge(b_clo.sem, b_clo.at(t, "lo"))
            if not early(t):
                pe.wait_ge(b_uhi.sem, b_uhi.at(t - 2, "hi"))
                pe.wait_ge(b_ulo.sem, b_ulo.at(t - 2, "lo"))
            for h in range(H0):
                mm = mm3(pe, u_a[u][:, h, :], both(tT, A, u, h, A), both(At, A, h, A), True, True)
            mm.then_inc(b_u.step("u"), 1)

        def b_out(t, u, r):
            pe.wait_ge(b_ulo.sem, b_ulo.at(t, "lo"))
            if not early(t):
                pe.wait_ge(b_keep.sem, b_keep.at(t - 2, "copy"))
                pe.wait_ge(b_stat.sem, b_stat.at(t - 2, "stats"))
            for h in range(H0):
                mm = mm3(pe, row_a[u][:, h * P:(h + 1) * P], both(qk, A, u, h, A), both(wh, A, h, A), True, True)
            mm.then_inc(b_o.step("o"), 1)

        after(pe, b_mask, a_gate, a_qlo)
        pipeline(pe, B, (2, b_mix), (4, b_out))

        def turn(t, u, r, ready, name, done, hi, lo):
            pe.wait_ge(ready.sem, ready.at(t, name))
            if not early(t):
                pe.wait_ge(hi.sem, hi.at(t - 2, "hi"))
                pe.wait_ge(lo.sem, lo.at(t - 2, "lo"))
            for k in range(KD):
                mm = pe.transpose(two_a[u][:, k, :], xn[:, u, k * P:(k + 1) * P], ident[:, :])
            mm.then_inc(done.step("tp"), 1)

        def c_turn(t, u, r):
            turn(t, u, r, c_wy, "scaled", c_tp, c_hi, c_lo)

        def c_project(t, u, r):
            pe.wait_ge(c_lo.sem, c_lo.at(t, "lo"))
            if not early(t):
                pe.wait_ge(c_res.sem, c_res.at(t - 2, "add"))
            for k in range(KD):
                mm = mm3(pe, row_a[u], both(tT, A, u, k, A), both(wos, A, k, A), k == 0, k == KD - 1)
            mm.then_inc(c_o.step("o"), 1)

        after(pe, pool_w, b_keep, b_stat, b_ulo)
        pipeline(pe, B, (2, c_turn), (3, c_project))

        def d_turn(t, u, r):
            turn(t, u, r, d_xn, "xn", d_tp, d_hi, d_lo)

        def d_logits(t, u, r):
            pe.wait_ge(d_lo.sem, d_lo.at(t, "lo"))
            if not early(t):
                pe.wait_ge(d_lgc.sem, d_lgc.at(t - 2, "copy"))
            for k in range(KD):
                mm = mm3(pe, lg_a[u], both(tT, A, u, k, A), both(gate0, A, k, A), k == 0, k == KD - 1)
            mm.then_inc(d_lg.step("logits"), 1)

        after(pe, c_res, c_lo)
        pipeline(pe, B, (1, d_turn), (2, d_logits))

        pe.wait_ge(r_dve.sem, r_dve.at(0, "mask"))
        after(pe, d_lo)
        pe.matmul(pos_r[:, 0:B, :], before[:, :], mask0[:, :, :], start=True, stop=False, skip_group_check=True)
        for s in range(1, B + 1):
            mm = pe.matmul(pos_r[:, s:B + 1, :], ones[:, :], mask0[:, 0:B + 1 - s, :], start=False, stop=s == B,
                           skip_group_check=True)
        mm.then_inc(r_pe.step("pos"), 1)
        pe.wait_ge(r_dve.sem, r_dve.at(0, "r_w"))
        for n in range(NPAIR):
            mm = pe.matmul(tab_r, rt["hotp"][:, n, :], rt["R"][:, n, :, :], start=n == 0, stop=n == NPAIR - 1)
        mm.then_inc(r_pe.step("tab"), 1)

        def e_turn(t, u, r):
            pe.wait_ge(e_xg[u], 16 * (r + 1))
            if not early(t):
                pe.wait_ge(e_xT.sem, e_xT.at(t - 2, "copy"))
            for k in range(KD):
                mm = pe.transpose(xT_c[u][:, k, :], xg[:, u, k * P:(k + 1) * P], ident[:, :])
            mm.then_inc(e_tp.step("tp"), 1)

        def expert(t):
            return pe.value_load(expert_of[0:1, bass.ds(t, 1)], min_val=0, max_val=E0 - 1)

        def e_gate(t, u, r):
            e = expert(t)
            pe.wait_ge(e_xT.sem, e_xT.at(t, "copy"))
            if not early(t):
                pe.wait_ge(e_silu.sem, e_silu.at(t - 2, "silu"))
            for k in range(KD):
                mm = pe.matmul(up_c[u][0], xTc[:, u, k, :],
                               W0[:, bass.ds(e, 1), k * I0:(k + 1) * I0].rearrange("p a n -> p (a n)"),
                               start=k == 0, stop=k == KD - 1)
            mm.then_inc(e_up.step("a"), 1)

        def e_value(t, u, r):
            e = expert(t)
            if not early(t):
                pe.wait_ge(e_h.sem, e_h.at(t - 2, "h"))
            for k in range(KD):
                mm = pe.matmul(up_c[u][1], xTc[:, u, k, :],
                               W0[:, bass.ds(e, 1), (KD + k) * I0:(KD + k + 1) * I0].rearrange("p a n -> p (a n)"),
                               start=k == 0, stop=k == KD - 1)
            mm.then_inc(e_up.step("b"), 1)

        def e_hturn(t, u, r):
            pe.wait_ge(e_h.sem, e_h.at(t, "h"))
            if not (isinstance(t, int) and t < 1):
                pe.wait_ge(e_hT.sem, e_hT.at(t - 1, "copy"))
            for k in range(KI):
                mm = pe.transpose(hT_c[:, k, :], hh[:, u, k * P:(k + 1) * P], ident[:, :])
            mm.then_inc(e_htp.step("tp"), 1)

        def e_down(t, u, r):
            e = expert(t)
            pe.wait_ge(e_hT.sem, e_hT.at(t, "copy"))
            if not (isinstance(t, int) and t < 1):
                pe.wait_ge(e_ys.sem, e_ys.at(t - 1, "y"))
            for k in range(KI):
                o = 2 * KD * I0 + k * D
                mm = pe.matmul(y_c, hTc[:, u, k, :],
                               W0[:, bass.ds(e, 1), o:o + D].rearrange("p a n -> p (a n)"),
                               start=k == 0, stop=k == KI - 1)
            mm.then_inc(e_dn.step("y"), 1)

        pe.wait_ge(got_w0, 16 * 3 * E0)
        after(pe, r_dve)
        pipeline(pe, TILES0, (0, e_turn), (1, e_gate), (2, e_hturn), (1, e_value), (2, e_down))

        def g_turn(t, u, r):
            pe.wait_ge(got_c3[u], 16 * (r + 1))
            if not early(t):
                pe.wait_ge(g_thi.sem, g_thi.at(t - 2, "hi"))
                pe.wait_ge(g_tlo.sem, g_tlo.at(t - 2, "lo"))
            for k in range(KD):
                mm = pe.transpose(cT_d[u][:, k, :], cin3[:, u, k * P:(k + 1) * P], ident[:, :])
            mm.then_inc(g_tp.step("tp"), 1)

        def g_score(t, u, r):
            pe.wait_ge(g_lo.sem, g_lo.at(t, "x"))
            if not early(t):
                pe.wait_ge(g_ex.sem, g_ex.at(t - 2, "e1"))
            for k in range(KD):
                mm = mm3(pe, sc_d[u][:, k, :], both(cs, A, u, slice(k * P, (k + 1) * P)), both(xs, A, u, A), True, True)
            mm.then_inc(g_sc.step("s"), 1)

        def g_value(t, u, r):
            pe.wait_ge(g_alo.sem, g_alo.at(t, "a1"))
            pe.wait_ge(g_tlo.sem, g_tlo.at(t, "lo"))
            if not early(t):
                pe.wait_ge(g_res.sem, g_res.at(t - 2, "add"))
            for k in range(KD):
                mm = mm3(pe, o_d[u], both(cT, A, u, k, A), both(at, A, u, k, A), k == 0, k == KD - 1)
            mm.then_inc(g_o.step("o"), 1)

        after(pe, e_ys)
        pipeline(pe, B, (2, g_score), (4, g_turn), (5, g_value))

        def x3_parts(u, k):
            return x3T[:, u, 0, k, :], x3T[:, u, 1, k, :]

        def p_turn(t, u, r):
            pe.wait_ge(p_xn.sem, p_xn.at(t, "xn"))
            if not early(t):
                pe.wait_ge(p_hi.sem, p_hi.at(t - 2, "hi"))
                pe.wait_ge(p_lo.sem, p_lo.at(t - 2, "lo"))
            for k in range(KD):
                mm = pe.transpose(x3T_e[u][:, k, :], xn3[:, u, k * P:(k + 1) * P], ident[:, :])
            mm.then_inc(p_tp.step("tp"), 1)

        def p_gates(t, u, r):
            pe.wait_ge(p_lo.sem, p_lo.at(t, "lo"))
            if not early(t):
                pe.wait_ge(p_act.sem, p_act.at(t - 2, "copy"))
            for k in range(KD):
                mm = mm3(pe, gs_e[u], x3_parts(u, k), both(gate1, A, k, A), k == 0, k == KD - 1)
            mm.then_inc(p_gs.step("gs"), 1)

        def h_place(t, u, r):
            pe.wait_ge(h_rt.sem, h_rt.at(t, "mask"))
            if not (isinstance(t, int) and t < 1):
                pe.wait_ge(h_wt.sem, h_wt.at(t - 1, "valid"))
            pe.matmul(pos_e, before[:, :], mask1[:, u, :], start=True, stop=False)
            pe.matmul(pos_e, ones[:, :], macc[:, u, :], start=False, stop=True).then_inc(h_pos.step("pos"), 1)

        def h_upc(c):
            def body(t, u, r):
                if c == 0:
                    pe.wait_ge(h_x.sem, h_x.at(t, "copy"))
                if c >= 2:
                    pe.wait_ge(h_hv.sem, h_hv.at(t, f"v{c - 2}"))
                elif not (isinstance(t, int) and t < 1):
                    pe.wait_ge(h_hv.sem, h_hv.at(t - 1, f"v{NCH - 2 + c}"))
                for k in range(KD):
                    mm = mm3(pe, up_e[c % 2], x3_parts(u, k), both(wup_s, A, k, slice(c * CH, (c + 1) * CH), A),
                             k == 0, k == KD - 1)
                mm.then_inc(h_up.step(f"u{c}"), 1)
            return body

        def h_tr(c):
            def body(t, u, r):
                b, _, in_t = h_buffer(t, u, c)
                if c == NCH:
                    wait_apart(pe, consts, (h_hlo.sem, h_hlo.at(t, f"t{c - 2}")), (h_rt.sem, h_rt.at(t, "hs")))
                elif c >= 2:
                    pe.wait_ge(h_hlo.sem, h_hlo.at(t, f"t{c - 2}"))
                elif not (isinstance(t, int) and t < 1):
                    pe.wait_ge(h_hlo.sem, h_hlo.at(t - 1, f"t{NCH - 1 + c}"))
                if c == NCH:
                    mm = pe.transpose(in_t, hs[:, u, :], ident[:, :])
                else:
                    pe.wait_ge(h_hw.sem, h_hw.at(t, f"w{c}"))
                    for k in range(KCH):
                        mm = pe.transpose(in_t[:, k, :], hw[:, c % 2, k * 4:(k + 1) * 4, :].rearrange("p e h -> p (e h)"),
                                          ident[:, :])
                mm.then_inc(h_htp.step(f"t{c}"), 1)
            return body

        def h_downc(c):
            def body(t, u, r):
                b, (hi, lo), _ = h_buffer(t, u, c)
                pe.wait_ge(h_hlo.sem, h_hlo.at(t, f"t{c}"))
                if c == 0 and not early(t):
                    pe.wait_ge(h_out.sem, h_out.at(t - 2, "out"))
                if c == NCH:
                    mm = mm3(pe, y_e[u], (hi, lo), both(wsd_s, A, A), False, True)
                else:
                    for k in range(KCH):
                        mm = mm3(pe, y_e[u], (hi[:, k, :], lo[:, k, :]), both(wdn_s, A, c * KCH + k, A),
                                 c == 0 and k == 0, False)
                mm.then_inc(h_dn.step(f"d{c}"), 1)
            return body

        after(pe, w1_sp, g_res)
        pipeline(pe, B, (1, p_turn), (2, p_gates))
        after(pe, p_act)
        pipeline(pe, B, *h_stages(dict(pos=h_place, up=h_upc, tr=h_tr, down=h_downc)))

    st.close()


_INS = ["x", "ctx_2048", "L0_xattn_Wh", "L0_xattn_wg_w", "L0_xattn_wo_w", "L0_xattn_gn_gamma", "L0_xattn_gn_beta",
        "L0_ffn_w_gate", "L0_ffn_w1", "L0_ffn_w3", "L0_ffn_w2", "L1_ffn_w_gate", "L1_ffn_w_shared_up",
        "L1_ffn_w_shared_down", "L1_ffn_w_up", "L1_ffn_w_down"]


def decay_table(heads, seq, width):
    gam = (1.0 - 2.0 ** (-5.0 - np.arange(heads, dtype=np.float32))).astype(np.float32)
    idx = np.arange(seq, dtype=np.float32)
    expo = idx[None, :] - idx[:, None]
    d = np.where(expo[None] <= 0, gam[:, None, None] ** expo[None], 0.0).astype(np.float32)
    d = d / np.sqrt(d.sum(axis=-1))[:, None, :] / np.sqrt(np.float32(width))
    return np.ascontiguousarray(d.transpose(2, 0, 1)).astype(np.float32)


def kernel(**inputs):
    import numpy as _np
    import concourse.bacc as _bacc
    from concourse import mybir as _mybir
    from concourse.bass_utils import run_bass_kernel_spmd as _run

    nc = _bacc.Bacc("TRN2", target_bir_lowering=False, num_devices=1)
    arrays, args = {}, []

    def give(name, a):
        arrays[f"in_{name}"] = a
        args.append(nc.dram_tensor(f"in_{name}", a.shape, _mybir.dt.from_np(a.dtype), kind="ExternalInput").ap())

    for name in _INS:
        give(name, _np.ascontiguousarray(inputs[name]))
    give("decay", decay_table(H0, P, P))
    shape = tuple(inputs["x"].shape)
    args.append(nc.dram_tensor("out_0", shape, _mybir.dt.float32, kind="ExternalOutput").ap())
    build(nc, *args)
    r = _run(nc, [arrays], core_ids=[0])
    return r.results[0]["out_0"]
```

```python
from contextlib import ExitStack

import numpy as np

import concourse.bass as bass
from concourse import mybir

F32 = mybir.dt.float32
F32R = mybir.dt.float32r
BF16 = mybir.dt.bfloat16
I32 = mybir.dt.int32
U32 = mybir.dt.uint32
ACT = mybir.ActivationFunctionType
ALU = mybir.AluOpType
X = mybir.AxisListType.X

P = 128
B = 16
D = 256
KD = D // P
H0 = 2
E0, TOP0, I0 = 8, 2, 512
KI = I0 // P
SOFTCAP = 30.0
E1, TOP1, HID1, CAP1 = 64, 6, 32, 128
HS = 64
LN_EPS, GN_EPS = 1e-5, 1e-3
TILES0 = (B * P * TOP0 - E0) // P + E0
TJ = TILES0 + 1
NOWHERE = float(1 << 20)
NPAIR = B * TOP0
W0E = 2 * KD * I0 + KI * D
CH = 8
NCH = E1 // CH

KCH = CH * HID1 // P
GS = E1 + 2 * HS


YG = 4
VG = 4
W1_FROM = 3
LOADS = (0, 2, 6, B)
LOADS = tuple(zip(LOADS[:-1], LOADS[1:]))


class Steps:

    def __init__(self, sem, names, items=1):
        self.sem, self.names, self.items, self.n = sem, names.split(), items, 0
        assert len(set(self.names)) == len(self.names)

    def step(self, name):
        want = self.names[self.n % len(self.names)]
        assert want == name, (name, want)
        self.n += 1
        return self.sem

    def at(self, item, name):
        return item * len(self.names) + (self.names.index(name) + 1)

    @property
    def all(self):
        return self.items * len(self.names)


def after(eng, *phases):
    for steps in phases:
        eng.wait_ge(steps.sem, steps.all)


def wait_apart(eng, consts, *waits):
    values = [v if isinstance(v, int) else eng.to_reg(v) for _, v in waits]
    eng.wait_ge(consts.sem, consts.all)
    for (sem, _), v in zip(waits, values):
        eng.wait_ge(sem, v)


def wait_loaded(eng, sems, t):
    for (start, end), sem in zip(LOADS, sems):
        if (isinstance(t, int) and t == start) or (not isinstance(t, int) and end == B):
            eng.wait_ge(sem, 16)


def early(t):
    return isinstance(t, int) and t < 2


def pipeline(eng, n, *stages, peel=0):
    most = max(lag for lag, _ in stages)
    head = max(most + 2 + most % 2, peel)

    def one(s, parity, half):
        for lag, body in stages:
            if isinstance(s, int) and not 0 <= s - lag < n:
                continue
            u = (parity - lag) % 2
            body(s - lag, u, half - (lag - parity + u) // 2)

    for s in range(head):
        one(s, s % 2, s // 2)
    with eng.Fori(head // 2, n // 2) as i:
        for v in range(2):
            one(2 * i + v, v, i)
    for s in range(n // 2 * 2, n + most):
        one(s, s % 2, s // 2)


def mm3(pe, out, lhs, rhs, first, last, **kw):
    (lh, ll), (rh, rl) = lhs, rhs
    pe.matmul(out, lh, rh, start=first, stop=False, **kw)
    pe.matmul(out, lh, rl, start=False, stop=False, **kw)
    return pe.matmul(out, ll, rh, start=False, stop=last, **kw)


class Map:

    def __init__(self, nc, at, end):
        self.nc, self.at, self.end = nc, at, end

    def __call__(self, name, shape, dt=F32):
        size = int(np.prod(shape[1:])) * (2 if dt == BF16 else 4)
        t = self.nc.alloc_sbuf_tensor_at(name, shape, dt, offset=self.at)
        self.at += (size + 31) // 32 * 32
        assert self.at <= self.end, (name, self.at, self.end)
        return t

    def pair(self, name, shape):
        return self(name + "_hi", shape, F32R), self(name + "_lo", shape, F32R)


def build(nc, x, ctx, Wh, wg, wo, gamma, beta, wgate0, w1, w3, w2, wgate1, wsu, wsd, wup, wdown, decay, out):
    st = ExitStack()
    KB = 1024
    base = (nc.sbuf_base + 63) // 64 * 64
    END = nc.sbuf_usable_end // 64 * 64
    keep = Map(nc, base, base + 27 * KB)
    big = Map(nc, keep.end, keep.end + 98 * KB)
    W = big.end
    big1 = Map(nc, keep.end, W)
    work_a, work_r, work_c, work_d = Map(nc, W, END), Map(nc, W, END), Map(nc, W, END), Map(nc, W, END)

    def psum(name, shape, dt=F32):
        return st.enter_context(nc.psum_tensor(name, shape, dt))

    def sem(name):
        return st.enter_context(nc.semaphore(name))

    xf = x.rearrange("b s d -> (b s) d")
    cf = ctx.rearrange("b s d -> (b s) d")
    of = out.rearrange("b s d -> (b s) d")
    xn_rows = nc.dram_tensor("xn_rows", [B * P, D], F32, kind="Internal").ap()
    y_rows = nc.dram_tensor("y_rows", [B * P * TOP0, D], F32, kind="Internal").ap()

    ident = keep("ident", [P, P])
    before = keep("before", [P, P], BF16)
    ones = keep("ones", [P, P], BF16)
    iota_row = keep("iota_row", [P, P])
    eps = keep("eps", [P, 2])
    x_res = keep("x_res", [P, B, D])
    bn = keep("bn", [P, B, 6])
    mom = keep("mom", [P, 5, B])
    mean = keep("mean", [P, B])
    sdev = keep("sdev", [P, B])
    rstd = keep("rstd", [P, B])
    gate1 = keep.pair("gate1", [P, KD, GS])
    wsd_s = keep.pair("wsd_s", [HS, D])
    lg = keep("lg", [P, B, E0])
    table = keep("table", [P, 3, TJ], I32)
    expert_of = keep("expert_of", [P, TJ], I32)

    W0 = big("W0", [P, E0, W0E])
    V = Map(nc, big1.at, W).pair("V", [P, H0, B, P])
    wup_s = big1.pair("wup_s", [P, E1, KD, 2 * HID1])
    wup_raw = Map(nc, big1.at - KD * E1 * 2 * HID1 * 4, W)("wup_raw", [P, E1, KD, 2 * HID1])
    wdn_s = big1.pair("wdn_s", [P, E1 * HID1 // P, D])
    wdn_raw = Map(nc, big1.at - E1 * HID1 // P * D * 4, W)("wdn_raw", [P, E1 * HID1 // P, D])
    w1_parts = [(wup[e:e + 16].rearrange("e (p k) n -> p e (k n)", k=KD),
                 *(w[:, e:e + 16, :, :].rearrange("p e k n -> p e (k n)") for w in (wup_raw, *wup_s)))
                for e in range(0, E1, 16)]
    w1_parts += [(wdown.rearrange("(c e) h d -> (e h) c d", e=P // HID1)[:, k:k + 8, :],
                  *(w[:, k:k + 8, :] for w in (wdn_raw, *wdn_s))) for k in (0, 8)]

    wh_raw = work_a("wh_raw", [P, H0, P])
    wg_raw = work_a("wg_raw", [P, KD, D])
    wo_raw = work_a("wo_raw", [P, KD, D])
    gate0_raw = work_a("gate0_raw", [P, KD, E0])
    gate1_raw = work_a("gate1_raw", [P, KD, GS])
    wsd_raw = work_a("wsd_raw", [HS, D])
    wh = work_a.pair("wh", [P, H0, P])
    wgs = work_a.pair("wgs", [P, KD, D])
    wos = work_a.pair("wos", [P, KD, D])
    xTd = work_a("xTd", [P, 2, KD, P])
    dec = work_a("dec", [P, H0, P])
    gam = work_a("gam", [P, D])
    bet = work_a("bet", [P, D])
    G = work_a("G", [P, B, D])
    Gg = work_a("Gg", [P, 2, D])
    Gb = work_a("Gb", [P, 2, D])
    cen = Map(nc, work_a.at, END)("cen", [P, 2, D])
    cin = work_a("cin", [P, 2, D])
    xn = work_a("xn", [P, 2, D])
    sm = work_a("sm", [P, 2, 10])
    tT = work_a.pair("tT", [P, 2, 4, P])
    xnd = Map(nc, work_a.at, END)("xnd", [P, 2, D])
    qk = work_a.pair("qk", [P, 2, 4, P])
    At = work_a.pair("At", [P, H0, P])
    Araw = work_a("Araw", [P, H0, P])
    rows = work_a("rows", [P, B, D])

    rt = {}
    for name, shape in (("prob", [B, E0]), ("rev", [E0]), ("key", [B, E0]), ("hot1", [B, E0]), ("hot2", [B, E0]),
                        ("rest", [B, E0]), ("wsel", [TOP0, B]), ("m", [B]), ("r", [B]), ("k", [B]), ("slot", [B, E0]),
                        ("pick", [B, E0]), ("slotk", [TOP0, B]), ("cnt", [E0]), ("steps128", [B]), ("over", [E0, B]),
                        ("tiles", [E0]), ("one8", [E0]), ("tend", [E0]), ("tstart", [E0]), ("j128", [TJ + 1]),
                        ("jrow", [TJ]), ("passed", [TJ, E0]), ("ef", [TJ]), ("ge", [NPAIR, TJ + 1]),
                        ("hotj", [NPAIR, TJ]), ("tile_of", [NPAIR]), ("row_of", [NPAIR]), ("hotp", [NPAIR, P]),
                        ("val", [3, NPAIR]), ("R", [NPAIR, 3, TJ]), ("T", [3, TJ]), ("none", [TJ])):
        rt[name] = work_r("rt_" + name, [P, *shape])
    mask0 = work_r("mask0", [P, B, E0], BF16)

    xg = work_c("xg", [P, 2, D])
    xTc = work_c.pair("xTc", [P, 2, KD, P])
    sa = work_c("sa", [P, 2, I0])
    hh = work_c("hh", [P, 2, I0])
    hTc = work_c.pair("hTc", [P, 2, KI, P])
    wsp = [work_c.pair("wsp_" + name, [P, 2, W0E // 3]) for name in ("w1", "w3", "w2")]
    ys = work_c("ys", [P, 2, D])
    stage_g = work_c("stage_g", [P, 2, 1], I32)
    stage_s = work_c("stage_s", [P, 2, 1], I32)



    ctx2 = work_d("ctx2", [P, B, D])
    cin3 = work_d("cin3", [P, 2, D])
    xn2 = work_d("xn2", [P, 2, D])
    cs = work_d.pair("cs", [P, 2, D])
    xs = work_d.pair("xs", [P, 2, D])
    cT = work_d.pair("cT", [P, 2, KD, P])
    yin = Map(nc, work_d.at, work_d.end)("yin", [P, B, TOP0 * D])
    ex = work_d("ex", [P, 2, KD, D])
    at = work_d.pair("at", [P, 2, KD, D])
    smx = work_d("smx", [P, 2, 4, KD])

    work_e = Map(nc, W, END)
    x3_all = work_e("x3_all", [P, B, 2 * KD * P], F32R)
    shr = work_e("shr", [P, B, 2 * HS])
    esc = work_e("esc", [P, B, E1])
    xn3 = work_e("xn3", [P, 2, D])
    x3T = work_e("x3T", [P, 2, 2, KD, P], F32R)
    sg = work_e("sg", [P, 2, CH, HID1])
    hv = work_e("hv", [P, 2, CH, HID1])
    hw = work_e("hw", [P, 2, CH, HID1])
    hT = work_e.pair("hT", [P, 2, KCH, P])
    sgs = work_e("sgs", [P, 2, HS])
    hs = work_e("hs", [P, 2, HS])
    escp = work_e("escp", [P, E1])
    sc = work_e("sc", [P, 2, E1])
    top8 = work_e("top8", [P, 8])
    idx8 = work_e("idx8", [P, 8], U32)
    idxf = work_e("idxf", [P, 8])
    hot = work_e("hot", [P, TOP1, E1])
    mask1 = work_e("mask1", [P, 2, E1], BF16)
    macc = work_e("macc", [P, 2, E1], BF16)
    ssel = work_e("ssel", [P, E1])
    wsum = work_e("wsum", [P, 2])
    valid = work_e("valid", [P, E1])
    wt = work_e("wt", [P, 2, E1])
    outb = work_e("outb", [P, 2, D])

    bank = [psum(f"bank{i}", [P, 512]) for i in range(8)]

    def view(i, *shape):
        names = "abc"[:len(shape)]
        n = int(np.prod(shape))
        return bank[i][:, 0:n].rearrange(f"p ({' '.join(names)}) -> p {' '.join(names)}",
                                         **dict(zip(names, shape)))

    tp_a = [view(i, 4, P) for i in (0, 1)]
    qk_a = [view(i, 4, P) for i in (2, 3)]
    S_a = [bank[4][:, h * P:(h + 1) * P] for h in range(H0)]
    v_a = view(5, H0, P)
    g_a = [bank[i][:, 0:D] for i in (6, 7)]
    two_a = [view(i, 2, P) for i in (0, 1)]
    o_b = [view(i, VG, P) for i in range(8)]
    row_a = [bank[i][:, 0:D] for i in (6, 7)]
    two_d = [view(i, 2, P) for i in (2, 3)]
    lg_d = [bank[i][:, 0:E0] for i in (4, 5)]
    pos_r = view(0, B + 1, E0)
    tab_r = view(1, 3, TJ)
    xT_c = [view(i, KD, P) for i in (0, 1)]
    up_c = [[bank[2][:, :], bank[3][:, :]], [bank[4][:, :], bank[5][:, :]]]
    hT_c = view(6, KI, P)
    y_c = bank[7][:, 0:D]
    cT_d = [view(i, KD, P) for i in (0, 1)]
    sc_d = [view(i, KD, D) for i in (2, 3)]
    o_d = [bank[i][:, 0:D] for i in (4, 5)]
    up_e = [view(i, CH, 2 * HID1) for i in (0, 1)]
    hT_e = [view(i, KCH, P) for i in (2, 3)]
    y_e = [bank[i][:, 0:D] for i in (4, 5)]
    x3T_e = [view(i, KD, P) for i in (0, 1)]
    gs_e = [bank[i][:, 0:GS] for i in (2, 3)]
    pos_e = bank[7][:, 0:E1]

    small = {n: sem("got_" + n) for n in ("wh", "wg", "wo", "gate0", "gate1", "wsd", "decay", "gamma", "beta")}
    got_x = [sem(f"got_x{g}") for g in range(len(LOADS))]
    got_c = [sem(f"got_c{g}") for g in range(len(LOADS))]
    got_w0 = sem("got_w0")
    got_w1 = [sem(f"got_w1_{n}") for n in range(len(w1_parts))]
    consts = Steps(sem("consts"), "zero_ident ident zero_before before ones iota eps_ln eps_gn")
    pool_w = Steps(sem("pool_weights"), "wo_hi wo_lo gate1_hi gate1_lo wsd_hi wsd_lo")
    dve_w = Steps(sem("dve_weights"), "wh_hi wh_lo wg_hi wg_lo")
    a_ln = Steps(sem("a_norm"), "stats aggr rstd xn", B)
    a_sd = Steps(sem("a_sdev"), "sd", B)
    a_cin = Steps(sem("a_context_taken"), "copy", B)
    a_tp = Steps(sem("a_turned"), "tp", B)
    a_thi = Steps(sem("a_turned_hi"), "hi", B)
    a_tlo = Steps(sem("a_turned_lo"), "lo", B)
    a_proj = Steps(sem("a_projected"), "qk gate v", B)
    a_vhi = Steps(sem("a_values_hi"), "hi", B)
    a_vlo = Steps(sem("a_values_lo"), "lo", B)
    a_qhi = Steps(sem("a_qk_hi"), "hi", B)
    a_qlo = Steps(sem("a_qk_lo"), "lo", B)
    a_sc = Steps(sem("a_scored"), "s", B)
    a_gate = Steps(sem("a_gate"), "relu", B)

    b_mask = Steps(sem("b_masked"), "masked0 masked1 abs floor hi lo")
    b_names = " ".join(f"g{g}h{h}" for g in range(B // VG) for h in range(H0))
    b_o = Steps(sem("b_heads"), b_names)
    b_keep = Steps(sem("b_heads_kept"), b_names)
    b_stat = Steps(sem("b_heads_stats"), "stats", B)
    MOMENTS = "sum diff m2 mean sq var"
    mo = [Steps(sem(f"moments{i}"), MOMENTS) for i in range(3)]
    mo_sd = [Steps(sem(f"moments_sdev{i}"), "sd") for i in range(3)]
    mo_rs = [Steps(sem(f"moments_rstd{i}"), "rstd") for i in range(3)]
    c_gb = Steps(sem("c_gate_affine"), "gamma beta", B)
    c_wy = Steps(sem("c_gated"), "centred scaled", B)
    c_tp = Steps(sem("c_turned"), "tp", B)
    c_hi = Steps(sem("c_turned_hi"), "hi", B)
    c_lo = Steps(sem("c_turned_lo"), "lo", B)
    c_o = Steps(sem("c_out"), "o", B)
    c_res = Steps(sem("c_residual"), "add stats", B)
    d_ln = Steps(sem("d_moments"), "aggr rstd", B)
    d_sd = Steps(sem("d_sdev"), "sd", B)
    d_xn = Steps(sem("d_norm"), "xn", B)
    d_row = Steps(sem("d_rows_kept"), "copy", B)
    d_st = [sem("d_stored0"), sem("d_stored1")]
    d_tp = Steps(sem("d_turned"), "tp", B)
    d_kept = Steps(sem("d_turned_kept"), "copy", B)
    d_lg = Steps(sem("d_logits"), "logits", B)
    d_lgc = Steps(sem("d_logits_kept"), "copy", B)
    r_act = Steps(sem("r_scalar"), "tanh exp")
    r_iota = Steps(sem("r_iotas"), "rev steps128 j128 jrow code token")
    r_dve = Steps(sem("r_vector"), "cap max sub sum rsum prob "
                  "best1 is1 key1 first1 hot1 w1 rest best2 is2 key2 first2 hot2 w2 mask "
                  "count over tiles one8 tend tstart slot pick1 slot1 pick2 slot2 passed e emin eint "
                  "ge hotj tile_of row_of hotp0 r_w0 hotp1 r_w1 none dest t_tok t_w t_dst")
    r_pool = Steps(sem("r_gpsimd"), "code0 tok0 code1 tok1")
    r_pe = Steps(sem("r_tensor"), "pos tab")
    e_tok = Steps(sem("e_tokens"), "copy", TILES0)

    e_xg = [sem("e_rows0"), sem("e_rows1")]
    e_yst = [sem("e_stored0"), sem("e_stored1")]
    e_tp = Steps(sem("e_turned"), "tp", TILES0)
    e_xhi = Steps(sem("e_turned_hi"), "hi", TILES0)
    e_xlo = Steps(sem("e_turned_lo"), "lo", TILES0)
    e_whi = [Steps(sem(f"e_{name}_hi"), "hi", TILES0) for name in ("w1", "w3", "w2")]
    e_wlo = [Steps(sem(f"e_{name}_lo"), "lo", TILES0) for name in ("w1", "w3", "w2")]
    e_up = Steps(sem("e_up"), "a b", TILES0)
    e_silu = Steps(sem("e_silu"), "silu", TILES0)
    e_h = Steps(sem("e_hidden"), "h", TILES0)
    e_htp = Steps(sem("e_hidden_turned"), "tp", TILES0)
    e_hhi = Steps(sem("e_hidden_hi"), "hi", TILES0)
    e_hlo = Steps(sem("e_hidden_lo"), "lo", TILES0)
    e_dn = Steps(sem("e_down"), "y", TILES0)
    e_ys = Steps(sem("e_weighted"), "dst y", TILES0)
    f_yin = [sem(f"f_rows{g}") for g in range(B // YG)]
    f_two = Steps(sem("f_both_experts"), "y", B // 2)
    f_add = Steps(sem("f_added"), "x", B // 2)
    f_stat = Steps(sem("f_stats"), "stats0 stats1", B // 2)
    w1_hi = Steps(sem("w1_split_hi"), " ".join(f"hi{i}" for i in range(len(w1_parts))))
    w1_lo_up = Steps(sem("w1_up_lo"), "lo", B)
    w1_lo_dn = Steps(sem("w1_down_lo"), "lo", B)
    got_c2 = [sem(f"got_ctx2_{g}") for g in range(len(LOADS))]
    got_c3 = [sem("took_ctx0"), sem("took_ctx1")]
    g_xn = Steps(sem("g_norm"), "xn", B)
    g_hi = Steps(sem("g_split_hi"), "ctx x", B)
    g_lo = Steps(sem("g_split_lo"), "ctx x", B)
    g_tp = Steps(sem("g_turned"), "tp", B)
    g_thi = Steps(sem("g_turned_hi"), "hi", B)
    g_tlo = Steps(sem("g_turned_lo"), "lo", B)
    g_sc = Steps(sem("g_scored"), "s", B)
    g_mx = Steps(sem("g_max"), "max neg", B)
    g_ex = Steps(sem("g_exp"), "e0 e1", B)
    g_rs = Steps(sem("g_rsum"), "r", B)
    g_ahi = Steps(sem("g_attn_hi"), "a0 a1", B)
    g_alo = Steps(sem("g_attn_lo"), "a0 a1", B)
    g_o = Steps(sem("g_out"), "o", B)
    g_res = Steps(sem("g_residual"), "add stats", B)
    p_xn = Steps(sem("p_norm"), "xn", B)
    p_tp = Steps(sem("p_turned"), "tp", B)
    p_hi = Steps(sem("p_turned_hi"), "hi kept", B)
    p_lo = Steps(sem("p_turned_lo"), "lo kept", B)
    p_gs = Steps(sem("p_gate_shared"), "gs", B)
    p_act = Steps(sem("p_gate_scalar"), "exp copy", B)
    h_x = [sem("h_tile_taken0"), sem("h_tile_taken1")]
    h_sh = Steps(sem("h_shared_silu"), "silu", B)
    h_hw = Steps(sem("h_hidden_weighted"), " ".join(f"w{c}" for c in range(NCH)), B)
    h_rt = Steps(sem("h_route"), "macc0 plus sig top index indexf hot mask sel sum rsum hs", B)
    h_pos = Steps(sem("h_position"), "pos", B)
    h_wt = Steps(sem("h_weights"), "valid wt", B)
    h_up = Steps(sem("h_up"), " ".join(f"u{c}" for c in range(NCH)), B)
    h_silu = Steps(sem("h_silu"), " ".join(f"s{c}" for c in range(NCH)), B)
    h_hv = Steps(sem("h_hidden"), " ".join(f"v{c}" for c in range(NCH)), B)
    h_htp = Steps(sem("h_hidden_turned"), " ".join(f"t{c}" for c in range(NCH + 1)), B)
    h_hhi = Steps(sem("h_hidden_hi"), " ".join(f"t{c}" for c in range(NCH + 1)), B)
    h_hlo = Steps(sem("h_hidden_lo"), " ".join(f"t{c}" for c in range(NCH + 1)), B)
    h_dn = Steps(sem("h_down"), " ".join(f"d{c}" for c in range(NCH + 1)), B)
    h_out = Steps(sem("h_result"), "out", B)
    h_st = [sem("h_stored0"), sem("h_stored1")]

    def h_slot(u, c):
        return (c + u) % 2

    def h_buffer(t, u, c):
        b = h_slot(u, c)
        if c == NCH:
            return b, (hT[0][0:HS, b, 0, :], hT[1][0:HS, b, 0, :]), hT_e[b][0:HS, 0, :]
        return b, (hT[0][:, b, :, :], hT[1][:, b, :, :]), hT_e[b]

    def wait_h_free(eng, t, c):
        if c >= 2:
            eng.wait_ge(h_dn.sem, h_dn.at(t, f"d{c - 2}"))
        elif not (isinstance(t, int) and t < 1):
            eng.wait_ge(h_dn.sem, h_dn.at(t - 1, f"d{NCH - 1 + c}"))

    def h_stages(f):
        order = []

        def put(lag, name, *args):
            if name in f:
                order.append((lag, f[name](*args) if args else f[name]))

        turned = {0: [(2, NCH - 1)], 1: [(2, NCH), (1, 0)]}
        downs = {0: [(2, NCH - 2)], 1: [(2, NCH - 1)], 2: [(2, NCH), (1, 0)]}
        for c in range(NCH):
            put(1, "up", c)
            put(1, "silu", c)
            put(1, "vec", c)
            put(1, "weigh", c)
            for lag, q in turned.get(c, [(1, c - 1)]):
                put(lag, "tr", q)
                put(lag, "high", q)
                put(lag, "low", q)
            for lag, q in downs.get(c, [(1, c - 2)]):
                put(lag, "down", q)
                if q == NCH:
                    put(2, "result")
            if c == 4:
                put(0, "shared")
            put(0, "route", c)
            if c == 6:
                put(0, "pos")
            if c == 7:
                put(0, "weights")
        return order

    def tile_of(buf, t):
        return buf[:, bass.ds(t, 1), :].rearrange("p a d -> p (a d)")

    def x3_part(t, j):
        return tile_of(x3_all, t)[:, j * KD * P:(j + 1) * KD * P]

    def load_expert(eng, t):
        return eng.value_load(expert_of[0:1, bass.ds(t, 1)], min_val=0, max_val=E0 - 1)

    def expert_part(e, n):
        return W0[:, bass.ds(e, 1), n * W0E // 3:(n + 1) * W0E // 3].rearrange("p a n -> p (a n)")

    def wait_part_used(eng, t, n):
        if not early(t):
            steps, name = ((e_up, "a"), (e_up, "b"), (e_dn, "y"))[n]
            eng.wait_ge(steps.sem, steps.at(t - 2, name))

    block = st.enter_context(nc.Block())

    @block.sync
    def _(sp):
        def store_rows(t, u, r):
            wait_apart(sp, consts, (d_row.sem, d_row.at(t, "copy")))
            sp.dma_start(xn_rows[bass.ds(t * P, P), :], rows[:, bass.ds(t, 1), :].rearrange("p a d -> p (a d)")
                         ).then_inc(d_st[u], 16)


        def take_ctx(t, u, r):
            wait_loaded(sp, got_c2, t)
            if not early(t):
                wait_apart(sp, consts, (g_tp.sem, g_tp.at(t - 2, "tp")))
            sp.dma_start(cin3[:, u, :], tile_of(ctx2, t)).then_inc(got_c3[u], 16)

        def take_tile(t, u, r):
            if not early(t):
                wait_apart(sp, consts, (h_up.sem, h_up.at(t - 2, f"u{NCH - 1}")))
            sp.dma_start(x3T[:, u].rearrange("p j k d -> p (j k d)").bitcast(F32), tile_of(x3_all, t).bitcast(F32)).then_inc(h_x[u], 16)

        def store(t, u, r):
            wait_apart(sp, consts, (h_out.sem, h_out.at(t, "out")))
            sp.dma_start(out[bass.ds(t, 1), :, :].rearrange("a p d -> p (a d)"), outb[:, u, :]
                         ).then_inc(h_st[u], 16)

        for (a, b), gx, gc in zip(LOADS, got_x, got_c):
            sp.dma_start(x_res[:, a:b, :], x[a:b].rearrange("b p d -> p b d")).then_inc(gx, 16)
            sp.dma_start(rows[:, a:b, :], ctx[a:b].rearrange("b p d -> p b d")).then_inc(gc, 16)
        sp.dma_start(dec[:, :, :], decay).then_inc(small["decay"], 16)
        sp.dma_start(gam[:, :], gamma.rearrange("(a d) -> a d", a=1).broadcast_to([P, D])).then_inc(small["gamma"], 16)
        sp.dma_start(bet[:, :], beta.rearrange("(a d) -> a d", a=1).broadcast_to([P, D])).then_inc(small["beta"], 16)
        sp.dma_start(wo_raw[:, :, :], wo.rearrange("(k p) n -> p k n", p=P)).then_inc(small["wo"], 16)
        sp.dma_start(gate0_raw[:, :, :], wgate0.rearrange("(k p) n -> p k n", p=P)).then_inc(small["gate0"], 16)
        sp.dma_start(gate1_raw[:, :, 0:E1], wgate1.rearrange("(p k) n -> p k n", p=P)).then_inc(small["gate1"], 16)
        sp.dma_start(gate1_raw[:, :, E1:GS], wsu.rearrange("(p k) n -> p k n", p=P)).then_inc(small["gate1"], 16)
        sp.dma_start(wsd_raw[:, :], wsd).then_inc(small["wsd"], 16)
        after(sp, b_o)
        with sp.Fori(0, E0) as e:
            for a, w in ((0, w1), (1, w3)):
                sp.dma_start(W0[:, bass.ds(e, 1), a * KD * I0:(a + 1) * KD * I0]
                             .rearrange("p a (k n) -> p (a k) n", k=KD),
                             w[bass.ds(e, 1), :, :].rearrange("a (k p) n -> p (a k) n", p=P)).then_inc(got_w0, 16)
            sp.dma_start(W0[:, bass.ds(e, 1), 2 * KD * I0:W0E].rearrange("p a (k n) -> p (a k) n", k=KI),
                         w2[bass.ds(e, 1), :, :].rearrange("a (k p) n -> p (a k) n", p=P)).then_inc(got_w0, 16)
        pipeline(sp, B, (0, store_rows))

        sp.wait_ge(e_yst[0], 16 * ((TILES0 + 1) // 2))
        sp.wait_ge(e_yst[1], 16 * (TILES0 // 2))
        for g in range(B // YG):
            sp.dma_start(yin[:, g * YG:(g + 1) * YG, :],
                         y_rows[g * YG * P * TOP0:(g + 1) * YG * P * TOP0, :]
                         .rearrange("(a p k) d -> p a (k d)", k=TOP0, p=P)).then_inc(f_yin[g], 16)
        for (a, b), gc in zip(LOADS, got_c2):
            sp.dma_start(ctx2[:, a:b, :], ctx[a:b].rearrange("b p d -> p b d")).then_inc(gc, 16)
        pipeline(sp, B, (0, take_ctx))
        after(sp, p_hi, p_lo, p_gs)
        pipeline(sp, B, (0, take_tile), (2, store))
        for u in range(2):
            sp.wait_ge(h_st[u], 16 * (B // 2))
            sp.wait_ge(d_st[u], 16 * (B // 2))

    @block.gpsimd
    def _(pool):
        pool.memset(ident[:, :], 0.0).then_inc(consts.step("zero_ident"), 1)
        pool.wait_ge(consts.sem, consts.at(0, "zero_ident"))
        pool.affine_select(out=ident[:, :], in_=ident[:, :], compare_op=ALU.not_equal, fill=1.0, base=0,
                           pattern=[[-1, P]], channel_multiplier=1).then_inc(consts.step("ident"), 1)
        pool.memset(before[:, :], 0.0).then_inc(consts.step("zero_before"), 1)
        pool.wait_ge(consts.sem, consts.at(0, "zero_before"))
        pool.affine_select(out=before[:, :], in_=before[:, :], compare_op=ALU.is_ge, fill=1.0, base=0,
                           pattern=[[-1, P]], channel_multiplier=1).then_inc(consts.step("before"), 1)
        pool.memset(ones[:, :], 1.0).then_inc(consts.step("ones"), 1)
        pool.iota(iota_row[:, :], [[1, P]], base=0, channel_multiplier=0,
                  allow_small_or_imprecise_dtypes=True).then_inc(consts.step("iota"), 1)
        pool.memset(eps[:, 0:1], LN_EPS).then_inc(consts.step("eps_ln"), 1)
        pool.memset(eps[:, 1:2], GN_EPS).then_inc(consts.step("eps_gn"), 1)

        def weights(*names):
            raws = dict(wo=(wo_raw, wos), gate1=(gate1_raw, gate1), wsd=(wsd_raw, wsd_s))
            for name in names:
                rawt, (hi, lo) = raws[name]
                pool.wait_ge(small[name], 32 if name == "gate1" else 16)
                pool.tensor_copy(hi[:], rawt[:]).then_inc(pool_w.step(name + "_hi"), 1)
                pool.wait_ge(pool_w.sem, pool_w.at(0, name + "_hi"))
                pool.tensor_tensor(lo[:], rawt[:], hi[:].bitcast(F32), ALU.subtract
                                   ).then_inc(pool_w.step(name + "_lo"), 1)

        def take_context(t, u, r):
            wait_loaded(pool, got_c, t)
            if not early(t):
                wait_apart(pool, consts, (a_tp.sem, a_tp.at(t - 2, "tp")))
            pool.tensor_copy(cin[:, u, :], tile_of(rows, t)).then_inc(a_cin.step("copy"), 1)

        def affine(t, u, r):
            if not early(t):
                wait_apart(pool, consts, (c_wy.sem, c_wy.at(t - 2, "scaled")))
            g = G[:, bass.ds(t, 1), :].rearrange("p a d -> p (a d)")
            pool.tensor_tensor(Gg[:, u, :], g, gam[:, :], ALU.mult).then_inc(c_gb.step("gamma"), 1)
            pool.tensor_tensor(Gb[:, u, :], g, bet[:, :], ALU.mult).then_inc(c_gb.step("beta"), 1)

        pipeline(pool, B, (0, take_context))
        weights("wo", "gate1", "wsd")
        pool.wait_ge(small["gamma"], 16)
        pool.wait_ge(small["beta"], 16)
        after(pool, a_gate)
        pipeline(pool, B, (0, affine))


        after(pool, d_xn, d_kept, d_lg, c_wy, c_o)
        pool.iota(rt["rev"][:, :], [[-1, E0]], base=E0, channel_multiplier=0,
                  allow_small_or_imprecise_dtypes=True).then_inc(r_iota.step("rev"), 1)
        pool.iota(rt["steps128"][:, :], [[P, B]], base=0, channel_multiplier=0,
                  allow_small_or_imprecise_dtypes=True).then_inc(r_iota.step("steps128"), 1)
        pool.iota(rt["j128"][:, :], [[P, TJ + 1]], base=0, channel_multiplier=0,
                  allow_small_or_imprecise_dtypes=True).then_inc(r_iota.step("j128"), 1)
        pool.iota(rt["jrow"][:, :], [[1, TJ]], base=0, channel_multiplier=0,
                  allow_small_or_imprecise_dtypes=True).then_inc(r_iota.step("jrow"), 1)
        pool.iota(rt["val"][:, 0, :], [[1, TOP0], [P * TOP0, B]], base=1, channel_multiplier=TOP0,
                  allow_small_or_imprecise_dtypes=True).then_inc(r_iota.step("code"), 1)
        pool.iota(rt["val"][:, 1, :], [[0, TOP0], [P, B]], base=0, channel_multiplier=1,
                  allow_small_or_imprecise_dtypes=True).then_inc(r_iota.step("token"), 1)

        pool.wait_ge(r_dve.sem, r_dve.at(0, "hotj"))
        for h in range(2):
            part = slice(h * NPAIR // 2, (h + 1) * NPAIR // 2)
            for n, name in enumerate(("code", "tok")):
                pool.tensor_tensor(rt["R"][:, part, n, :], rt["hotj"][:, part, :],
                                   rt["val"][:, n, part].unsqueeze(2).to_broadcast([P, NPAIR // 2, TJ]), ALU.mult
                                   ).then_inc(r_pool.step(f"{name}{h}"), 1)

        def gather(t, u, r):
            waits = [(e_tok.sem, e_tok.at(t, "copy"))]
            if not early(t):
                waits.append((e_tp.sem, e_tp.at(t - 2, "tp")))
            wait_apart(pool, consts, *waits)
            pool.indirect_dma_start(xg[:, u, :], None, xn_rows,
                                    bass.IndirectOffsetOnAxis(stage_g[:, u, :].bitcast(U32), 0)).then_inc(e_xg[u], 16)

        def scatter(t, u, r):
            wait_apart(pool, consts, (e_ys.sem, e_ys.at(t, "y")))
            pool.indirect_dma_start(y_rows, bass.IndirectOffsetOnAxis(stage_s[:, u, :].bitcast(U32), 0),
                                    ys[:, u, :], None, bounds_check=B * P * TOP0 - 1, oob_is_err=False
                                    ).then_inc(e_yst[u], 16)

        after(pool, r_dve)
        for u in range(2):
            pool.wait_ge(d_st[u], 16 * (B // 2))
        def w2_low(t, u, r):
            part = expert_part(load_expert(pool, t), 2)
            wait_part_used(pool, t, 2)
            wait_apart(pool, consts, (e_whi[2].sem, e_whi[2].at(t, "hi")))
            pool.tensor_tensor(wsp[2][1][:, u, :], part, wsp[2][0][:, u, :].bitcast(F32), ALU.subtract
                               ).then_inc(e_wlo[2].step("lo"), 1)

        pool.wait_ge(got_w0, 16 * 3 * E0)
        pipeline(pool, TILES0, (6, scatter), (4, w2_low), (0, gather))

        for t in range(B // 2):
            if 2 * t % YG == 0:
                pool.wait_ge(f_yin[2 * t // YG], 16)
            y = yin[:, 2 * t:2 * t + 2, :]
            pool.tensor_tensor(y[:, :, 0:D], y[:, :, 0:D], y[:, :, D:2 * D], ALU.add).then_inc(f_two.step("y"), 1)

        def g_low(t, u, r):
            waits = [(g_hi.sem, g_hi.at(t, "x"))]
            if not early(t):
                waits.append((g_sc.sem, g_sc.at(t - 2, "s")))
            wait_apart(pool, consts, *waits)
            pool.tensor_tensor(cs[1][:, u, :], tile_of(ctx2, t), cs[0][:, u, :].bitcast(F32), ALU.subtract
                               ).then_inc(g_lo.step("ctx"), 1)
            pool.tensor_tensor(xs[1][:, u, :], xn2[:, u, :], xs[0][:, u, :].bitcast(F32), ALU.subtract
                               ).then_inc(g_lo.step("x"), 1)

        def weights_low(raw, pair, steps, size, ready):
            def piece(w, t):
                w = w[:].rearrange("p a b c -> p (a b c)") if len(w.shape) == 4 else w[:].rearrange("p a b -> p (a b)")
                return w[:, bass.ds(t * size, size)]

            def body(t, u, r):
                pool.wait_ge(w1_hi.sem, ready(t))
                pool.tensor_tensor(piece(pair[1], t), piece(raw, t), piece(pair[0], t).bitcast(F32), ALU.subtract
                                   ).then_inc(steps.step("lo"), 1)
            return body

        def up_ready(t):
            return w1_hi.at(0, f"hi{t // (B // 4)}") if isinstance(t, int) else w1_hi.all

        pipeline(pool, B, (1, g_low),
                 (W1_FROM + 1, weights_low(wup_raw, wup_s, w1_lo_up, KD * E1 * 2 * HID1 // B, up_ready)),
                 (W1_FROM + 6, weights_low(wdn_raw, wdn_s, w1_lo_dn, E1 * HID1 // P * D // B, lambda t: w1_hi.all)))

        after(pool, g_o, g_res)

        def h_weigh(c):
            def body(t, u, r):
                waits = [(h_hv.sem, h_hv.at(t, f"v{c}")), (h_wt.sem, h_wt.at(t, "wt"))]
                if c >= 2:
                    waits.append((h_htp.sem, h_htp.at(t, f"t{c - 2}")))
                elif not (isinstance(t, int) and t < 1):
                    waits.append((h_htp.sem, h_htp.at(t - 1, f"t{NCH - 2 + c}")))
                wait_apart(pool, consts, *waits)
                pool.tensor_tensor(hw[:, c % 2, :, :], hv[:, c % 2, :, :],
                                   wt[:, u, c * CH:(c + 1) * CH].unsqueeze(2).to_broadcast([P, CH, HID1]), ALU.mult
                                   ).then_inc(h_hw.step(f"w{c}"), 1)
            return body

        pipeline(pool, B, *h_stages(dict(weigh=h_weigh)))

    @block.scalar
    def _(act):
        act.dma_start(wh_raw[:, :, :], Wh.rearrange("h d e -> d h e")).then_inc(small["wh"], 16)
        act.dma_start(wg_raw[:, :, :], wg.rearrange("(k p) n -> p k n", p=P)).then_inc(small["wg"], 16)


        def a_sdev(t, u, r):
            act.wait_ge(a_ln.sem, a_ln.at(t, "aggr"))
            act.activation(sm[:, u, 8:9], sm[:, u, 7:8], ACT.Sqrt, bias=eps[:, 0:1]).then_inc(a_sd.step("sd"), 1)

        def a_hi(t, u, r):
            act.wait_ge(a_tp.sem, a_tp.at(t, "tp"))
            if not early(t):
                act.wait_ge(a_proj.sem, a_proj.at(t - 2, "v"))
                act.wait_ge(a_tlo.sem, a_tlo.at(t - 2, "lo"))
            act.activation(tT[0][:, u, :, :], tp_a[u], ACT.Copy).then_inc(a_thi.step("hi"), 1)

        def a_qk(t, u, r):
            act.wait_ge(a_proj.sem, a_proj.at(t, "qk"))
            if not early(t):
                act.wait_ge(a_sc.sem, a_sc.at(t - 2, "s"))
                act.wait_ge(a_qlo.sem, a_qlo.at(t - 2, "lo"))
            act.activation(qk[0][:, u, :, :], qk_a[u], ACT.Copy).then_inc(a_qhi.step("hi"), 1)

        def a_relu(t, u, r):
            act.wait_ge(a_proj.sem, a_proj.at(t, "gate"))
            act.activation(G[:, bass.ds(t, 1), :].rearrange("p a d -> p (a d)"), g_a[u], ACT.Relu
                           ).then_inc(a_gate.step("relu"), 1)

        def a_values(t, u, r):
            act.wait_ge(a_proj.sem, a_proj.at(t, "v"))
            act.activation(V[0][:, :, bass.ds(t, 1), :].rearrange("p h a e -> p h (a e)"), v_a, ACT.Copy
                           ).then_inc(a_vhi.step("hi"), 1)

        after(act, consts)
        pipeline(act, B, (4, a_values), (4, a_qk), (0, a_sdev), (4, a_relu), (2, a_hi))

        after(act, a_cin, a_sc)
        for g in range(B // VG):
            for h in range(H0):
                act.wait_ge(b_o.sem, b_o.at(0, f"g{g}h{h}"))
                act.activation(rows[:, g * VG:(g + 1) * VG, h * P:(h + 1) * P], o_b[g * H0 + h], ACT.Copy
                               ).then_inc(b_keep.step(f"g{g}h{h}"), 1)

        def sdev_all(i, e):
            act.wait_ge(mo[i].sem, mo[i].at(0, "var"))
            act.activation(sdev[:, :], mom[:, 4, :], ACT.Sqrt, bias=eps[:, e:e + 1], scale=1.0 / D).then_inc(mo_sd[i].step("sd"), 1)

        sdev_all(0, 1)
        after(act, b_o)

        def c_split(t, u, r):
            act.wait_ge(c_tp.sem, c_tp.at(t, "tp"))
            if not early(t):
                act.wait_ge(c_o.sem, c_o.at(t - 2, "o"))
                act.wait_ge(c_lo.sem, c_lo.at(t - 2, "lo"))
            act.activation(tT[0][:, u, 0:2, :], two_a[u], ACT.Copy).then_inc(c_hi.step("hi"), 1)

        def d_sdev(t, u, r):
            act.wait_ge(d_ln.sem, d_ln.at(t, "aggr"))
            act.activation(sm[:, u, 8:9], sm[:, u, 7:8], ACT.Sqrt, bias=eps[:, 0:1]).then_inc(d_sd.step("sd"), 1)

        def d_turned(t, u, r):
            act.wait_ge(d_tp.sem, d_tp.at(t, "tp"))
            if not early(t):
                act.wait_ge(d_lg.sem, d_lg.at(t - 2, "logits"))
            act.activation(xTd[:, u, :, :], two_d[u], ACT.Copy).then_inc(d_kept.step("copy"), 1)

        def d_keep(t, u, r):
            act.wait_ge(d_lg.sem, d_lg.at(t, "logits"))
            act.activation(lg[:, bass.ds(t, 1), :].rearrange("p a e -> p (a e)"), lg_d[u], ACT.Copy
                           ).then_inc(d_lgc.step("copy"), 1)

        def d_rows(t, u, r):
            act.wait_ge(d_xn.sem, d_xn.at(t, "xn"))
            act.activation(tile_of(rows, t), xnd[:, u, :], ACT.Copy).then_inc(d_row.step("copy"), 1)

        pipeline(act, B, (2, c_split), (8, d_keep), (6, d_turned), (6, d_rows), (4, d_sdev))

        after(act, d_lgc)
        act.activation(lg[:, :, :], lg[:, :, :], ACT.Tanh, scale=1.0 / SOFTCAP).then_inc(r_act.step("tanh"), 1)
        act.wait_ge(r_dve.sem, r_dve.at(0, "sub"))
        act.activation(rt["prob"][:, :, :], lg[:, :, :], ACT.Exp).then_inc(r_act.step("exp"), 1)

        def e_rows(t, u, r):
            act.wait_ge(e_tp.sem, e_tp.at(t, "tp"))
            if not early(t):
                act.wait_ge(e_up.sem, e_up.at(t - 2, "b"))
                act.wait_ge(e_xlo.sem, e_xlo.at(t - 2, "lo"))
            act.activation(xTc[0][:, u, :, :], xT_c[u], ACT.Copy).then_inc(e_xhi.step("hi"), 1)

        def e_act(t, u, r):
            act.wait_ge(e_up.sem, e_up.at(t, "a"))
            if not early(t):
                act.wait_ge(e_h.sem, e_h.at(t - 2, "h"))
            act.activation(sa[:, u, :], up_c[u][0], ACT.Silu).then_inc(e_silu.step("silu"), 1)

        def e_hid(t, u, r):
            act.wait_ge(e_htp.sem, e_htp.at(t, "tp"))
            if not early(t):
                act.wait_ge(e_dn.sem, e_dn.at(t - 2, "y"))
                act.wait_ge(e_hlo.sem, e_hlo.at(t - 2, "lo"))
            act.activation(hTc[0][:, u, :, :], hT_c, ACT.Copy).then_inc(e_hhi.step("hi"), 1)

        expert = {}

        def weight_high(n):
            def body(t, u, r):
                if n != 1:
                    expert[n] = load_expert(act, t)
                part = expert_part(expert[0 if n == 1 else n], n)
                wait_part_used(act, t, n)
                if not early(t):
                    act.wait_ge(e_wlo[n].sem, e_wlo[n].at(t - 2, "lo"))
                act.activation(wsp[n][0][:, u, :], part, ACT.Copy).then_inc(e_whi[n].step("hi"), 1)
            return body

        act.wait_ge(got_w0, 16 * 3 * E0)
        after(act, r_dve, r_pe)
        pipeline(act, TILES0, (1, weight_high(0)), (2, e_act), (1, e_rows), (3, e_hid), (1, weight_high(1)),
                 (3, weight_high(2)))

        def load_w1(n, half):
            if n < len(w1_parts):
                fr, rawt, _, _ = w1_parts[n]
                m = rawt.shape[1] // 2
                act.dma_start(rawt[:, half * m:(half + 1) * m], fr[:, half * m:(half + 1) * m]
                              ).then_inc(got_w1[n], 16)

        after(act, e_dn, *e_wlo)
        act.wait_ge(got_c2[0], 16)
        for n in range(2):
            for half in range(2):
                load_w1(n, half)

        def w1_high(t, u, r):
            if isinstance(t, int) and 0 <= t - W1_FROM < len(w1_parts):
                split_w1(t - W1_FROM)

        def split_w1(n):
            load_w1(n + 2, 0)
            _, rawt, hi, _ = w1_parts[n]
            act.wait_ge(got_w1[n], 32)
            act.activation(hi, rawt, ACT.Copy).then_inc(w1_hi.step(f"hi{n}"), 1)
            load_w1(n + 2, 1)

        sdev_all(1, 0)

        def g_high(t, u, r):
            wait_loaded(act, got_c2, t)
            if not early(t):
                act.wait_ge(g_sc.sem, g_sc.at(t - 2, "s"))
                act.wait_ge(g_lo.sem, g_lo.at(t - 2, "x"))
            act.activation(cs[0][:, u, :], tile_of(ctx2, t), ACT.Copy).then_inc(g_hi.step("ctx"), 1)
            act.wait_ge(g_xn.sem, g_xn.at(t, "xn"))
            act.activation(xs[0][:, u, :], xn2[:, u, :], ACT.Copy).then_inc(g_hi.step("x"), 1)

        def g_turn(t, u, r):
            act.wait_ge(g_tp.sem, g_tp.at(t, "tp"))
            if not early(t):
                act.wait_ge(g_o.sem, g_o.at(t - 2, "o"))
                act.wait_ge(g_tlo.sem, g_tlo.at(t - 2, "lo"))
            act.activation(cT[0][:, u, :, :], cT_d[u], ACT.Copy).then_inc(g_thi.step("hi"), 1)

        def g_expo(t, u, r):
            act.wait_ge(g_mx.sem, g_mx.at(t, "neg"))
            if not early(t):
                act.wait_ge(g_ahi.sem, g_ahi.at(t - 2, "a1"))
                act.wait_ge(g_alo.sem, g_alo.at(t - 2, "a1"))
            for k in range(KD):
                act.activation(ex[:, u, k, :], sc_d[u][:, k, :], ACT.Exp, bias=smx[:, u, 1, k:k + 1],
                               scale=D ** -0.5, accum_out=smx[:, u, 2, k:k + 1]).then_inc(g_ex.step(f"e{k}"), 1)

        def g_attn(t, u, r):
            act.wait_ge(g_rs.sem, g_rs.at(t, "r"))
            if not early(t):
                act.wait_ge(g_o.sem, g_o.at(t - 2, "o"))
            for k in range(KD):
                act.activation(at[0][:, u, k, :], ex[:, u, k, :], ACT.Copy, scale=smx[:, u, 3, k:k + 1]
                               ).then_inc(g_ahi.step(f"a{k}"), 1)

        after(act, e_ys, f_add)
        pipeline(act, B, (1, g_high), (4, g_turn), (4, g_attn), (3, g_expo), (0, w1_high), peel=W1_FROM + len(w1_parts) + 1)
        sdev_all(2, 0)
        after(act, g_o, g_res)

        def p_high(t, u, r):
            act.wait_ge(p_tp.sem, p_tp.at(t, "tp"))
            if not early(t):
                act.wait_ge(p_gs.sem, p_gs.at(t - 2, "gs"))
                act.wait_ge(p_lo.sem, p_lo.at(t - 2, "kept"))
            act.activation(x3T[:, u, 0, :, :], x3T_e[u], ACT.Copy).then_inc(p_hi.step("hi"), 1)
            act.activation(x3_part(t, 0), x3T_e[u].rearrange("p k d -> p (k d)"), ACT.Copy
                           ).then_inc(p_hi.step("kept"), 1)

        def p_gate(t, u, r):
            act.wait_ge(p_gs.sem, p_gs.at(t, "gs"))
            act.activation(tile_of(esc, t), gs_e[u][:, 0:E1], ACT.Exp, scale=-1.0).then_inc(p_act.step("exp"), 1)
            act.activation(tile_of(shr, t), gs_e[u][:, E1:GS], ACT.Copy).then_inc(p_act.step("copy"), 1)

        pipeline(act, B, (3, p_gate), (1, p_high))

        def h_shared(t, u, r):
            if not early(t):
                act.wait_ge(h_rt.sem, h_rt.at(t - 2, "hs"))
            act.activation(sgs[:, u, :], tile_of(shr, t)[:, HS:2 * HS], ACT.Silu).then_inc(h_sh.step("silu"), 1)

        def h_act_c(c):
            def body(t, u, r):
                act.wait_ge(h_up.sem, h_up.at(t, f"u{c}"))
                if c >= 2:
                    act.wait_ge(h_hv.sem, h_hv.at(t, f"v{c - 2}"))
                elif not (isinstance(t, int) and t < 1):
                    act.wait_ge(h_hv.sem, h_hv.at(t - 1, f"v{NCH - 2 + c}"))
                act.activation(sg[:, c % 2, :, :], up_e[c % 2][:, :, 0:HID1], ACT.Silu
                               ).then_inc(h_silu.step(f"s{c}"), 1)
            return body

        def h_high(c):
            def body(t, u, r):
                act.wait_ge(h_htp.sem, h_htp.at(t, f"t{c}"))
                b, out_t, in_t = h_buffer(t, u, c)
                wait_h_free(act, t, c)
                act.activation(out_t[0], in_t, ACT.Copy).then_inc(h_hhi.step(f"t{c}"), 1)
            return body

        after(act, p_act)
        pipeline(act, B, *h_stages(dict(shared=h_shared, silu=h_act_c, high=h_high)))

    @block.vector
    def _(dve):
        def a_weights(t, u, r):
            if isinstance(t, int) and t == 0:
                for name, rawt, (hi, lo) in (("wh", wh_raw, wh), ("wg", wg_raw, wgs)):
                    dve.wait_ge(small[name], 16)
                    dve.tensor_copy(hi[:], rawt[:]).then_inc(dve_w.step(name + "_hi"), 1)
                    dve.wait_ge(dve_w.sem, dve_w.at(0, name + "_hi"))
                    dve.tensor_tensor(lo[:], rawt[:], hi[:].bitcast(F32), ALU.subtract
                                      ).then_inc(dve_w.step(name + "_lo"), 1)

        def row(buf, t):
            return buf[:, bass.ds(t, 1), :].rearrange("p a d -> p (a d)")

        def a_stats(t, u, r):
            wait_loaded(dve, got_x, t)
            dve.bn_stats(sm[:, u, 0:6], row(x_res, t)).then_inc(a_ln.step("stats"), 1)

        def a_aggr(t, u, r):
            wait_apart(dve, consts, (a_ln.sem, a_ln.at(t, "stats")))
            dve.bn_aggr(sm[:, u, 6:8], sm[:, u, 0:6]).then_inc(a_ln.step("aggr"), 1)

        def a_norm(t, u, r):
            dve.wait_ge(a_sd.sem, a_sd.at(t, "sd"))
            dve.reciprocal(sm[:, u, 9:10], sm[:, u, 8:9]).then_inc(a_ln.step("rstd"), 1)

        def a_xn(t, u, r):
            dve.wait_ge(a_ln.sem, a_ln.at(t, "rstd"))
            if not early(t):
                dve.wait_ge(a_tp.sem, a_tp.at(t - 2, "tp"))
            dve.tensor_scalar(xn[:, u, :], row(x_res, t), sm[:, u, 6:7], sm[:, u, 9:10], ALU.subtract, ALU.mult
                              ).then_inc(a_ln.step("xn"), 1)

        def a_low(t, u, r):
            dve.wait_ge(a_thi.sem, a_thi.at(t, "hi"))
            if not early(t):
                dve.wait_ge(a_proj.sem, a_proj.at(t - 2, "v"))
            dve.tensor_tensor(tT[1][:, u, :, :], tp_a[u], tT[0][:, u, :, :].bitcast(F32), ALU.subtract
                              ).then_inc(a_tlo.step("lo"), 1)

        def a_qklow(t, u, r):
            dve.wait_ge(a_qhi.sem, a_qhi.at(t, "hi"))
            if not early(t):
                dve.wait_ge(a_sc.sem, a_sc.at(t - 2, "s"))
            dve.tensor_tensor(qk[1][:, u, :, :], qk_a[u], qk[0][:, u, :, :].bitcast(F32), ALU.subtract
                              ).then_inc(a_qlo.step("lo"), 1)

        def a_vlow(t, u, r):
            dve.wait_ge(a_vhi.sem, a_vhi.at(t, "hi"))
            at_t = bass.ds(t, 1)
            dve.tensor_tensor(V[1][:, :, at_t, :].rearrange("p h a e -> p h (a e)"), v_a,
                              V[0][:, :, at_t, :].rearrange("p h a e -> p h (a e)").bitcast(F32), ALU.subtract
                              ).then_inc(a_vlo.step("lo"), 1)

        pipeline(dve, B, (0, a_stats), (4, a_vlow), (0, a_aggr), (0, a_weights), (4, a_qklow), (0, a_norm), (2, a_low),
                 (0, a_xn))

        after(dve, a_sc)
        dve.wait_ge(small["decay"], 16)
        for h in range(H0):
            dve.tensor_tensor(Araw[:, h, :], S_a[h], dec[:, h, :], ALU.mult).then_inc(b_mask.step(f"masked{h}"), 1)
        dve.wait_ge(b_mask.sem, b_mask.at(0, "masked1"))
        dve.scalar_tensor_tensor(out=Araw[:, :, :], in0=Araw[:, :, :], scalar=-1.0, in1=Araw[:, :, :],
                                 op0=ALU.mult, op1=ALU.max).then_inc(b_mask.step("abs"), 1)
        dve.wait_ge(b_mask.sem, b_mask.at(0, "abs"))
        dve.tensor_scalar(Araw[:, :, :], Araw[:, :, :], 1.0, None, ALU.max).then_inc(b_mask.step("floor"), 1)
        dve.wait_ge(b_mask.sem, b_mask.at(0, "floor"))
        dve.tensor_copy(At[0][:, :, :], Araw[:, :, :]).then_inc(b_mask.step("hi"), 1)
        dve.wait_ge(b_mask.sem, b_mask.at(0, "hi"))
        dve.tensor_tensor(At[1][:, :, :], Araw[:, :, :], At[0][:, :, :].bitcast(F32), ALU.subtract
                          ).then_inc(b_mask.step("lo"), 1)

        for t in range(B):
            if t % VG == 0:
                dve.wait_ge(b_keep.sem, b_keep.at(0, f"g{t // VG}h{H0 - 1}"))
            dve.bn_stats(bn[:, t, :], rows[:, t, :]).then_inc(b_stat.step("stats"), 1)

        def moments(i, stats, e):
            m = mo[i]
            after(dve, stats)
            dve.tensor_tensor(mom[:, 0, :], bn[:, :, 1], bn[:, :, 4], ALU.add).then_inc(m.step("sum"), 1)
            dve.tensor_tensor(mom[:, 1, :], bn[:, :, 1], bn[:, :, 4], ALU.subtract).then_inc(m.step("diff"), 1)
            dve.tensor_tensor(mom[:, 2, :], bn[:, :, 2], bn[:, :, 5], ALU.add).then_inc(m.step("m2"), 1)
            dve.wait_ge(m.sem, m.at(0, "m2"))
            dve.tensor_scalar(mean[:, :], mom[:, 0, :], 0.5, None, ALU.mult).then_inc(m.step("mean"), 1)
            dve.scalar_tensor_tensor(out=mom[:, 3, :], in0=mom[:, 1, :], scalar=D / 4.0, in1=mom[:, 1, :],
                                     op0=ALU.mult, op1=ALU.mult).then_inc(m.step("sq"), 1)
            dve.wait_ge(m.sem, m.at(0, "sq"))
            dve.tensor_tensor(mom[:, 4, :], mom[:, 3, :], mom[:, 2, :], ALU.add).then_inc(m.step("var"), 1)
            dve.wait_ge(mo_sd[i].sem, mo_sd[i].at(0, "sd"))
            dve.reciprocal(rstd[:, :], sdev[:, :]).then_inc(mo_rs[i].step("rstd"), 1)
            dve.wait_ge(mo_rs[i].sem, mo_rs[i].at(0, "rstd"))

        moments(0, b_stat, 1)
        after(dve, b_keep, b_o)

        def c_gate(t, u, r):
            dve.wait_ge(c_gb.sem, c_gb.at(t, "beta"))
            dve.scalar_tensor_tensor(out=cen[:, u, :], in0=row(rows, t), scalar=mean[:, bass.ds(t, 1)],
                                     in1=Gg[:, u, :], op0=ALU.subtract, op1=ALU.mult).then_inc(c_wy.step("centred"), 1)

        def c_scale(t, u, r):
            dve.wait_ge(c_wy.sem, c_wy.at(t, "centred"))
            if not early(t):
                dve.wait_ge(c_tp.sem, c_tp.at(t - 2, "tp"))
            dve.scalar_tensor_tensor(out=xn[:, u, :], in0=cen[:, u, :], scalar=rstd[:, bass.ds(t, 1)],
                                     in1=Gb[:, u, :], op0=ALU.mult, op1=ALU.add).then_inc(c_wy.step("scaled"), 1)

        def c_low(t, u, r):
            dve.wait_ge(c_hi.sem, c_hi.at(t, "hi"))
            if not early(t):
                dve.wait_ge(c_o.sem, c_o.at(t - 2, "o"))
            dve.tensor_tensor(tT[1][:, u, 0:2, :], two_a[u], tT[0][:, u, 0:2, :].bitcast(F32), ALU.subtract
                              ).then_inc(c_lo.step("lo"), 1)

        def c_add(t, u, r):
            dve.wait_ge(c_o.sem, c_o.at(t, "o"))
            dve.tensor_tensor(row(x_res, t), row_a[u], row(x_res, t), ALU.add).then_inc(c_res.step("add"), 1)

        def c_stats(t, u, r):
            wait_apart(dve, consts, (c_res.sem, c_res.at(t, "add")))
            dve.bn_stats(sm[:, u, 0:6], row(x_res, t)).then_inc(c_res.step("stats"), 1)

        def d_aggr(t, u, r):
            wait_apart(dve, consts, (c_res.sem, c_res.at(t, "stats")))
            dve.bn_aggr(sm[:, u, 6:8], sm[:, u, 0:6]).then_inc(d_ln.step("aggr"), 1)

        def d_rstd(t, u, r):
            dve.wait_ge(d_sd.sem, d_sd.at(t, "sd"))
            dve.reciprocal(sm[:, u, 9:10], sm[:, u, 8:9]).then_inc(d_ln.step("rstd"), 1)

        def d_norm(t, u, r):
            dve.wait_ge(d_ln.sem, d_ln.at(t, "rstd"))
            if not early(t):
                dve.wait_ge(d_tp.sem, d_tp.at(t - 2, "tp"))
                dve.wait_ge(d_row.sem, d_row.at(t - 2, "copy"))
            dve.tensor_scalar(xnd[:, u, :], row(x_res, t), sm[:, u, 6:7], sm[:, u, 9:10],
                              ALU.subtract, ALU.mult).then_inc(d_xn.step("xn"), 1)

        pipeline(dve, B, (4, c_add), (1, c_gate), (4, c_stats), (2, c_low), (4, d_aggr), (1, c_scale), (5, d_norm),
                 (4, d_rstd))

        R = r_dve

        def own(name):
            dve.wait_ge(R.sem, R.at(0, name))

        def over(ap, *shape):
            return ap.to_broadcast([P, *shape])

        after(dve, r_iota, d_lg)
        for u in range(2):
            dve.wait_ge(d_st[u], 16 * (B // 2))
        dve.wait_ge(r_act.sem, r_act.at(0, "tanh"))
        prob, rest, key, m, k_ = rt["prob"], rt["rest"], rt["key"], rt["m"], rt["k"]
        dve.tensor_scalar(lg[:, :, :], lg[:, :, :], SOFTCAP, None, ALU.mult).then_inc(R.step("cap"), 1)
        own("cap")
        dve.tensor_reduce(m[:, :], lg[:, :, :], X, ALU.max).then_inc(R.step("max"), 1)
        own("max")
        dve.tensor_tensor(lg[:, :, :], lg[:, :, :], over(m[:, :].unsqueeze(2), B, E0), ALU.subtract
                          ).then_inc(R.step("sub"), 1)
        dve.wait_ge(r_act.sem, r_act.at(0, "exp"))
        dve.tensor_reduce(m[:, :], prob[:, :, :], X, ALU.add).then_inc(R.step("sum"), 1)
        own("sum")
        dve.reciprocal(rt["r"][:, :], m[:, :]).then_inc(R.step("rsum"), 1)
        own("rsum")
        dve.tensor_tensor(prob[:, :, :], prob[:, :, :], over(rt["r"][:, :].unsqueeze(2), B, E0), ALU.mult
                          ).then_inc(R.step("prob"), 1)
        own("prob")
        for n, source in ((1, prob), (2, rest)):
            hot_n = rt[f"hot{n}"]
            dve.tensor_reduce(rt["val"][:, 2, (n - 1) * B:n * B], source[:, :, :], X, ALU.max
                              ).then_inc(R.step(f"best{n}"), 1)
            own(f"best{n}")
            best = over(rt["val"][:, 2, (n - 1) * B:n * B].unsqueeze(2), B, E0)
            dve.tensor_tensor(key[:, :, :], source[:, :, :], best, ALU.is_equal).then_inc(R.step(f"is{n}"), 1)
            own(f"is{n}")
            dve.tensor_tensor(key[:, :, :], key[:, :, :], over(rt["rev"][:, :].unsqueeze(1), B, E0), ALU.mult
                              ).then_inc(R.step(f"key{n}"), 1)
            own(f"key{n}")
            dve.tensor_reduce(k_[:, :], key[:, :, :], X, ALU.max).then_inc(R.step(f"first{n}"), 1)
            own(f"first{n}")
            dve.tensor_tensor(hot_n[:, :, :], key[:, :, :], over(k_[:, :].unsqueeze(2), B, E0), ALU.is_equal
                              ).then_inc(R.step(f"hot{n}"), 1)
            own(f"hot{n}")
            dve.tensor_copy(rt["wsel"][:, n - 1, :], rt["val"][:, 2, (n - 1) * B:n * B]).then_inc(R.step(f"w{n}"), 1)
            if n == 1:
                dve.scalar_tensor_tensor(out=rest[:, :, :], in0=hot_n[:, :, :], scalar=-4.0, in1=prob[:, :, :],
                                         op0=ALU.mult, op1=ALU.add).then_inc(R.step("rest"), 1)
                own("rest")
        dve.tensor_tensor(mask0[:, :, :], rt["hot1"][:, :, :], rt["hot2"][:, :, :], ALU.add).then_inc(R.step("mask"), 1)
        dve.wait_ge(r_pe.sem, r_pe.at(0, "pos"))
        dve.tensor_copy(rt["cnt"][:, :], pos_r[:, B, :]).then_inc(R.step("count"), 1)
        own("count")
        two = rt["over"]
        dve.tensor_tensor(two[:, :, :], over(rt["cnt"][:, :].unsqueeze(2), E0, B),
                          over(rt["steps128"][:, :].unsqueeze(1), E0, B), ALU.is_gt).then_inc(R.step("over"), 1)
        own("over")
        dve.tensor_reduce(rt["tiles"][:, :], two[:, :, :], X, ALU.add).then_inc(R.step("tiles"), 1)
        dve.memset(rt["one8"][:, :], 1.0).then_inc(R.step("one8"), 1)
        own("one8")
        dve.tensor_tensor_scan(rt["tend"][:, :], rt["one8"][:, :], rt["tiles"][:, :], 0.0, ALU.mult, ALU.add
                               ).then_inc(R.step("tend"), 1)
        own("tend")
        dve.tensor_tensor(rt["tstart"][:, :], rt["tend"][:, :], rt["tiles"][:, :], ALU.subtract
                          ).then_inc(R.step("tstart"), 1)
        own("tstart")
        dve.scalar_tensor_tensor(out=rt["slot"][:, :, :], in0=over(rt["tstart"][:, :].unsqueeze(1), B, E0),
                                 scalar=float(P), in1=pos_r[:, 0:B, :], op0=ALU.mult, op1=ALU.add
                                 ).then_inc(R.step("slot"), 1)
        own("slot")
        for n in (1, 2):
            dve.tensor_tensor(rt["pick"][:, :, :], rt["slot"][:, :, :], rt[f"hot{n}"][:, :, :], ALU.mult
                              ).then_inc(R.step(f"pick{n}"), 1)
            own(f"pick{n}")
            dve.tensor_reduce(rt["slotk"][:, n - 1, :], rt["pick"][:, :, :], X, ALU.add).then_inc(R.step(f"slot{n}"), 1)
            own(f"slot{n}")
        dve.tensor_tensor(rt["passed"][:, :, :], over(rt["tend"][:, :].unsqueeze(1), TJ, E0),
                          over(rt["jrow"][:, :].unsqueeze(2), TJ, E0), ALU.is_le).then_inc(R.step("passed"), 1)
        own("passed")
        dve.tensor_reduce(rt["ef"][:, :], rt["passed"][:, :, :], X, ALU.add).then_inc(R.step("e"), 1)
        own("e")
        dve.tensor_scalar(rt["ef"][:, :], rt["ef"][:, :], float(E0 - 1), None, ALU.min).then_inc(R.step("emin"), 1)
        own("emin")
        dve.tensor_copy(expert_of[:, :], rt["ef"][:, :]).then_inc(R.step("eint"), 1)
        slotk = rt["slotk"][:, :, :].rearrange("p k b -> p (k b)")
        dve.tensor_tensor(rt["ge"][:, :, :], over(slotk.unsqueeze(2), NPAIR, TJ + 1),
                          over(rt["j128"][:, :].unsqueeze(1), NPAIR, TJ + 1), ALU.is_ge).then_inc(R.step("ge"), 1)
        own("ge")
        dve.tensor_tensor(rt["hotj"][:, :, :], rt["ge"][:, :, 0:TJ], rt["ge"][:, :, 1:TJ + 1], ALU.subtract
                          ).then_inc(R.step("hotj"), 1)
        dve.tensor_reduce(rt["tile_of"][:, :], rt["ge"][:, :, 1:TJ + 1], X, ALU.add).then_inc(R.step("tile_of"), 1)
        own("tile_of")
        dve.scalar_tensor_tensor(out=rt["row_of"][:, :], in0=rt["tile_of"][:, :], scalar=-float(P), in1=slotk,
                                 op0=ALU.mult, op1=ALU.add).then_inc(R.step("row_of"), 1)
        own("row_of")
        half = NPAIR // 2
        for h in range(2):
            part = slice(h * half, (h + 1) * half)
            dve.tensor_tensor(rt["hotp"][:, part, :], over(rt["row_of"][:, part].unsqueeze(2), half, P),
                              over(iota_row[:, :].unsqueeze(1), half, P), ALU.is_equal).then_inc(R.step(f"hotp{h}"), 1)
            dve.tensor_tensor(rt["R"][:, part, 2, :], rt["hotj"][:, part, :],
                              over(rt["val"][:, 2, part].unsqueeze(2), half, TJ), ALU.mult
                              ).then_inc(R.step(f"r_w{h}"), 1)
        dve.wait_ge(r_pe.sem, r_pe.at(0, "tab"))
        dve.tensor_scalar(rt["none"][:, :], tab_r[:, 0, :], 0.0, NOWHERE, ALU.is_equal, ALU.mult
                          ).then_inc(R.step("none"), 1)
        own("none")
        dve.scalar_tensor_tensor(out=rt["T"][:, 0, :], in0=tab_r[:, 0, :], scalar=-1.0, in1=rt["none"][:, :],
                                 op0=ALU.add, op1=ALU.add).then_inc(R.step("dest"), 1)
        dve.tensor_copy(table[:, 0, :], tab_r[:, 1, :]).then_inc(R.step("t_tok"), 1)
        dve.tensor_copy(table[:, 2, :].bitcast(F32), tab_r[:, 2, :]).then_inc(R.step("t_w"), 1)
        own("dest")
        dve.tensor_copy(table[:, 1, :], rt["T"][:, 0, :]).then_inc(R.step("t_dst"), 1)

        def e_hidden(t, u, r):
            dve.wait_ge(e_silu.sem, e_silu.at(t, "silu"))
            dve.wait_ge(e_up.sem, e_up.at(t, "b"))
            if not early(t):
                dve.wait_ge(e_htp.sem, e_htp.at(t - 2, "tp"))
            dve.tensor_tensor(hh[:, u, :], sa[:, u, :], up_c[u][1], ALU.mult).then_inc(e_h.step("h"), 1)

        def e_weigh(t, u, r):
            dve.wait_ge(e_dn.sem, e_dn.at(t, "y"))
            if not early(t):
                dve.wait_ge(e_yst[u], 16 * r)
            dve.tensor_copy(stage_s[:, u, :], table[:, 1, bass.ds(t, 1)]).then_inc(e_ys.step("dst"), 1)
            dve.tensor_scalar(ys[:, u, :], y_c, table[:, 2, bass.ds(t, 1)].bitcast(F32), None, ALU.mult
                              ).then_inc(e_ys.step("y"), 1)

        def e_xlow(t, u, r):
            dve.wait_ge(e_xhi.sem, e_xhi.at(t, "hi"))
            if not early(t):
                dve.wait_ge(e_up.sem, e_up.at(t - 2, "b"))
            dve.tensor_tensor(xTc[1][:, u, :, :], xT_c[u], xTc[0][:, u, :, :].bitcast(F32), ALU.subtract
                              ).then_inc(e_xlo.step("lo"), 1)

        def e_hlow(t, u, r):
            dve.wait_ge(e_hhi.sem, e_hhi.at(t, "hi"))
            if not early(t):
                dve.wait_ge(e_dn.sem, e_dn.at(t - 2, "y"))
            dve.tensor_tensor(hTc[1][:, u, :, :], hT_c, hTc[0][:, u, :, :].bitcast(F32), ALU.subtract
                              ).then_inc(e_hlo.step("lo"), 1)

        expert = {}

        def weight_low(n):
            def body(t, u, r):
                if n == 0:
                    expert[0] = load_expert(dve, t)
                part = expert_part(expert[0], n)
                wait_part_used(dve, t, n)
                dve.wait_ge(e_whi[n].sem, e_whi[n].at(t, "hi"))
                dve.tensor_tensor(wsp[n][1][:, u, :], part, wsp[n][0][:, u, :].bitcast(F32), ALU.subtract
                                  ).then_inc(e_wlo[n].step("lo"), 1)
            return body

        dve.wait_ge(got_w0, 16 * 3 * E0)
        after(dve, R)
        def e_tokens(t, u, r):
            if not early(t):
                dve.wait_ge(e_xg[u], 16 * r)
            dve.tensor_copy(stage_g[:, u, :], table[:, 0, bass.ds(t, 1)]).then_inc(e_tok.step("copy"), 1)

        pipeline(dve, TILES0, (0, e_tokens), (3, e_hidden), (5, e_weigh), (1, weight_low(0)), (1, e_xlow), (3, e_hlow),
                 (1, weight_low(1)))

        def f_sum(t, u, r):
            dve.wait_ge(f_two.sem, f_two.at(t, "y"))
            both_x = x_res[:, bass.ds(2 * t, 2), :]
            dve.tensor_tensor(both_x, both_x, yin[:, bass.ds(2 * t, 2), 0:D], ALU.add).then_inc(f_add.step("x"), 1)

        def f_stats(t, u, r):
            dve.wait_ge(f_add.sem, f_add.at(t, "x"))
            for v in range(2):
                dve.bn_stats(row(bn, 2 * t + v), row(x_res, 2 * t + v)).then_inc(f_stat.step(f"stats{v}"), 1)

        pipeline(dve, B // 2, (0, f_sum), (1, f_stats))
        moments(1, f_stat, 0)

        def g_norm(t, u, r):
            if not early(t):
                dve.wait_ge(g_hi.sem, g_hi.at(t - 2, "x"))
                dve.wait_ge(g_lo.sem, g_lo.at(t - 2, "x"))
            dve.tensor_scalar(xn2[:, u, :], row(x_res, t), mean[:, bass.ds(t, 1)], rstd[:, bass.ds(t, 1)],
                              ALU.subtract, ALU.mult).then_inc(g_xn.step("xn"), 1)


        def g_turnlow(t, u, r):
            dve.wait_ge(g_thi.sem, g_thi.at(t, "hi"))
            if not early(t):
                dve.wait_ge(g_o.sem, g_o.at(t - 2, "o"))
            dve.tensor_tensor(cT[1][:, u, :, :], cT_d[u], cT[0][:, u, :, :].bitcast(F32), ALU.subtract
                              ).then_inc(g_tlo.step("lo"), 1)

        def g_max(t, u, r):
            dve.wait_ge(g_sc.sem, g_sc.at(t, "s"))
            dve.tensor_reduce(smx[:, u, 0, :], sc_d[u], X, ALU.max).then_inc(g_mx.step("max"), 1)

        def g_neg(t, u, r):
            dve.wait_ge(g_mx.sem, g_mx.at(t, "max"))
            dve.tensor_scalar(smx[:, u, 1, :], smx[:, u, 0, :], -(D ** -0.5), None, ALU.mult
                              ).then_inc(g_mx.step("neg"), 1)

        def g_rsum(t, u, r):
            dve.wait_ge(g_ex.sem, g_ex.at(t, "e1"))
            dve.reciprocal(smx[:, u, 3, :], smx[:, u, 2, :]).then_inc(g_rs.step("r"), 1)

        def g_soft(t, u, r):
            if not early(t):
                dve.wait_ge(g_o.sem, g_o.at(t - 2, "o"))
            for k in range(KD):
                dve.wait_ge(g_ahi.sem, g_ahi.at(t, f"a{k}"))
                dve.scalar_tensor_tensor(out=at[1][:, u, k, :], in0=ex[:, u, k, :], scalar=smx[:, u, 3, k:k + 1],
                                         in1=at[0][:, u, k, :].bitcast(F32), op0=ALU.mult, op1=ALU.subtract
                                         ).then_inc(g_alo.step(f"a{k}"), 1)

        def g_add(t, u, r):
            dve.wait_ge(g_o.sem, g_o.at(t, "o"))
            dve.tensor_tensor(row(x_res, t), o_d[u], row(x_res, t), ALU.add).then_inc(g_res.step("add"), 1)

        def g_stats(t, u, r):
            dve.wait_ge(g_res.sem, g_res.at(t, "add"))
            dve.bn_stats(row(bn, t), row(x_res, t)).then_inc(g_res.step("stats"), 1)

        pipeline(dve, B, (4, g_rsum), (6, g_add), (3, g_max), (6, g_stats), (3, g_neg), (0, g_norm),
                 (4, g_turnlow), (4, g_soft))
        moments(2, g_res, 0)

        def p_norm(t, u, r):
            if not early(t):
                dve.wait_ge(p_tp.sem, p_tp.at(t - 2, "tp"))
            dve.tensor_scalar(xn3[:, u, :].rearrange("p (k j) -> p k j", k=KD),
                              row(x_res, t).rearrange("p (j k) -> p k j", k=KD),
                              mean[:, bass.ds(t, 1)], rstd[:, bass.ds(t, 1)],
                              ALU.subtract, ALU.mult).then_inc(p_xn.step("xn"), 1)

        def p_low(t, u, r):
            dve.wait_ge(p_hi.sem, p_hi.at(t, "kept"))
            if not early(t):
                dve.wait_ge(p_gs.sem, p_gs.at(t - 2, "gs"))
            dve.tensor_tensor(x3T[:, u, 1, :, :], x3T_e[u], x3T[:, u, 0, :, :].bitcast(F32), ALU.subtract
                              ).then_inc(p_lo.step("lo"), 1)
            dve.tensor_tensor(x3_part(t, 1), x3T_e[u].rearrange("p k d -> p (k d)"),
                              x3T[:, u, 0, :, :].rearrange("p k d -> p (k d)").bitcast(F32), ALU.subtract
                              ).then_inc(p_lo.step("kept"), 1)

        def h_route(c):
            Q = h_rt

            def body(t, u, r):
                def mine(name):
                    dve.wait_ge(Q.sem, Q.at(t, name))

                if c == 0:
                    if isinstance(t, int) and t == 0:
                        dve.memset(macc[:, 0, :], 0.0).then_inc(Q.step("macc0"), 1)
                    else:
                        if not early(t):
                            dve.wait_ge(h_pos.sem, h_pos.at(t - 2, "pos"))
                        dve.tensor_tensor(macc[:, u, :], macc[:, 1 - u, :], mask1[:, 1 - u, :], ALU.add
                                          ).then_inc(Q.step("macc0"), 1)
                    dve.tensor_scalar(escp[:, :], row(esc, t), 1.0, None, ALU.add).then_inc(Q.step("plus"), 1)
                if c == 1:
                    mine("plus")
                    dve.reciprocal(sc[:, u, :], escp[:, :]).then_inc(Q.step("sig"), 1)
                if c == 2:
                    wait_apart(dve, consts, (Q.sem, Q.at(t, "sig")))
                    dve.max(top8[:, :], sc[:, u, :]).then_inc(Q.step("top"), 1)
                    wait_apart(dve, consts, (Q.sem, Q.at(t, "top")))
                    dve.max_index(idx8[:, :], top8[:, :], sc[:, u, :]).then_inc(Q.step("index"), 1)
                    mine("index")
                    dve.tensor_copy(idxf[:, :], idx8[:, :]).then_inc(Q.step("indexf"), 1)
                if c == 3:
                    mine("indexf")
                    dve.tensor_tensor(hot[:, :, :], over(idxf[:, 0:TOP1].unsqueeze(2), TOP1, E1),
                                      over(iota_row[:, 0:E1].unsqueeze(1), TOP1, E1), ALU.is_equal
                                      ).then_inc(Q.step("hot"), 1)
                if c == 4:
                    mine("hot")
                    if not early(t):
                        dve.wait_ge(h_pos.sem, h_pos.at(t - 2, "pos"))
                    with nc.allow_low_precision(reason="zeros and ones"):
                        dve.tensor_reduce(mask1[:, u, :], hot[:, :, :].rearrange("p k e -> p e k"), X, ALU.add
                                          ).then_inc(Q.step("mask"), 1)
                if c == 5:
                    mine("mask")
                    dve.tensor_tensor(ssel[:, :], sc[:, u, :], mask1[:, u, :], ALU.mult).then_inc(Q.step("sel"), 1)
                    mine("sel")
                    dve.tensor_reduce(wsum[:, 0:1], ssel[:, :], X, ALU.add).then_inc(Q.step("sum"), 1)
                    mine("sum")
                    dve.reciprocal(wsum[:, 1:2], wsum[:, 0:1]).then_inc(Q.step("rsum"), 1)
                if c == 6:
                    dve.wait_ge(h_sh.sem, h_sh.at(t, "silu"))
                    if not early(t):
                        dve.wait_ge(h_htp.sem, h_htp.at(t - 2, f"t{NCH}"))
                    dve.tensor_tensor(hs[:, u, :], sgs[:, u, :], row(shr, t)[:, 0:HS], ALU.mult).then_inc(Q.step("hs"), 1)

            return body

        def h_weights(t, u, r):
            dve.wait_ge(h_pos.sem, h_pos.at(t, "pos"))
            dve.wait_ge(h_rt.sem, h_rt.at(t, "rsum"))
            dve.tensor_scalar(valid[:, :], pos_e, float(CAP1), None, ALU.is_lt).then_inc(h_wt.step("valid"), 1)
            dve.wait_ge(h_wt.sem, h_wt.at(t, "valid"))
            if not early(t):
                dve.wait_ge(h_hw.sem, h_hw.at(t - 2, f"w{NCH - 1}"))
            dve.scalar_tensor_tensor(out=wt[:, u, :], in0=ssel[:, :], scalar=wsum[:, 1:2], in1=valid[:, :],
                                     op0=ALU.mult, op1=ALU.mult).then_inc(h_wt.step("wt"), 1)

        def h_vec(c):
            def body(t, u, r):
                dve.wait_ge(h_silu.sem, h_silu.at(t, f"s{c}"))
                if c >= 2:
                    dve.wait_ge(h_hw.sem, h_hw.at(t, f"w{c - 2}"))
                elif not (isinstance(t, int) and t < 1):
                    dve.wait_ge(h_hw.sem, h_hw.at(t - 1, f"w{NCH - 2 + c}"))
                dve.tensor_tensor(hv[:, c % 2, :, :], sg[:, c % 2, :, :], up_e[c % 2][:, :, HID1:2 * HID1], ALU.mult
                                  ).then_inc(h_hv.step(f"v{c}"), 1)
            return body

        def h_low(c):
            def body(t, u, r):
                dve.wait_ge(h_hhi.sem, h_hhi.at(t, f"t{c}"))
                b, out_t, in_t = h_buffer(t, u, c)
                wait_h_free(dve, t, c)
                dve.tensor_tensor(out_t[1], in_t, out_t[0].bitcast(F32), ALU.subtract).then_inc(h_hlo.step(f"t{c}"), 1)
            return body

        def h_result(t, u, r):
            dve.wait_ge(h_dn.sem, h_dn.at(t, f"d{NCH}"))
            if not early(t):
                dve.wait_ge(h_st[u], 16 * r)
            dve.tensor_tensor(outb[:, u, :], y_e[u], row(x_res, t), ALU.add).then_inc(h_out.step("out"), 1)

        after(dve, g_o)
        pipeline(dve, B, (0, p_norm), (1, p_low))
        after(dve, p_act)
        pipeline(dve, B, *h_stages(dict(route=h_route, weights=h_weights, vec=h_vec,
                                        low=h_low, result=h_result)))

    @block.tensor
    def _(pe):
        def both(pair, *idx):
            return pair[0][idx], pair[1][idx]

        A = slice(None)

        def a_turn(t, u, r):
            pe.wait_ge(a_cin.sem, a_cin.at(t, "copy"))
            pe.wait_ge(a_ln.sem, a_ln.at(t, "xn"))
            if not early(t):
                pe.wait_ge(a_thi.sem, a_thi.at(t - 2, "hi"))
                pe.wait_ge(a_tlo.sem, a_tlo.at(t - 2, "lo"))
            for k in range(KD):
                pe.transpose(tp_a[u][:, k, :], xn[:, u, k * P:(k + 1) * P], ident[:, :])
            for k in range(KD):
                mm = pe.transpose(tp_a[u][:, KD + k, :], cin[:, u, k * P:(k + 1) * P], ident[:, :])
            mm.then_inc(a_tp.step("tp"), 1)

        def a_project(t, u, r):
            pe.wait_ge(a_tlo.sem, a_tlo.at(t, "lo"))
            if isinstance(t, int) and t == 0:
                after(pe, dve_w)
            if not early(t):
                pe.wait_ge(a_qhi.sem, a_qhi.at(t - 2, "hi"))
                pe.wait_ge(a_qlo.sem, a_qlo.at(t - 2, "lo"))
            for h in range(H0):
                mm = mm3(pe, qk_a[u][:, 2 * h:2 * h + 2, :], both(wh, A, h, A), both(tT, A, u, slice(h, 4, 2), A),
                         True, True)
            mm.then_inc(a_proj.step("qk"), 1)
            if not early(t):
                pe.wait_ge(a_gate.sem, a_gate.at(t - 2, "relu"))
            for k in range(KD):
                mm = mm3(pe, g_a[u], both(tT, A, u, k, A), both(wgs, A, k, A), k == 0, k == KD - 1)
            mm.then_inc(a_proj.step("gate"), 1)
            if not (isinstance(t, int) and t < 1):
                pe.wait_ge(a_vlo.sem, a_vlo.at(t - 1, "lo"))
            for h in range(H0):
                mm = mm3(pe, v_a[:, h, :], both(tT, A, u, KD + h, A), both(wh, A, h, A), True, True)
            mm.then_inc(a_proj.step("v"), 1)

        def a_score(t, u, r):
            pe.wait_ge(a_qlo.sem, a_qlo.at(t, "lo"))
            for h in range(H0):
                mm = mm3(pe, S_a[h], both(qk, A, u, 2 * h + 1, A), both(qk, A, u, 2 * h, A),
                         isinstance(t, int) and t == 0 and h == 0,
                         isinstance(t, int) and t == B - 1 and h == H0 - 1, skip_group_check=True)
            mm.then_inc(a_sc.step("s"), 1)

        after(pe, consts)
        pipeline(pe, B, (2, a_turn), (5, a_score), (3, a_project))

        after(pe, b_mask, a_gate, a_qlo, a_vlo)
        for g in range(B // VG):
            for h in range(H0):
                mm3(pe, o_b[g * H0 + h], both(At, A, h, A), both(V, A, h, slice(g * VG, (g + 1) * VG), A), True, True
                    ).then_inc(b_o.step(f"g{g}h{h}"), 1)


        def c_turn(t, u, r):
            pe.wait_ge(c_wy.sem, c_wy.at(t, "scaled"))
            if not early(t):
                pe.wait_ge(c_hi.sem, c_hi.at(t - 2, "hi"))
                pe.wait_ge(c_lo.sem, c_lo.at(t - 2, "lo"))
            for k in range(KD):
                mm = pe.transpose(two_a[u][:, k, :], xn[:, u, k * P:(k + 1) * P], ident[:, :])
            mm.then_inc(c_tp.step("tp"), 1)

        def c_project(t, u, r):
            pe.wait_ge(c_lo.sem, c_lo.at(t, "lo"))
            if not early(t):
                pe.wait_ge(c_res.sem, c_res.at(t - 2, "add"))
            for k in range(KD):
                mm = mm3(pe, row_a[u], both(tT, A, u, k, A), both(wos, A, k, A), k == 0, k == KD - 1)
            mm.then_inc(c_o.step("o"), 1)

        def d_turn(t, u, r):
            pe.wait_ge(d_xn.sem, d_xn.at(t, "xn"))
            if not early(t):
                pe.wait_ge(d_kept.sem, d_kept.at(t - 2, "copy"))
            for k in range(KD):
                mm = pe.transpose(two_d[u][:, k, :], xnd[:, u, k * P:(k + 1) * P], ident[:, :])
            mm.then_inc(d_tp.step("tp"), 1)

        def d_logits(t, u, r):
            pe.wait_ge(d_kept.sem, d_kept.at(t, "copy"))
            if not early(t):
                pe.wait_ge(d_lgc.sem, d_lgc.at(t - 2, "copy"))
            for k in range(KD):
                mm = pe.matmul(lg_d[u], xTd[:, u, k, :], gate0_raw[:, k, :], start=k == 0, stop=k == KD - 1)
            mm.then_inc(d_lg.step("logits"), 1)

        after(pe, pool_w, b_keep)
        pe.wait_ge(small["gate0"], 16)
        pipeline(pe, B, (2, c_turn), (3, c_project), (6, d_turn), (7, d_logits))

        pe.wait_ge(r_dve.sem, r_dve.at(0, "mask"))
        after(pe, d_kept)
        pe.matmul(pos_r[:, 0:B, :], before[:, :], mask0[:, :, :], start=True, stop=False, skip_group_check=True)
        for s in range(1, B + 1):
            mm = pe.matmul(pos_r[:, s:B + 1, :], ones[:, :], mask0[:, 0:B + 1 - s, :], start=False, stop=s == B,
                           skip_group_check=True)
        mm.then_inc(r_pe.step("pos"), 1)
        for n in range(NPAIR):
            if n % (NPAIR // 2) == 0:
                h = n // (NPAIR // 2)
                pe.wait_ge(r_dve.sem, r_dve.at(0, f"r_w{h}"))
                pe.wait_ge(r_pool.sem, r_pool.at(0, f"tok{h}"))
            mm = pe.matmul(tab_r, rt["hotp"][:, n, :], rt["R"][:, n, :, :], start=n == 0, stop=n == NPAIR - 1)
        mm.then_inc(r_pe.step("tab"), 1)

        def e_turn(t, u, r):
            pe.wait_ge(e_xg[u], 16 * (r + 1))
            if not early(t):
                pe.wait_ge(e_xlo.sem, e_xlo.at(t - 2, "lo"))
            for k in range(KD):
                mm = pe.transpose(xT_c[u][:, k, :], xg[:, u, k * P:(k + 1) * P], ident[:, :])
            mm.then_inc(e_tp.step("tp"), 1)

        def e_gate(t, u, r):
            pe.wait_ge(e_xlo.sem, e_xlo.at(t, "lo"))
            pe.wait_ge(e_wlo[0].sem, e_wlo[0].at(t, "lo"))
            if not early(t):
                pe.wait_ge(e_silu.sem, e_silu.at(t - 2, "silu"))
            for k in range(KD):
                mm = mm3(pe, up_c[u][0], both(xTc, A, u, k, A), both(wsp[0], A, u, slice(k * I0, (k + 1) * I0)),
                         k == 0, k == KD - 1)
            mm.then_inc(e_up.step("a"), 1)

        def e_value(t, u, r):
            pe.wait_ge(e_wlo[1].sem, e_wlo[1].at(t, "lo"))
            if not early(t):
                pe.wait_ge(e_h.sem, e_h.at(t - 2, "h"))
            for k in range(KD):
                mm = mm3(pe, up_c[u][1], both(xTc, A, u, k, A), both(wsp[1], A, u, slice(k * I0, (k + 1) * I0)),
                         k == 0, k == KD - 1)
            mm.then_inc(e_up.step("b"), 1)

        def e_hturn(t, u, r):
            pe.wait_ge(e_h.sem, e_h.at(t, "h"))
            if not (isinstance(t, int) and t < 1):
                pe.wait_ge(e_hlo.sem, e_hlo.at(t - 1, "lo"))
            for k in range(KI):
                mm = pe.transpose(hT_c[:, k, :], hh[:, u, k * P:(k + 1) * P], ident[:, :])
            mm.then_inc(e_htp.step("tp"), 1)

        def e_down(t, u, r):
            pe.wait_ge(e_hlo.sem, e_hlo.at(t, "lo"))
            pe.wait_ge(e_wlo[2].sem, e_wlo[2].at(t, "lo"))
            if not (isinstance(t, int) and t < 1):
                pe.wait_ge(e_ys.sem, e_ys.at(t - 1, "y"))
            for k in range(KI):
                mm = mm3(pe, y_c, both(hTc, A, u, k, A), both(wsp[2], A, u, slice(k * D, (k + 1) * D)),
                         k == 0, k == KI - 1)
            mm.then_inc(e_dn.step("y"), 1)

        pipeline(pe, TILES0, (2, e_gate), (1, e_turn), (3, e_hturn), (2, e_value), (4, e_down))

        def g_turn(t, u, r):
            pe.wait_ge(got_c3[u], 16 * (r + 1))
            if not early(t):
                pe.wait_ge(g_thi.sem, g_thi.at(t - 2, "hi"))
                pe.wait_ge(g_tlo.sem, g_tlo.at(t - 2, "lo"))
            for k in range(KD):
                mm = pe.transpose(cT_d[u][:, k, :], cin3[:, u, k * P:(k + 1) * P], ident[:, :])
            mm.then_inc(g_tp.step("tp"), 1)

        def g_score(t, u, r):
            pe.wait_ge(g_lo.sem, g_lo.at(t, "x"))
            if not early(t):
                pe.wait_ge(g_ex.sem, g_ex.at(t - 2, "e1"))
            for k in range(KD):
                mm = mm3(pe, sc_d[u][:, k, :], both(cs, A, u, slice(k * P, (k + 1) * P)), both(xs, A, u, A), True, True)
            mm.then_inc(g_sc.step("s"), 1)

        def g_value(t, u, r):
            pe.wait_ge(g_alo.sem, g_alo.at(t, "a1"))
            pe.wait_ge(g_tlo.sem, g_tlo.at(t, "lo"))
            if not early(t):
                pe.wait_ge(g_res.sem, g_res.at(t - 2, "add"))
            for k in range(KD):
                mm = mm3(pe, o_d[u], both(cT, A, u, k, A), both(at, A, u, k, A), k == 0, k == KD - 1)
            mm.then_inc(g_o.step("o"), 1)

        after(pe, e_ys)
        pipeline(pe, B, (2, g_score), (4, g_turn), (5, g_value))

        def x3_parts(u, k):
            return x3T[:, u, 0, k, :], x3T[:, u, 1, k, :]

        def p_turn(t, u, r):
            pe.wait_ge(p_xn.sem, p_xn.at(t, "xn"))
            if not early(t):
                pe.wait_ge(p_hi.sem, p_hi.at(t - 2, "hi"))
                pe.wait_ge(p_lo.sem, p_lo.at(t - 2, "kept"))
            for k in range(KD):
                mm = pe.transpose(x3T_e[u][:, k, :], xn3[:, u, k * P:(k + 1) * P], ident[:, :])
            mm.then_inc(p_tp.step("tp"), 1)

        def p_gates(t, u, r):
            pe.wait_ge(p_lo.sem, p_lo.at(t, "lo"))
            if not early(t):
                pe.wait_ge(p_act.sem, p_act.at(t - 2, "copy"))
            for k in range(KD):
                mm = mm3(pe, gs_e[u], x3_parts(u, k), both(gate1, A, k, A), k == 0, k == KD - 1)
            mm.then_inc(p_gs.step("gs"), 1)

        def h_place(t, u, r):
            pe.wait_ge(h_rt.sem, h_rt.at(t, "mask"))
            if not (isinstance(t, int) and t < 1):
                pe.wait_ge(h_wt.sem, h_wt.at(t - 1, "valid"))
            pe.matmul(pos_e, before[:, :], mask1[:, u, :], start=True, stop=False)
            pe.matmul(pos_e, ones[:, :], macc[:, u, :], start=False, stop=True).then_inc(h_pos.step("pos"), 1)

        def h_upc(c):
            def body(t, u, r):
                if c == 0:
                    pe.wait_ge(h_x[u], 16 * (r + 1))
                if c >= 2:
                    pe.wait_ge(h_hv.sem, h_hv.at(t, f"v{c - 2}"))
                elif not (isinstance(t, int) and t < 1):
                    pe.wait_ge(h_hv.sem, h_hv.at(t - 1, f"v{NCH - 2 + c}"))
                for k in range(KD):
                    mm = mm3(pe, up_e[c % 2], x3_parts(u, k), both(wup_s, A, slice(c * CH, (c + 1) * CH), k, A),
                             k == 0, k == KD - 1)
                mm.then_inc(h_up.step(f"u{c}"), 1)
            return body

        def h_tr(c):
            def body(t, u, r):
                b, _, in_t = h_buffer(t, u, c)
                if c == NCH:
                    wait_apart(pe, consts, (h_hlo.sem, h_hlo.at(t, f"t{c - 2}")), (h_rt.sem, h_rt.at(t, "hs")))
                elif c >= 2:
                    pe.wait_ge(h_hlo.sem, h_hlo.at(t, f"t{c - 2}"))
                elif not (isinstance(t, int) and t < 1):
                    pe.wait_ge(h_hlo.sem, h_hlo.at(t - 1, f"t{NCH - 1 + c}"))
                if c == NCH:
                    mm = pe.transpose(in_t, hs[:, u, :], ident[:, :])
                else:
                    pe.wait_ge(h_hw.sem, h_hw.at(t, f"w{c}"))
                    for k in range(KCH):
                        mm = pe.transpose(in_t[:, k, :], hw[:, c % 2, k * 4:(k + 1) * 4, :].rearrange("p e h -> p (e h)"),
                                          ident[:, :])
                mm.then_inc(h_htp.step(f"t{c}"), 1)
            return body

        def h_downc(c):
            def body(t, u, r):
                b, (hi, lo), _ = h_buffer(t, u, c)
                pe.wait_ge(h_hlo.sem, h_hlo.at(t, f"t{c}"))
                if c == 0 and not early(t):
                    pe.wait_ge(h_out.sem, h_out.at(t - 2, "out"))
                if c == NCH:
                    mm = mm3(pe, y_e[u], (hi, lo), both(wsd_s, A, A), False, True)
                else:
                    for k in range(KCH):
                        mm = mm3(pe, y_e[u], (hi[:, k, :], lo[:, k, :]), both(wdn_s, A, c * KCH + k, A),
                                 c == 0 and k == 0, False)
                mm.then_inc(h_dn.step(f"d{c}"), 1)
            return body

        after(pe, g_res)
        pipeline(pe, B, (1, p_turn), (2, p_gates))
        after(pe, p_act, w1_hi, w1_lo_up, w1_lo_dn)
        pipeline(pe, B, *h_stages(dict(pos=h_place, up=h_upc, tr=h_tr, down=h_downc)))

    st.close()


_INS = ["x", "ctx_2048", "L0_xattn_Wh", "L0_xattn_wg_w", "L0_xattn_wo_w", "L0_xattn_gn_gamma", "L0_xattn_gn_beta",
        "L0_ffn_w_gate", "L0_ffn_w1", "L0_ffn_w3", "L0_ffn_w2", "L1_ffn_w_gate", "L1_ffn_w_shared_up",
        "L1_ffn_w_shared_down", "L1_ffn_w_up", "L1_ffn_w_down"]


def decay_table(heads, seq, width):
    gam = (1.0 - 2.0 ** (-5.0 - np.arange(heads, dtype=np.float32))).astype(np.float32)
    idx = np.arange(seq, dtype=np.float32)
    expo = idx[None, :] - idx[:, None]
    d = np.where(expo[None] <= 0, gam[:, None, None] ** expo[None], 0.0).astype(np.float32)
    d = d / np.sqrt(d.sum(axis=-1))[:, None, :] / np.sqrt(np.float32(width))
    return np.ascontiguousarray(d.transpose(2, 0, 1)).astype(np.float32)


def kernel(**inputs):
    import numpy as _np
    import concourse.bacc as _bacc
    from concourse import mybir as _mybir
    from concourse.bass_utils import run_bass_kernel_spmd as _run

    nc = _bacc.Bacc("TRN2", target_bir_lowering=False, num_devices=1)
    arrays, args = {}, []

    def give(name, a):
        arrays[f"in_{name}"] = a
        args.append(nc.dram_tensor(f"in_{name}", a.shape, _mybir.dt.from_np(a.dtype), kind="ExternalInput").ap())

    for name in _INS:
        give(name, _np.ascontiguousarray(inputs[name]))
    give("decay", decay_table(H0, P, P))
    shape = tuple(inputs["x"].shape)
    args.append(nc.dram_tensor("out_0", shape, _mybir.dt.float32, kind="ExternalOutput").ap())
    build(nc, *args)
    r = _run(nc, [arrays], core_ids=[0])
    return r.results[0]["out_0"]
```
